# Optimizing a Trainium2 kernel written in Bass

```python
import numpy as np
import jax
import jax.numpy as jnp

def _softmax(x, axis=-1):
    return jax.nn.softmax(x, axis=axis)

def _gelu(x):
    return jax.nn.gelu(x, approximate=True)

def _silu(x):
    return jax.nn.silu(x)

def _sigmoid(x):
    return jax.nn.sigmoid(x)

def _layernorm(x, axis=-1, eps=1e-05):
    m = jnp.mean(x, axis=axis, keepdims=True)
    v = jnp.var(x, axis=axis, keepdims=True)
    return (x - m) / jnp.sqrt(v + eps)

def _scatter_add(tgt, idx, src, axis=0):
    return tgt.at[idx].add(src)

def _segment_sum(src, seg, n):
    return jax.ops.segment_sum(src, seg, n)
kernel_name = 'mk_adaln_ffn_d2_seqx_r4_91a8a2'

def setup_inputs(seed: int=0):
    np.random.seed(seed)
    _w = jnp.asarray

    def _rec_inputs():
        import jax
        import jax.numpy as jnp
        _rk = jax.random.key(seed)
        x = -0.0003929 + 0.9999 * jax.random.normal(jax.random.fold_in(_rk, 1), (32, 64, 512), jnp.float32)
        _lenS = 64 - jax.random.randint(jax.random.fold_in(_rk, 7), (32,), 0, max(1, 64 // 4) + 1, jnp.int32)
        _lenS2 = 64 - jax.random.randint(jax.random.fold_in(_rk, 8), (32,), 0, max(1, 64 // 4) + 1, jnp.int32)
        cond_1 = jax.random.uniform(jax.random.fold_in(_rk, 11), (32, 1), jnp.float32, 0.0, 1.37214)
        itok_B_0_6 = jax.random.randint(jax.random.fold_in(_rk, 12), (32,), 0, 7, jnp.int32)
        return (x, cond_1, itok_B_0_6)
    x, cond_1, itok_B_0_6 = _rec_inputs()

    def _L0_cond_setup():
        import jax, jax.numpy as jnp
        import numpy as np
        B, S, D_MODEL, NHEAD = (4, 512, 512, 16)
        HEAD_DIM = D_MODEL // NHEAD
        key = jax.random.key(seed)
        ks = jax.random.split(key, 6)
        scale = 1.0 / np.sqrt(D_MODEL)
        return {'hidden_states': jax.random.normal(ks[0], (B, S, D_MODEL), dtype=jnp.float32), 'attention_precision': jax.random.uniform(ks[1], (B, 1, 1), dtype=jnp.float32, minval=0.5, maxval=2.0), 'Wq': jax.random.normal(ks[2], (D_MODEL, D_MODEL), dtype=jnp.float32) * scale, 'Wk': jax.random.normal(ks[3], (D_MODEL, D_MODEL), dtype=jnp.float32) * scale, 'Wv': jax.random.normal(ks[4], (D_MODEL, D_MODEL), dtype=jnp.float32) * scale, 'Wo': jax.random.normal(ks[5], (D_MODEL, D_MODEL), dtype=jnp.float32) * scale}
    _L0_cond_all = _L0_cond_setup()
    _L0_cond_in = {k: v for k, v in _L0_cond_all.items() if k in ('Wq', 'Wk', 'Wv', 'Wo')}
    del _L0_cond_all

    def _L0_ffn_setup():
        import jax, jax.numpy as jnp
        import numpy as np
        HIDDEN = 512
        INTER = 1376
        LUT_SIZE = 16

        def _ghost_linear(x, idx, lut):
            w = lut[idx]
            return jnp.einsum('bsh,oh->bso', x, w)
        key = jax.random.key(seed)
        k_x, k_lut, k_g, k_u, k_d = jax.random.split(key, 5)
        x = jax.random.normal(k_x, (2, 1024, HIDDEN), dtype=jnp.float32)
        lut = jax.random.normal(k_lut, (LUT_SIZE,), dtype=jnp.float32) * 0.02
        gate_idx = jax.random.randint(k_g, (INTER, HIDDEN), 0, LUT_SIZE, dtype=jnp.int32)
        up_idx = jax.random.randint(k_u, (INTER, HIDDEN), 0, LUT_SIZE, dtype=jnp.int32)
        down_idx = jax.random.randint(k_d, (HIDDEN, INTER), 0, LUT_SIZE, dtype=jnp.int32)
        return {'x': x, 'lut': lut, 'gate_idx': gate_idx, 'up_idx': up_idx, 'down_idx': down_idx}
    _L0_ffn_all = _L0_ffn_setup()
    _L0_ffn_in = {k: v for k, v in _L0_ffn_all.items() if k in ('lut', 'gate_idx', 'up_idx', 'down_idx')}
    del _L0_ffn_all

    def _L1_cond_setup():
        import jax, jax.numpy as jnp
        import numpy as np
        B, T, D_IN, D_OUT = (16, 512, 512, 512)
        N_ADAPTERS, RANK = (8, 16)
        key = jax.random.key(seed)
        k_x, k_w, k_a, k_b, k_s, k_idx = jax.random.split(key, 6)
        x = jax.random.normal(k_x, (B, T, D_IN), dtype=jnp.float32)
        W = jax.random.normal(k_w, (D_OUT, D_IN), dtype=jnp.float32) * (1.0 / np.sqrt(D_IN))
        A = jax.random.normal(k_a, (N_ADAPTERS, RANK, D_IN), dtype=jnp.float32) * 0.02
        Bm = jax.random.normal(k_b, (N_ADAPTERS, D_OUT, RANK), dtype=jnp.float32) * 0.02
        scalings = jnp.ones((N_ADAPTERS,), dtype=jnp.float32)
        adapter_idx = jax.random.randint(k_idx, (B,), 0, N_ADAPTERS, dtype=jnp.int32)
        return {'x': x, 'W': W, 'A': A, 'Bm': Bm, 'scalings': scalings, 'adapter_idx': adapter_idx}
    _L1_cond_all = _L1_cond_setup()
    _L1_cond_in = {k: v for k, v in _L1_cond_all.items() if k in ('W', 'A', 'Bm', 'scalings')}
    del _L1_cond_all

    def _L1_ffn_setup():
        import jax, jax.numpy as jnp
        import numpy as np
        CAPACITY = 0.125
        HEAD_DIM = 128
        N_HEADS = 16
        N_KV_HEADS = 8
        ROPE_THETA = 10000.0
        EPS = 1e-06

        def _rms_norm(x, w):
            return x * jax.lax.rsqrt(jnp.mean(x * x, axis=-1, keepdims=True) + EPS) * w

        def _rotate_half(t):
            h = t.shape[-1] // 2
            return jnp.concatenate([-t[..., h:], t[..., :h]], axis=-1)
        key = jax.random.key(seed)
        ks = jax.random.split(key, 12)
        B, T, D = (4, 1024, 512)
        I = 2048
        s = 0.02
        return {'hidden_states': jax.random.normal(ks[0], (B, T, D), jnp.float32), 'w_router': jax.random.normal(ks[1], (D,), jnp.float32) * s, 'wq': jax.random.normal(ks[2], (D, N_HEADS * HEAD_DIM), jnp.float32) * s, 'bq': jnp.zeros((N_HEADS * HEAD_DIM,), jnp.float32), 'wk': jax.random.normal(ks[3], (D, N_KV_HEADS * HEAD_DIM), jnp.float32) * s, 'bk': jnp.zeros((N_KV_HEADS * HEAD_DIM,), jnp.float32), 'wv': jax.random.normal(ks[4], (D, N_KV_HEADS * HEAD_DIM), jnp.float32) * s, 'bv': jnp.zeros((N_KV_HEADS * HEAD_DIM,), jnp.float32), 'wo': jax.random.normal(ks[5], (N_HEADS * HEAD_DIM, D), jnp.float32) * s, 'w_gate': jax.random.normal(ks[6], (D, I), jnp.float32) * s, 'w_up': jax.random.normal(ks[7], (D, I), jnp.float32) * s, 'w_down': jax.random.normal(ks[8], (I, D), jnp.float32) * s, 'ln1_w': jnp.ones((D,), jnp.float32), 'ln2_w': jnp.ones((D,), jnp.float32)}
    _L1_ffn_all = _L1_ffn_setup()
    _L1_ffn_in = {k: v for k, v in _L1_ffn_all.items() if k in ('w_router', 'wq', 'bq', 'wk', 'bk', 'wv', 'bv', 'wo', 'w_gate', 'w_up', 'w_down', 'ln1_w', 'ln2_w')}
    del _L1_ffn_all
    return {'x': x, 'cond_1': cond_1, 'itok_B_0_6': itok_B_0_6, 'L0_cond_Wq': _L0_cond_in['Wq'], 'L0_cond_Wk': _L0_cond_in['Wk'], 'L0_cond_Wv': _L0_cond_in['Wv'], 'L0_cond_Wo': _L0_cond_in['Wo'], 'L0_ffn_lut': _L0_ffn_in['lut'], 'L0_ffn_gate_idx': _L0_ffn_in['gate_idx'], 'L0_ffn_up_idx': _L0_ffn_in['up_idx'], 'L0_ffn_down_idx': _L0_ffn_in['down_idx'], 'L1_cond_W': _L1_cond_in['W'], 'L1_cond_A': _L1_cond_in['A'], 'L1_cond_Bm': _L1_cond_in['Bm'], 'L1_cond_scalings': _L1_cond_in['scalings'], 'L1_ffn_w_router': _L1_ffn_in['w_router'], 'L1_ffn_wq': _L1_ffn_in['wq'], 'L1_ffn_bq': _L1_ffn_in['bq'], 'L1_ffn_wk': _L1_ffn_in['wk'], 'L1_ffn_bk': _L1_ffn_in['bk'], 'L1_ffn_wv': _L1_ffn_in['wv'], 'L1_ffn_bv': _L1_ffn_in['bv'], 'L1_ffn_wo': _L1_ffn_in['wo'], 'L1_ffn_w_gate': _L1_ffn_in['w_gate'], 'L1_ffn_w_up': _L1_ffn_in['w_up'], 'L1_ffn_w_down': _L1_ffn_in['w_down'], 'L1_ffn_ln1_w': _L1_ffn_in['ln1_w'], 'L1_ffn_ln2_w': _L1_ffn_in['ln2_w']}

def reference(x, cond_1, itok_B_0_6, L0_cond_Wq, L0_cond_Wk, L0_cond_Wv, L0_cond_Wo, L0_ffn_lut, L0_ffn_gate_idx, L0_ffn_up_idx, L0_ffn_down_idx, L1_cond_W, L1_cond_A, L1_cond_Bm, L1_cond_scalings, L1_ffn_w_router, L1_ffn_wq, L1_ffn_bq, L1_ffn_wk, L1_ffn_bk, L1_ffn_wv, L1_ffn_bv, L1_ffn_wo, L1_ffn_w_gate, L1_ffn_w_up, L1_ffn_w_down, L1_ffn_ln1_w, L1_ffn_ln2_w):
    import jax
    import jax.numpy as jnp

    def _L0_cond_ref(hidden_states, attention_precision, Wq, Wk, Wv, Wo):
        import jax, jax.numpy as jnp
        import numpy as np
        B, S, D_MODEL, NHEAD = (4, 512, 512, 16)
        HEAD_DIM = D_MODEL // NHEAD
        b, s, _ = hidden_states.shape

        def proj(x, W):
            y = jnp.einsum('bsd,ed->bse', x, W)
            return y.reshape(b, s, NHEAD, HEAD_DIM).transpose(0, 2, 1, 3)
        q = proj(hidden_states, Wq)
        k = proj(hidden_states, Wk)
        v = proj(hidden_states, Wv)
        beta = jnp.minimum(attention_precision, 4.0)[:, None]
        q = q * beta
        scores = jnp.einsum('bhqd,bhkd->bhqk', q, k) / np.sqrt(HEAD_DIM)
        causal = jnp.tril(jnp.ones((s, s), dtype=bool))
        scores = jnp.where(causal, scores, jnp.finfo(scores.dtype).min)
        attn = jax.nn.softmax(scores, axis=-1)
        out = jnp.einsum('bhqk,bhkd->bhqd', attn, v)
        out = out.transpose(0, 2, 1, 3).reshape(b, s, D_MODEL)
        return jnp.einsum('bsd,ed->bse', out, Wo)

    def _L0_ffn_ref(x, lut, gate_idx, up_idx, down_idx):
        import jax, jax.numpy as jnp
        import numpy as np
        HIDDEN = 512
        INTER = 1376
        LUT_SIZE = 16

        def _ghost_linear(x, idx, lut):
            w = lut[idx]
            return jnp.einsum('bsh,oh->bso', x, w)
        gate = _ghost_linear(x, gate_idx, lut)
        up = _ghost_linear(x, up_idx, lut)
        h = jax.nn.silu(gate) * up
        return _ghost_linear(h, down_idx, lut)

    def _L1_cond_ref(x, W, A, Bm, scalings, adapter_idx):
        import jax, jax.numpy as jnp
        import numpy as np
        B, T, D_IN, D_OUT = (16, 512, 512, 512)
        N_ADAPTERS, RANK = (8, 16)
        H = jnp.einsum('btd,od->bto', x, W)
        A_b = A[adapter_idx]
        B_b = Bm[adapter_idx]
        s_b = scalings[adapter_idx]
        xa = jnp.einsum('btd,brd->btr', x, A_b)
        delta = jnp.einsum('btr,bor->bto', xa, B_b)
        delta = jax.lax.stop_gradient(delta * s_b[:, None, None])
        return H + delta

    def _L1_ffn_ref(hidden_states, w_router, wq, bq, wk, bk, wv, bv, wo, w_gate, w_up, w_down, ln1_w, ln2_w):
        import jax, jax.numpy as jnp
        import numpy as np
        CAPACITY = 0.125
        HEAD_DIM = 128
        N_HEADS = 16
        N_KV_HEADS = 8
        ROPE_THETA = 10000.0
        EPS = 1e-06

        def _rms_norm(x, w):
            return x * jax.lax.rsqrt(jnp.mean(x * x, axis=-1, keepdims=True) + EPS) * w

        def _rotate_half(t):
            h = t.shape[-1] // 2
            return jnp.concatenate([-t[..., h:], t[..., :h]], axis=-1)
        B, T, D = hidden_states.shape
        k = max(1, int(T * CAPACITY))
        scores = jnp.einsum('btd,d->bt', hidden_states, w_router)
        _, idx = jax.lax.top_k(scores, k)
        idx = jnp.sort(idx, axis=-1)
        b = jnp.arange(B)[:, None]
        sel = hidden_states[b, idx]
        sel_scores = scores[b, idx]
        S = B * k
        x = sel.reshape(S, D)
        pos = idx.reshape(S)
        inv_freq = 1.0 / ROPE_THETA ** (jnp.arange(0, HEAD_DIM, 2, dtype=jnp.float32) / HEAD_DIM)
        ang = pos.astype(jnp.float32)[:, None] * inv_freq
        cos = jnp.concatenate([jnp.cos(ang), jnp.cos(ang)], axis=-1)[:, None, :]
        sin = jnp.concatenate([jnp.sin(ang), jnp.sin(ang)], axis=-1)[:, None, :]
        h = _rms_norm(x, ln1_w)
        q = (h @ wq + bq).reshape(S, N_HEADS, HEAD_DIM)
        kk = (h @ wk + bk).reshape(S, N_KV_HEADS, HEAD_DIM)
        v = (h @ wv + bv).reshape(S, N_KV_HEADS, HEAD_DIM)
        q = q * cos + _rotate_half(q) * sin
        kk = kk * cos + _rotate_half(kk) * sin
        rep = N_HEADS // N_KV_HEADS
        kk = jnp.repeat(kk, rep, axis=1)
        v = jnp.repeat(v, rep, axis=1)
        att = jnp.einsum('shd,thd->hst', q, kk) / np.sqrt(HEAD_DIM)
        causal = jnp.tril(jnp.ones((S, S), bool))
        att = jnp.where(causal[None], att, jnp.finfo(att.dtype).min)
        att = jax.nn.softmax(att, axis=-1)
        attn_out = jnp.einsum('hst,thd->shd', att, v).reshape(S, N_HEADS * HEAD_DIM) @ wo
        x1 = x + attn_out
        h2 = _rms_norm(x1, ln2_w)
        mlp = jax.nn.silu(h2 @ w_gate) * (h2 @ w_up) @ w_down
        processed = x1 + mlp
        gate = jax.nn.sigmoid(sel_scores).reshape(S, 1)
        gated = gate * processed + (1.0 - gate) * x
        output = hidden_states.at[b, idx].set(gated.reshape(B, k, D))
        return output
    x = x + _L0_ffn_ref(_L0_cond_ref(x, cond_1[:, None, :], L0_cond_Wq, L0_cond_Wk, L0_cond_Wv, L0_cond_Wo), L0_ffn_lut, L0_ffn_gate_idx, L0_ffn_up_idx, L0_ffn_down_idx)
    x = x + _L1_ffn_ref(_L1_cond_ref(x, L1_cond_W, L1_cond_A, L1_cond_Bm, L1_cond_scalings, itok_B_0_6), L1_ffn_w_router, L1_ffn_wq, L1_ffn_bq, L1_ffn_wk, L1_ffn_bk, L1_ffn_wv, L1_ffn_bv, L1_ffn_wo, L1_ffn_w_gate, L1_ffn_w_up, L1_ffn_w_down, L1_ffn_ln1_w, L1_ffn_ln2_w)
    return x

_drawn_inputs = setup_inputs


def setup_inputs(seed=0):
    import zlib

    import numpy as np

    out = dict(_drawn_inputs(seed))
    spreads = {'L1_cond_scalings': (1.0, 0.6),
     'L1_ffn_bq': (0.0, 0.8),
     'L1_ffn_bk': (0.0, 0.8),
     'L1_ffn_bv': (0.0, 0.566),
     'L1_ffn_ln1_w': (1.0, 0.6),
     'L1_ffn_ln2_w': (1.0, 0.6)}
    factors = {'L1_ffn_wq': 8.0,
     'L1_ffn_wk': 8.0,
     'L1_ffn_wv': 4.239,
     'L1_ffn_wo': 2.851,
     'L1_ffn_w_gate': 3.253,
     'L1_ffn_w_up': 3.187,
     'L1_ffn_w_down': 3.17}
    for name, (base, spread) in spreads.items():
        noise = np.random.default_rng([zlib.crc32(name.encode()), seed]).standard_normal(out[name].shape)
        drawn = base * np.exp(spread * noise) if base else spread * noise
        out[name] = jnp.asarray(drawn.astype(out[name].dtype))
    for name, factor in factors.items():
        out[name] = (out[name] * factor).astype(out[name].dtype)
    return out
```

```python
import concourse.bass as bass
from concourse import mybir
from contextlib import ExitStack

F32 = mybir.dt.float32
F32R = mybir.dt.float32r
BF16 = mybir.dt.bfloat16
I32 = mybir.dt.int32
ALU = mybir.AluOpType
ACT = mybir.ActivationFunctionType
AX = mybir.AxisListType.X

P = 128
B, S, D = 32, 64, 512
KD = D // P
TOK = B * S
INTER = 1376
NBLK = -(-INTER // P)
LAST = INTER - (NBLK - 1) * P
NH0, HD0 = 16, 32
CA = 256
NCA = TOK // CA
BC = CA // S
NP_ = BC // 2
CF = 512
NCF = TOK // CF
BLKW = 3 * D
HALF = BLKW // 2
LUTN = 16
GROUPS = [(0, 4), (4, 3), (7, 4)]
PASSES = [(0, 0), (0, 1), (1, 0)]


NPAIR = B // 2
NA, RANK = 8, 16
TOPK = 8
SEL = B * TOPK
NSB = SEL // P
NHQ, NHKV, HD = 16, 8, 128
HG = 4
I1 = 2048
NF1 = I1 // P
EPS = 1e-6
ROPE_W = HD // 2
TABW = 3 * ROPE_W + 1


def adaln_ffn_kernel(nc, xT, w0, idx, lut, cond, causal, w1, aT, bmT, tokens_adapter, adapter_of_row, scalings,
                     router, slots, rope, causal2, pair_base, ln, wq, wk, wv, bias, wo, wgate, wup, wdown,
                     y_dram, h_dram, out):
    ctx = ExitStack()
    with ctx:
        base = [-(-nc.sbuf_base // 64) * 64]
        start = base[0]

        def at(name, offset, shape, dt):
            return nc.alloc_sbuf_tensor_at(name, [P] + shape, dt, offset=start + offset)

        def sem(name):
            return ctx.enter_context(nc.semaphore(name))

        ident = at("ident", 0, [P], F32)
        mask = at("mask", 512, [4 * S], F32)
        beta = at("beta", 1536, [B // 2], F32)
        lut_sb = at("lut_sb", 1600, [LUTN], F32)
        rowmax = at("rowmax", 1664, [NP_, NH0], F32)
        rowsum = at("rowsum", 1792, [NP_, NH0], F32)
        rowinv = at("rowinv", 1920, [NP_, NH0], F32)
        K1 = 2048
        SLOT = BLKW * 4
        wtabA = [at(f"wtabA{i}", K1 + 4 * SLOT * i, [4 * BLKW], F32R) for i in range(2)]
        K2 = K1 + 8 * SLOT
        idx_raw = at("idx_raw", K2, [HALF], I32)
        idx_bf = at("idx_bf", K2 + 4 * HALF, [HALF], BF16)
        onehot = at("onehot", K2 + 6 * HALF, [3, HALF], BF16)
        lut_acc = at("lut_acc", K2 + 12 * HALF, [HALF], F32)
        K3 = K2 + 16 * HALF
        w_raw = [at(f"w_raw{n}", K1 + 4 * SLOT * (n // 2) + SLOT + 8192 * (n % 2), [KD, D], F32) for n in range(4)]
        o = K3
        w_sb = []
        for n in range(4):
            w_sb.append([at(f"w_sb{n}_{i}", o + 8192 * i, [KD, D], F32R) for i in range(2)])
            o += 16384
        xr = at("xr", o, [KD, CA], F32); o += 4096
        xs = [at(f"xs{i}", o + 4096 * i, [KD, CA], F32R) for i in range(2)]; o += 8192
        qT = at("qT", o, [KD, CA], F32); o += 4096
        kbd = at("kbd", o, [KD, BC, 4 * S], F32); o += 16384
        vbd = at("vbd", o, [BC, NH0 // 2, 2 * HD0], F32); o += 8192
        prob = at("prob", o, [NP_, NH0, S], F32); o += 8192
        probT = at("probT", o, [NP_, NH0 // 2, P], F32); o += 8192
        oN = at("oN", o, [NP_, D], F32); o += 4096
        oT = [at(f"oT{i}", o + 4096 * i, [KD, CA], F32R) for i in range(2)]; o += 8192
        yc = at("yc", o, [KD, CA], F32); o += 4096
        o = K3
        y_raw = at("y_raw", o, [KD, TOK], F32)
        ys = [at("ys1", o, [KD, TOK], F32R)]; o += 32768
        ys.insert(0, at("ys0", o, [KD, TOK], F32R)); o += 32768
        x1 = at("x1", o, [KD, TOK], F32); o += 32768
        wtabB = [at(f"wtabB{i}", o + 3 * SLOT * i, [3 * BLKW], F32R) for i in range(2)]; o += 6 * SLOT
        sg = at("sg", o, [2, CF], F32); o += 4096
        hf = at("hf", o, [2, CF], F32); o += 4096
        hs = [at(f"hs{i}", o + 4096 * i, [2, CF], F32R) for i in range(2)]; o += 8192
        small = o
        o += 8192
        assert start + o <= nc.sbuf_usable_end, (start + o, nc.sbuf_usable_end)

        def little(name, shape, dt=F32):
            nonlocal small
            n = 1
            for x in shape:
                n *= x
            t = at(name, small, shape, dt)
            small += -(-4 * n // 32) * 32
            return t

        router_sb = little("router_sb", [D])
        slots_sb = little("slots_sb", [2 * TOPK])
        rope_sb = little("rope_sb", [TABW])
        mask2 = little("mask2", [3 * P])
        pair_sb = little("pair_sb", [NSB])
        ln_sb = little("ln_sb", [2, KD])
        tok_ad = little("tok_ad", [B], I32)
        tok_adf = little("tok_adf", [B])
        row_ad = little("row_ad", [1])
        scal_sb = little("scal_sb", [1])
        admask = little("admask", [B])
        score = little("score", [NPAIR])
        scoreT = little("scoreT", [P])
        replaced = little("replaced", [P])
        best = little("best", [2, TOPK])
        picked = little("picked", [P])
        rank = little("rank", [P])
        onesr = little("onesr", [S])
        rankT = little("rankT", [NPAIR])
        rowidx = little("rowidx", [NSB], I32)
        stat = little("stat", [8, NSB])
        assert small <= o

        AW, AI, AY, AX1, AB, AS = K1, K2, K3, K3 + 65536, K3 + 98304, K3 + 98304 + 6 * SLOT
        w1_raw = at("w1_raw", AB, [KD, D], F32)
        w1_sb = [at(f"w1_sb{i}", AB + 8192 + 8192 * i, [KD, D], F32R) for i in range(2)]
        a_raw = at("a_raw", AB + 24576, [KD, P], F32)
        a_sb = [at(f"a_sb{i}", AB + 26624 + 2048 * i, [KD, P], F32R) for i in range(2)]
        b_raw = at("b_raw", AB + 30720, [D], F32)
        b_sb = [at(f"b_sb{i}", AB + 32768 + 2048 * i, [D], F32R) for i in range(2)]
        x1c = at("x1c", AY, [2, KD, CF], F32)
        x1s = [at(f"x1s{i}", AY + 16384 + 16384 * i, [2, KD, CF], F32R) for i in range(2)]
        h_tile = at("h_tile", AS, [2, D], F32)
        out_tile = at("out_tile", AS + 4096, [2, D], F32)
        xa = at("xa", AS + 8192, [CF], F32)
        xas = [at(f"xas{i}", AS + 10240 + 2048 * i, [CF], F32R) for i in range(2)]
        prod = at("prod", AS + 14336, [D], F32)
        wq_sb = at("wq_sb", AW, [KD, NHQ * HD], F32)
        wk_sb = at("wk_sb", AW + 32768, [KD, NHKV * HD], F32)
        wv_sb = at("wv_sb", AY + 49152, [KD, NHKV * HD], F32)
        wo_sb = at("wo_sb", AX1, [NHQ, D], F32)
        wd_sb = at("wd_sb", AB, [NF1, D], F32)
        bias_sb = at("bias_sb", AS, [(NHQ + 2 * NHKV) * HD], F32)
        qT2 = at("qT2", AY, [NHQ, SEL], F32)
        kT2 = at("kT2", AY + 16384, [NHKV, SEL], F32)
        v2 = at("v2", AY + 24576, [NSB, NHKV * HD], F32)
        hsel = at("hsel", AY + 32768, [NSB, D], F32)
        outsel = at("outsel", AY + 36864, [NSB, D], F32)
        hT = at("hT", AY + 40960, [KD, SEL], F32)
        xres = at("xres", AY + 45056, [NSB, D], F32)
        biased = at("biased", AI, [1, D], F32)
        times_cos = at("times_cos", AI + 4096, [D], F32)
        times_sin = at("times_sin", AI + 6144, [D], F32)
        turned = at("turned", AI + 8192, [D], F32)
        tables = at("tables", AI + 10240, [NSB, TABW], F32)
        pick = at("pick", AB + 32768, [NPAIR, 2 * TOPK], F32)
        scratch = at("scratch", AB + 33792, [D], F32)
        prob2 = at("prob2", AW, [2, HG, 3 * P], F32)
        prob2T = at("prob2T", AW + 12288, [2, HG, 3 * P], F32)
        oT2 = at("oT2", AW + 24576, [NHQ, SEL], F32)
        st2 = at("st2", AW + 40960, [4, HG, NSB], F32)
        h2T = at("h2T", AW + 45056, [KD, SEL], F32)
        wg_sb = [at("wg_sb0", AY + 49152, [KD // 2, I1], F32), at("wg_sb1", AS, [KD // 2, I1], F32)]
        wu_sb = at("wu_sb", AY, [KD, I1], F32)
        mT = at("mT", AW, [NF1, SEL], F32)
        sg1 = at("sg1", AW + 16384, [2, SEL], F32)
        fin = at("fin", AI, [NSB, D], F32)

        turned_b = at("turned_b", AI + 2048, [D], F32)
        hsel_normed = at("hsel_normed", AI, [NSB, D], F32)

        def turned_of(m):
            return turned[:, :] if m % 2 else turned_b[:, :]

        PS = ctx.enter_context(nc.psum_tensor("PS", [P, 8, 512], F32))

        def wtab(blk, part):
            if GROUPS[1][0] <= blk < GROUPS[2][0]:
                return wtabB[part][:, (blk - GROUPS[1][0]) * BLKW:(blk - GROUPS[1][0] + 1) * BLKW]
            s = blk if blk < GROUPS[1][0] else blk - GROUPS[2][0]
            return wtabA[part][:, s * BLKW:(s + 1) * BLKW]

        consts_in = sem("consts_in")
        ident_made = sem("ident_made")
        zeroed = sem("zeroed")
        beta_ready = sem("beta_ready")
        w_in = [sem(f"w_in{n}") for n in range(4)]
        w_hi = sem("w_hi")
        w_lo = sem("w_lo")
        x_in = sem("x_in")
        x_hi = sem("x_hi")
        x_lo = sem("x_lo")
        q_done = sem("q_done")
        k_done = sem("k_done")
        v_done = sem("v_done")
        q_copied = sem("q_copied")
        k_copied = sem("k_copied")
        v_copied = sem("v_copied")
        s_done = sem("s_done")
        shifted = sem("shifted")
        exped = sem("exped")
        pt_done = sem("pt_done")
        pt_copied = sem("pt_copied")
        pv_done = sem("pv_done")
        o_normed = sem("o_normed")
        ot_done = sem("ot_done")
        ot_hi = sem("ot_hi")
        ot_lo = sem("ot_lo")
        wo_done = sem("wo_done")
        y_copied = sem("y_copied")
        y_stored = sem("y_stored")
        soft = sem("soft")
        idx_in = sem("idx_in")
        lut_seq = sem("lut_seq")
        tab_ready = sem("tab_ready")
        y_in = sem("y_in")
        x1_in = sem("x1_in")
        y_hi = sem("y_hi")
        y_lo = sem("y_lo")
        gu_done = sem("gu_done")
        silu_done = sem("silu_done")
        mul_done = sem("mul_done")
        h_hi = sem("h_hi")
        h_lo = sem("h_lo")
        d_done = sem("d_done")
        acc_added = sem("acc_added")
        small_in = sem("small_in")
        w1_in = sem("w1_in")
        w1_hi = sem("w1_hi")
        w1_lo = sem("w1_lo")
        admask_made = sem("admask_made")
        x1_copied = sem("x1_copied")
        x1_hi = sem("x1_hi")
        x1_lo = sem("x1_lo")
        xa_done = sem("xa_done")
        xa_masked = sem("xa_masked")
        xa_hi = sem("xa_hi")
        xa_lo = sem("xa_lo")
        h_done = sem("h_done")
        xn_done = sem("xn_done")
        h_copied = sem("h_copied")
        scored = sem("scored")
        out_added = sem("out_added")
        h_stored = [sem(f"h_stored{i}") for i in range(2)]
        out_stored = [sem(f"out_stored{i}") for i in range(2)]
        top = sem("top")
        top_pe = sem("top_pe")
        rows_ready = sem("rows_ready")
        sel_in = sem("sel_in")
        outsel_in = sem("outsel_in")
        qkv_in = sem("qkv_in")
        wo_in = sem("wo_in")
        wd_in = sem("wd_in")
        bias_in = sem("bias_in")
        wg_in = sem("wg_in")
        wu_in = sem("wu_in")
        norm = sem("norm")
        root = sem("root")
        normed = sem("normed")
        ht_done = sem("ht_done")
        ht_copied = sem("ht_copied")
        qkv_done = sem("qkv_done")
        qkv_read = sem("qkv_read")
        rope_seq = sem("rope_seq")
        roped = sem("roped")
        rt_done = sem("rt_done")
        rt_copied = sem("rt_copied")
        s2_done = sem("s2_done")
        s2_masked = sem("s2_masked")
        s2_max = sem("s2_max")
        s2_exp = sem("s2_exp")
        s2_inv = sem("s2_inv")
        s2_norm = sem("s2_norm")
        p2t_done = sem("p2t_done")
        p2t_copied = sem("p2t_copied")
        pv2_done = sem("pv2_done")
        o2_copied = sem("o2_copied")
        wo2_done = sem("wo2_done")
        g2_done = sem("g2_done")
        silu2 = sem("silu2")
        mul2 = sem("mul2")
        d2_done = sem("d2_done")
        gate_seq = sem("gate_seq")
        gate_exp = sem("gate_exp")
        fin_ready = sem("fin_ready")
        scattered = sem("scattered")

        block = ctx.enter_context(nc.Block())

        NT = CF // P
        group_step = [sum(n for _, n in GROUPS[:g]) * NCF for g in range(len(GROUPS) + 1)]

        LUT_OPS = 2 * LUTN + 1

        @block.sync
        def _(sp):
            sp.dma_start(lut_sb[:, :], lut).then_inc(consts_in, 16)
            sp.dma_start(idx_raw[:, :], idx[0]).then_inc(idx_in, 16)
            for n in (1, 0, 2, 3):
                sp.dma_start(w_raw[n][:, :, :], w0[n]).then_inc(w_in[n], 16)
                if n == 1:
                    sp.dma_start(xr[:, :, :], xT[:, :, 0:CA]).then_inc(x_in, 16)
                    sp.dma_start(beta[:, :], cond).then_inc(consts_in, 16)
                    sp.dma_start(mask[:, :], causal).then_inc(consts_in, 16)
            sp.wait_ge(x_hi, 1)
            sp.wait_ge(x_lo, 1)
            sp.dma_start(xr[:, :, :], xT[:, :, CA:2 * CA]).then_inc(x_in, 16)

            def load_idx(h):
                sp.wait_ge(lut_seq, LUT_OPS * (h - 1) + 1)
                sp.dma_start(idx_raw[:, :], idx[bass.ds(h, 1)].rearrange("a p n -> (a p) n")).then_inc(idx_in, 16)

            def turn(i):
                sp.wait_ge(x_hi, i + 2)
                sp.wait_ge(x_lo, i + 2)
                sp.dma_start(xr[:, :, :], xT[:, :, bass.ds((i + 2) * CA, CA)]).then_inc(x_in, 16)

            def store_y(c):
                sp.wait_ge(y_copied, 2 * c + 2)
                sp.dma_start(y_dram[:, :, bass.ds(c * CA, CA)], yc[:, :, :]).then_inc(y_stored, 16)

            load_idx(1)
            turn(0)
            with sp.Fori(1, NCA - 2) as i:
                store_y(i - 1)
                load_idx(i + 1)
                turn(i)
            for c in range(NCA - 3, NCA):
                store_y(c)
                if c + 2 < NCA + 1:
                    load_idx(c + 2)
            sp.wait_ge(y_stored, 16 * NCA)
            for c in range(NCF):
                sp.dma_start(y_raw[:, :, c * CF:(c + 1) * CF], y_dram[:, :, c * CF:(c + 1) * CF]).then_inc(y_in, 16)
            sp.dma_start(x1[:, :, :], xT).then_inc(x1_in, 16)
            with sp.Fori(NCA + 1, 2 * NBLK) as h:
                load_idx(h)
            for dst, src in ((router_sb, router), (slots_sb, slots), (rope_sb, rope), (mask2, causal2), (pair_sb, pair_base),
                             (tok_ad, tokens_adapter), (row_ad, adapter_of_row), (scal_sb, scalings)):
                sp.dma_start(dst[:, :], src).then_inc(small_in, 16)
            sp.dma_start(ln_sb[:, :, :], ln).then_inc(small_in, 16)
            sp.wait_ge(d_done, group_step[2])
            sp.dma_start(w1_raw[:, :, :], w1).then_inc(w1_in, 16)
            sp.dma_start(a_raw[:, :, :], aT).then_inc(w1_in, 16)
            sp.dma_start(b_raw[:, :], bmT).then_inc(w1_in, 16)
            sp.wait_ge(d_done, group_step[3])
            sp.dma_start(wq_sb[:, :, :], wq).then_inc(qkv_in, 16)
            sp.dma_start(wk_sb[:, :, :], wk).then_inc(qkv_in, 16)
            sp.dma_start(wv_sb[:, :, :], wv).then_inc(qkv_in, 16)

            def tile_rows(dram, n):
                return dram.rearrange("(n p) d -> n p d", p=P)[bass.ds(n, 1)].rearrange("a p d -> (a p) d")

            def store_tiles(c, u):
                for t in range(NT):
                    n = NT * (c + u) + t
                    sp.wait_ge(h_copied, n + 1)
                    sp.dma_start(tile_rows(h_dram, n), h_tile[:, t % 2, :]).then_inc(h_stored[t % 2], 16)
                    sp.wait_ge(out_added, n + 1)
                    sp.dma_start(tile_rows(out, n), out_tile[:, t % 2, :]).then_inc(out_stored[t % 2], 16)

            with sp.Fori(0, NCF // 2) as pair:
                for u in range(2):
                    store_tiles(2 * pair, u)
            sp.wait_ge(h_done, NPAIR)
            sp.wait_ge(xn_done, NPAIR)
            sp.dma_start(wo_sb[:, :, :], wo).then_inc(wo_in, 16)
            sp.dma_start(wd_sb[:, :, :], wdown).then_inc(wd_in, 16)
            for i in range(2):
                sp.wait_ge(h_stored[i], 16 * NPAIR // 2)
                sp.wait_ge(out_stored[i], 16 * NPAIR // 2)
            sp.wait_ge(scored, NPAIR)
            sp.dma_start(bias_sb[:, :], bias).then_inc(bias_in, 16)
            sp.wait_ge(qkv_done, 16)
            sp.dma_start(wg_sb[0][:, :, :], wgate[:, 0:2, :]).then_inc(wg_in, 16)
            sp.wait_ge(qkv_read, 16)
            sp.dma_start(wg_sb[1][:, :, :], wgate[:, 2:4, :]).then_inc(wg_in, 16)
            sp.wait_ge(pv2_done, NHQ)
            sp.dma_start(wu_sb[:, :, :], wup).then_inc(wu_in, 16)

        @block.gpsimd
        def _(pool):
            nc.gpsimd.memset(ident[:, :], 0.0).then_inc(ident_made, 1)
            pool.wait_ge(ident_made, 1)
            nc.gpsimd.affine_select(out=ident[:, :], in_=ident[:, :], compare_op=ALU.not_equal, fill=1.0,
                                    base=0, pattern=[[-1, P]], channel_multiplier=1).then_inc(ident_made, 1)
            nc.gpsimd.memset(kbd[:, :, :, :], 0.0).then_inc(zeroed, 1)
            nc.gpsimd.memset(vbd[:, :, :, :], 0.0).then_inc(zeroed, 1)
            nc.gpsimd.memset(onesr[:, :], 1.0).then_inc(zeroed, 1)

            pool.wait_ge(rows_ready, 1)
            for i in range(2):
                pool.wait_ge(h_stored[i], 16 * NPAIR // 2)
                pool.wait_ge(out_stored[i], 16 * NPAIR // 2)
            pool.wait_ge(h_done, NPAIR)
            pool.wait_ge(xn_done, NPAIR)
            for sb in range(NSB):
                nc.gpsimd.indirect_dma_start(out=hsel[:, sb, :], out_offset=None, in_=h_dram[:, :],
                                             in_offset=bass.IndirectOffsetOnAxis(ap=rowidx[:, sb:sb + 1], axis=0)
                                             ).then_inc(sel_in, 16)
            for sb in range(NSB):
                nc.gpsimd.indirect_dma_start(out=outsel[:, sb, :], out_offset=None, in_=out[:, :],
                                             in_offset=bass.IndirectOffsetOnAxis(ap=rowidx[:, sb:sb + 1], axis=0)
                                             ).then_inc(outsel_in, 16)
            for sb in range(NSB):
                pool.wait_ge(fin_ready, sb + 1)
                nc.gpsimd.indirect_dma_start(out=out[:, :],
                                             out_offset=bass.IndirectOffsetOnAxis(ap=rowidx[:, sb:sb + 1], axis=0),
                                             in_=fin[:, sb, :], in_offset=None).then_inc(scattered, 16)
            pool.wait_ge(scattered, 16 * NSB)

        @block.tensor
        def _(pe):
            def project(w, bank0, done):
                for e in range(KD):
                    out = PS[:, bank0 + e // 2, (e % 2) * CA:(e % 2 + 1) * CA]
                    n = 0
                    for k in range(KD):
                        for a, b in PASSES:
                            mm = nc.tensor.matmul(out, w_sb[w][a][:, k, e * P:(e + 1) * P], xs[b][:, k, :],
                                                  start=(n == 0), stop=(n == 3 * KD - 1))
                            n += 1
                    if e % 2:
                        mm.then_inc(done, 1)

            def keys(c):
                pe.wait_ge(x_hi, c + 1)
                pe.wait_ge(x_lo, c + 1)
                project(1, 6, k_done)

            def queries(c):
                pe.wait_ge(k_copied, 2 * c + 2)
                project(0, 6, q_done)

            def values(c):
                for t in range(NP_):
                    n = 0
                    for k in range(KD):
                        for a, b in PASSES:
                            mm = nc.tensor.matmul(PS[:, 4 + t, :], xs[a][:, k, t * P:(t + 1) * P], w_sb[2][b][:, k, :],
                                                  start=(n == 0), stop=(n == 3 * KD - 1))
                            n += 1
                    mm.then_inc(v_done, 1)

            def scores(c):
                pe.wait_ge(q_copied, 2 * c + 2)
                pe.wait_ge(k_copied, 2 * c + 2)
                for e in range(KD):
                    for b in range(BC):
                        j, t = b % 2, b // 2
                        mm = nc.tensor.matmul(PS[64 * j:64 * j + 64, e, t * 256:(t + 1) * 256],
                                              qT[:, e, b * S:(b + 1) * S], kbd[:, e, b, :], start=True, stop=True,
                                              skip_group_check=True)
                mm.then_inc(s_done, 1)

            def prob_transposes(c):
                for t in range(NP_):
                    pe.wait_ge(exped, 2 * c + t + 1)
                    for m in range(NH0 // 2):
                        mm = nc.tensor.transpose(PS[:, 2 * t + m // 4, (m % 4) * P:(m % 4 + 1) * P],
                                                 prob[:, t, 2 * m:2 * m + 2, :].rearrange("p a b -> p (a b)"),
                                                 ident[:, :])
                    mm.then_inc(pt_done, 1)

            def attend(c):
                pe.wait_ge(q_copied, 2 * min_next(c) + 2)
                pe.wait_ge(v_copied, 2 * c + 2)
                for t in range(NP_):
                    pe.wait_ge(pt_copied, 2 * c + t + 1)
                    for j in range(2):
                        for m in range(NH0 // 2):
                            mm = nc.tensor.matmul(PS[64 * j:64 * j + 64, 6 + t, m * 64:(m + 1) * 64],
                                                  probT[:, t, m, 64 * j:64 * j + 64], vbd[:, 2 * t + j, m, :],
                                                  start=True, stop=True, skip_group_check=True)
                    mm.then_inc(pv_done, 1)

            def out_transposes(c):
                if not (isinstance(c, int) and c == NCA - 1):
                    pe.wait_ge(v_copied, 2 * c + 4)
                for t in range(NP_):
                    pe.wait_ge(o_normed, 2 * c + t + 1)
                    for e in range(KD):
                        mm = nc.tensor.transpose(PS[:, 4 + t, e * P:(e + 1) * P], oN[:, t, e * P:(e + 1) * P], ident[:, :])
                    mm.then_inc(ot_done, 1)

            def out_project(c):
                pe.wait_ge(ot_hi, 2 * c + 2)
                pe.wait_ge(ot_lo, 2 * c + 2)
                for e in range(KD):
                    out = PS[:, 4 + e // 2, (e % 2) * CA:(e % 2 + 1) * CA]
                    n = 0
                    for k in range(KD):
                        for a, b in PASSES:
                            mm = nc.tensor.matmul(out, w_sb[3][a][:, k, e * P:(e + 1) * P], oT[b][:, k, :],
                                                  start=(n == 0), stop=(n == 3 * KD - 1))
                            n += 1
                    if e % 2:
                        mm.then_inc(wo_done, 1)

            def min_next(c):
                return c + 1 if not isinstance(c, int) else min(c + 1, NCA - 1)

            def turn(i, first=False, last=False):
                scores(i)
                if not first:
                    out_transposes(i - 1)
                if not last:
                    keys(i + 1)
                if not first:
                    out_project(i - 1)
                if not last:
                    queries(i + 1)
                prob_transposes(i)
                if not last:
                    if not first:
                        pe.wait_ge(y_copied, 2 * i)
                    values(i + 1)
                attend(i)

            pe.wait_ge(w_hi, 1)
            pe.wait_ge(w_lo, 1)
            pe.wait_ge(ident_made, 2)
            keys(0)
            pe.wait_ge(w_hi, 2)
            pe.wait_ge(w_lo, 2)
            queries(0)
            pe.wait_ge(w_hi, 3)
            pe.wait_ge(w_lo, 3)
            values(0)
            pe.wait_ge(w_hi, 4)
            pe.wait_ge(w_lo, 4)
            pe.wait_ge(v_copied, 2)
            turn(0, first=True)
            with pe.Fori(1, NCA - 1) as i:
                turn(i)
            turn(NCA - 1, last=True)
            out_transposes(NCA - 1)
            out_project(NCA - 1)

            def gate_up(g, f, c):
                s = group_step[g] + GROUPS[g][1] * c + f
                blk = GROUPS[g][0] + f
                p = f % 2
                if not (isinstance(s, int) and s < 2):
                    repeat = f == 0 and (GROUPS[g][1] % 2 and not (isinstance(c, int) and c == 0)
                                         or g and GROUPS[g - 1][1] % 2 and isinstance(c, int) and c == 0)
                    pe.wait_ge(mul_done, s if repeat else s - 1)
                if g == 0 and f == 0:
                    pe.wait_ge(y_hi, c + 1)
                    pe.wait_ge(y_lo, c + 1)
                if isinstance(c, int) and c == 0:
                    pe.wait_ge(tab_ready, 2 * blk + 2)
                w = [wtab(blk, a) for a in range(2)]
                for q in range(2):
                    n = 0
                    for k in range(KD):
                        for a, b in PASSES:
                            mm = nc.tensor.matmul(PS[:, 4 + 2 * p + q, :], w[a][:, q * D + k * P:q * D + (k + 1) * P],
                                                  ys[b][:, k, bass.ds(c * CF, CF)],
                                                  start=(n == 0), stop=(n == 3 * KD - 1))
                            n += 1
                mm.then_inc(gu_done, 1)

            def down(g, f, c):
                s = group_step[g] + GROUPS[g][1] * c + f
                blk = GROUPS[g][0] + f
                rows = P if blk < NBLK - 1 else LAST
                p = f % 2
                pe.wait_ge(h_hi, s + 1)
                pe.wait_ge(h_lo, s + 1)
                if f == 0 and not (g == 0 and isinstance(c, int) and c == 0):
                    pe.wait_ge(acc_added, 4 * (NCF * g + c))
                w = [wtab(blk, a) for a in range(2)]
                for d in range(KD):
                    for n, (a, b) in enumerate(PASSES):
                        mm = nc.tensor.matmul(PS[:, d, :], w[a][0:rows, 2 * D + d * P:2 * D + (d + 1) * P],
                                              hs[b][0:rows, p, :], start=(f == 0 and n == 0),
                                              stop=(f == GROUPS[g][1] - 1 and n == 2))
                mm.then_inc(d_done, 1)

            def ffn_chunk(g, c, before):
                for f in range(GROUPS[g][1]):
                    gate_up(g, f, c)
                    if f:
                        down(g, f - 1, c)
                    elif before is not None:
                        down(*before)

            before = None
            for g in range(len(GROUPS)):
                ffn_chunk(g, 0, before)
                with pe.Fori(1, NCF) as c:
                    ffn_chunk(g, c, (g, GROUPS[g][1] - 1, c - 1))
                before = (g, GROUPS[g][1] - 1, NCF - 1)
            down(*before)

            def linear_chunk(c, u, first=False):
                cu = c + u
                pe.wait_ge(x1_hi, cu + 1)
                pe.wait_ge(x1_lo, cu + 1)
                if u or not first:
                    pe.wait_ge(xa_masked, cu)
                n = 0
                for k in range(KD):
                    for a, b in PASSES:
                        mm = nc.tensor.matmul(PS[:, 4, :], a_sb[a][:, k, :], x1s[b][:, u, k, :],
                                              start=(n == 0), stop=(n == 3 * KD - 1))
                        n += 1
                mm.then_inc(xa_done, 1)
                pe.wait_ge(x1_copied, cu + 1)
                for t in range(NT):
                    m = NT * cu + t
                    if not (first and NT * u + t < 2):
                        pe.wait_ge(scored, m - 1)
                        pe.wait_ge(out_added, m - 1)
                    for k in range(KD):
                        mm = nc.tensor.transpose(PS[:, 2 + t % 2, k * P:(k + 1) * P], x1c[:, u, k, t * P:(t + 1) * P],
                                                 ident[:, :])
                    mm.then_inc(xn_done, 1)
                    n = 0
                    for k in range(KD):
                        for a, b in PASSES:
                            nc.tensor.matmul(PS[:, t % 2, :], x1s[a][:, u, k, t * P:(t + 1) * P], w1_sb[b][:, k, :],
                                             start=(n == 0), stop=False)
                            n += 1
                    if t == 0:
                        pe.wait_ge(xa_hi, cu + 1)
                        pe.wait_ge(xa_lo, cu + 1)
                    for n, (a, b) in enumerate(PASSES):
                        mm = nc.tensor.matmul(PS[:, t % 2, :], xas[a][:, t * P:(t + 1) * P], b_sb[b][:, :],
                                              start=False, stop=(n == 2))
                    mm.then_inc(h_done, 1)

            pe.wait_ge(w1_hi, 3)
            pe.wait_ge(w1_lo, 3)
            pe.wait_ge(acc_added, 4 * NCF * len(GROUPS))
            pe.wait_ge(mul_done, group_step[3])
            linear_chunk(0, 0, first=True)
            linear_chunk(0, 1, first=True)
            with pe.Fori(1, NCF // 2) as pair:
                c = 2 * pair
                for u in range(2):
                    linear_chunk(c, u)

            pe.wait_ge(scored, NPAIR)
            pe.wait_ge(out_added, NPAIR)
            nc.tensor.transpose(PS[0:NPAIR, 5, 0:P], score[:, :], ident[:, :]).then_inc(top_pe, 1)
            pe.wait_ge(top, 9)
            nc.tensor.transpose(PS[:, 6, 0:NPAIR], rank[0:NPAIR, :], ident[0:NPAIR, 0:NPAIR]).then_inc(top_pe, 1)
            pe.wait_ge(top, 11)
            for sb in range(NSB):
                mm = nc.tensor.matmul(PS[:, 7, sb * TABW:(sb + 1) * TABW],
                                      pick[:, 8 * sb:8 * sb + 8, :].rearrange("p a b -> p (a b)"), rope_sb[:, :],
                                      start=True, stop=True, skip_group_check=True)
            mm.then_inc(top_pe, 1)

            def rows_to_columns(src, bank):
                for sb in range(NSB):
                    for k in range(KD):
                        mm = nc.tensor.transpose(PS[:, bank + k // 2, (k % 2) * SEL + sb * P:(k % 2) * SEL + (sb + 1) * P],
                                                 src[:, sb, k * P:(k + 1) * P], ident[:, :])
                mm.then_inc(ht_done, 1)

            pe.wait_ge(normed, 1)
            rows_to_columns(xres, 4)
            pe.wait_ge(ht_copied, KD)
            pe.wait_ge(qkv_in, 48)
            tiles = [(w, n) for w, n in ((wq_sb, 4), (wk_sb, 2), (wv_sb, 2))]
            m = 0

            def turn_tile(m):
                pe.wait_ge(roped, m + 1)
                if m >= 2:
                    pe.wait_ge(rt_copied, m - 1)
                for h in range(4):
                    mm = nc.tensor.transpose(PS[:, 6 + m % 2, h * P:(h + 1) * P], turned_of(m)[:, h * P:(h + 1) * P],
                                             ident[:, :])
                mm.then_inc(rt_done, 1)

            for w, count in tiles:
                for nt in range(count):
                    for sb in range(NSB):
                        if m >= 4:
                            pe.wait_ge(qkv_read, m - 3)
                        for k in range(KD):
                            mm = nc.tensor.matmul(PS[:, m % 4, :], hT[:, k, sb * P:(sb + 1) * P],
                                                  w[:, k, nt * 512:(nt + 1) * 512], start=(k == 0), stop=(k == KD - 1))
                        mm.then_inc(qkv_done, 1)
                        if 2 <= m < 14:
                            turn_tile(m - 2)
                        m += 1

            pe.wait_ge(rt_copied, 12)
            pe.wait_ge(qkv_read, 16)

            def scores2(g):
                if g:
                    pe.wait_ge(s2_masked, g)
                for j in range(HG):
                    h = HG * g + j
                    nc.tensor.matmul(PS[:, j, 0:P], qT2[:, h, 0:P], kT2[:, h // 2, 0:P], start=True, stop=True,
                                     skip_group_check=True)
                    mm = nc.tensor.matmul(PS[:, j, P:3 * P], qT2[:, h, P:SEL], kT2[:, h // 2, :], start=True, stop=True,
                                          skip_group_check=True)
                mm.then_inc(s2_done, 1)

            def attend2(g):
                pe.wait_ge(s2_norm, 2 * g + 2)
                for j in range(HG):
                    h = HG * g + j
                    if h >= 2:
                        pe.wait_ge(p2t_copied, h - 1)
                    for n in range(3):
                        mm = nc.tensor.transpose(PS[:, 4 + h % 2, n * P:(n + 1) * P],
                                                 prob2[:, g % 2, j, n * P:(n + 1) * P], ident[:, :])
                    mm.then_inc(p2t_done, 1)
                    if j:
                        values2(h - 1)
                values2(HG * g + HG - 1)

            def values2(h):
                g, j = h // HG, h % HG
                pe.wait_ge(p2t_copied, h + 1)
                if h >= 2:
                    pe.wait_ge(o2_copied, h - 1)
                o = 6 + h % 2
                hv = slice((h // 2) * HD, (h // 2 + 1) * HD)
                nc.tensor.matmul(PS[:, o, 0:SEL], v2[:, 0, hv], prob2T[:, g % 2, j, 0:SEL], start=True, stop=False)
                nc.tensor.matmul(PS[:, o, P:SEL], v2[:, 1, hv], prob2T[:, g % 2, j, SEL:3 * P],
                                 start=False, stop=True).then_inc(pv2_done, 1)

            scores2(0)
            for g in range(NHQ // HG):
                if g + 1 < NHQ // HG:
                    scores2(g + 1)
                attend2(g)

            pe.wait_ge(o2_copied, NHQ)
            pe.wait_ge(wo_in, 16)
            for sb in range(NSB):
                for h in range(NHQ):
                    mm = nc.tensor.matmul(PS[:, sb, :], oT2[:, h, sb * P:(sb + 1) * P], wo_sb[:, h, :],
                                          start=(h == 0), stop=(h == NHQ - 1))
                mm.then_inc(wo2_done, 1)

            pe.wait_ge(normed, 2)
            rows_to_columns(hsel_normed, 4)
            pe.wait_ge(ht_copied, 2 * KD)
            pe.wait_ge(wg_in, 32)
            pe.wait_ge(wu_in, 16)
            pe.wait_ge(wd_in, 16)

            def gate_up2(f):
                if f >= 2:
                    pe.wait_ge(mul2, f - 1)
                bank = 4 + f % 2
                for q in range(2):
                    for k in range(KD):
                        w = wu_sb[:, k, f * P:(f + 1) * P] if q else wg_sb[k // 2][:, k % 2, f * P:(f + 1) * P]
                        mm = nc.tensor.matmul(PS[:, bank, q * SEL:(q + 1) * SEL], w, h2T[:, k, :],
                                              start=(k == 0), stop=(k == KD - 1))
                mm.then_inc(g2_done, 1)

            def down2(f):
                pe.wait_ge(mul2, f + 1)
                for sb in range(NSB):
                    mm = nc.tensor.matmul(PS[:, 2 + sb, :], mT[:, f, sb * P:(sb + 1) * P], wd_sb[:, f, :],
                                          start=(f == 0), stop=(f == NF1 - 1))
                mm.then_inc(d2_done, 1)

            gate_up2(0)
            for f in range(NF1):
                if f + 1 < NF1:
                    gate_up2(f + 1)
                down2(f)

        @block.scalar
        def _(act):
            order = (1, 0, 2, 3)
            for m, n in enumerate(order):
                act.wait_ge(w_in[n], 16)
                nc.scalar.copy(w_sb[n][0][:, :, :], w_raw[n][:, :, :]).then_inc(w_hi, 1)
                if m == 0:
                    act.wait_ge(x_in, 16)
                    nc.scalar.copy(xs[0][:, :, :], xr[:, :, :]).then_inc(x_hi, 1)

            def copy_keys(c, bank):
                act.wait_ge(k_done, 2 * c + bank + 1)
                for e in (2 * bank, 2 * bank + 1):
                    for h in range(4):
                        src = PS[32 * h:32 * h + 32, 6 + bank, (e % 2) * CA:(e % 2 + 1) * CA].rearrange("p (b t) -> p b t", b=BC)
                        ins = nc.scalar.copy(kbd[32 * h:32 * h + 32, e, :, h * S:(h + 1) * S], src)
                ins.then_inc(k_copied, 1)

            def copy_queries(c):
                for bank in range(2):
                    act.wait_ge(q_done, 2 * c + bank + 1)
                    nc.scalar.copy(qT[:, 2 * bank:2 * bank + 2, :].rearrange("p a b -> p (a b)"),
                                   PS[:, 6 + bank, :]).then_inc(q_copied, 1)

            def copy_values(c):
                for t in range(NP_):
                    act.wait_ge(v_done, 2 * c + t + 1)
                    for j in range(2):
                        for h in range(2):
                            src = PS[64 * j:64 * j + 64, 4 + t, :].rearrange("p (m h d) -> p m h d", h=2, d=HD0)[:, :, h, :]
                            ins = nc.scalar.copy(vbd[64 * h:64 * h + 64, 2 * t + j, :, h * HD0:(h + 1) * HD0], src)
                    ins.then_inc(v_copied, 1)

            def split_x(c):
                act.wait_ge(v_done, 2 * c)
                act.wait_ge(x_in, 16 * c + 16)
                nc.scalar.copy(xs[0][:, :, :], xr[:, :, :]).then_inc(x_hi, 1)

            def exps(c):
                for t in range(NP_):
                    act.wait_ge(shifted, 2 * c + t + 1)
                    pr = prob[:, t, :, :].rearrange("p a b -> p (a b)")
                    nc.scalar.activation(pr, pr, ACT.Exp).then_inc(exped, 1)

            def copy_prob(c):
                for t in range(NP_):
                    act.wait_ge(pt_done, 2 * c + t + 1)
                    nc.scalar.copy(probT[:, t, :, :].rearrange("p a b -> p (a b)"),
                                   PS[:, 2 * t:2 * t + 2, :].rearrange("p a b -> p (a b)")).then_inc(pt_copied, 1)

            def split_out(c):
                for t in range(NP_):
                    act.wait_ge(ot_done, 2 * c + t + 1)
                    nc.scalar.copy(oT[0][:, :, t * P:(t + 1) * P],
                                   PS[:, 4 + t, :].rearrange("p (e q) -> p e q", e=KD)).then_inc(ot_hi, 1)

            def copy_y(c, stored=True):
                if stored:
                    act.wait_ge(y_stored, 16 * c)
                for bank in range(2):
                    act.wait_ge(wo_done, 2 * c + bank + 1)
                    nc.scalar.copy(yc[:, 2 * bank:2 * bank + 2, :].rearrange("p a b -> p (a b)"),
                                   PS[:, 4 + bank, :]).then_inc(y_copied, 1)

            def turn(i, first=False, second=False, last=False, split=True):
                act.wait_ge(s_done, i + 1)
                if not first:
                    split_out(i - 1)
                if not last:
                    copy_keys(i + 1, 0)
                exps(i)
                if not last:
                    copy_keys(i + 1, 1)
                if not first:
                    copy_y(i - 1, stored=not second)
                if not last:
                    copy_queries(i + 1)
                copy_prob(i)
                if not last:
                    act.wait_ge(pv_done, 2 * i + 2)
                    copy_values(i + 1)
                    if split:
                        split_x(i + 2)

            act.wait_ge(zeroed, 2)
            copy_keys(0, 0)
            copy_keys(0, 1)
            copy_queries(0)
            copy_values(0)
            split_x(1)
            turn(0, first=True)
            turn(1, second=True)
            with act.Fori(2, NCA - 2) as i:
                turn(i)
            turn(NCA - 2, split=False)
            turn(NCA - 1, last=True)
            split_out(NCA - 1)
            copy_y(NCA - 1)

            for c in range(NCF):
                act.wait_ge(y_in, 16 * NCF)
                nc.scalar.copy(ys[0][:, :, c * CF:(c + 1) * CF], y_raw[:, :, c * CF:(c + 1) * CF]).then_inc(y_hi, 1)

            def ffn_step(g, f, c):
                s = group_step[g] + GROUPS[g][1] * c + f
                p = f % 2
                act.wait_ge(gu_done, s + 1)
                nc.scalar.activation(sg[:, p, :], PS[:, 4 + 2 * p, :], ACT.Silu).then_inc(silu_done, 1)
                act.wait_ge(mul_done, s + 1)
                if not (isinstance(s, int) and s < 2):
                    repeat = f == 0 and (GROUPS[g][1] % 2 and not (isinstance(c, int) and c == 0)
                                         or g and GROUPS[g - 1][1] % 2 and isinstance(c, int) and c == 0)
                    act.wait_ge(d_done, s if repeat else s - 1)
                nc.scalar.copy(hs[0][:, p, :], hf[:, p, :]).then_inc(h_hi, 1)

            for g in range(len(GROUPS)):
                if g == 2:
                    act.wait_ge(w1_in, 48)
                    nc.scalar.copy(w1_sb[0][:, :, :], w1_raw[:, :, :]).then_inc(w1_hi, 1)
                    nc.scalar.copy(a_sb[0][:, :, :], a_raw[:, :, :]).then_inc(w1_hi, 1)
                    nc.scalar.copy(b_sb[0][:, :], b_raw[:, :]).then_inc(w1_hi, 1)
                for f in range(GROUPS[g][1]):
                    ffn_step(g, f, 0)
                with act.Fori(1, NCF) as c:
                    for f in range(GROUPS[g][1]):
                        ffn_step(g, f, c)

            def split_x1(c, u, first=False):
                act.wait_ge(acc_added, 4 * (2 * NCF + c + u) + 4)
                if not first:
                    act.wait_ge(h_done, NT * (c + u) - NT)
                part = x1[:, :, bass.ds((c + u) * CF, CF)]
                nc.scalar.copy(x1s[0][:, u, :, :], part).then_inc(x1_hi, 1)
                nc.scalar.copy(x1c[:, u, :, :], part).then_inc(x1_copied, 1)

            def linear_tiles(c, u, first=False):
                cu = c + u
                act.wait_ge(xa_masked, cu + 1)
                if u or not first:
                    act.wait_ge(h_done, NT * cu)
                nc.scalar.copy(xas[0][:, :], xa[:, :]).then_inc(xa_hi, 1)
                for t in range(NT):
                    m = NT * cu + t
                    act.wait_ge(h_done, m + 1)
                    if not (first and NT * u + t < 2):
                        act.wait_ge(h_stored[t % 2], 16 * (NT // 2 * cu + t // 2))
                        act.wait_ge(out_added, m - 1)
                        act.wait_ge(scored, m - 1)
                    nc.scalar.copy(h_tile[:, t % 2, :], PS[:, t % 2, :]).then_inc(h_copied, 1)

            act.wait_ge(d_done, group_step[3])
            split_x1(0, 0, first=True)
            split_x1(0, 1, first=True)
            linear_tiles(0, 0, first=True)
            linear_tiles(0, 1, first=True)
            with act.Fori(1, NCF // 2) as pair:
                c = 2 * pair
                for u in range(2):
                    split_x1(c, u)
                for u in range(2):
                    linear_tiles(c, u)

            def root_of(n):
                act.wait_ge(norm, 9 * n + 3)
                nc.scalar.activation(stat[:, 1, :], stat[:, 0, :], ACT.Sqrt).then_inc(root, 1)

            def copy_columns(dst, n):
                act.wait_ge(ht_done, n + 1)
                for k in range(KD):
                    nc.scalar.activation(dst[:, k, :], PS[:, 4 + k // 2, (k % 2) * SEL:(k % 2 + 1) * SEL], ACT.Copy,
                                         scale=ln_sb[:, n, k:k + 1]).then_inc(ht_copied, 1)

            root_of(0)
            copy_columns(hT, 0)
            for m in range(12):
                act.wait_ge(rt_done, m + 1)
                head, sb = 4 * (m // 2), m % 2
                dst = qT2[:, head:head + 4, sb * P:(sb + 1) * P] if m < 8 else kT2[:, head - 16:head - 12, sb * P:(sb + 1) * P]
                nc.scalar.copy(dst, PS[:, 6 + m % 2, :].rearrange("p (h q) -> p h q", h=4)).then_inc(rt_copied, 1)

            def exps2(g):
                act.wait_ge(s2_max, 2 * g + 2)
                for j in range(HG):
                    for sb in range(NSB):
                        part = prob2[:, g % 2, j, sb * P:(2 * sb + 1) * P]
                        nc.scalar.activation(part, part, ACT.Exp, bias=st2[:, g % 2, j, sb:sb + 1],
                                             accum_out=st2[:, 2 + g % 2, j, sb:sb + 1]).then_inc(s2_exp, 1)

            def copy_attended(g):
                for j in range(HG):
                    h = HG * g + j
                    act.wait_ge(p2t_done, h + 1)
                    nc.scalar.copy(prob2T[:, g % 2, j, :], PS[:, 4 + h % 2, 0:3 * P]).then_inc(p2t_copied, 1)
                    if j:
                        copy_out(h - 1)
                copy_out(HG * g + HG - 1)

            def copy_out(h):
                act.wait_ge(pv2_done, h + 1)
                nc.scalar.copy(oT2[:, h, :], PS[:, 6 + h % 2, 0:SEL]).then_inc(o2_copied, 1)

            exps2(0)
            for g in range(NHQ // HG):
                if g + 1 < NHQ // HG:
                    exps2(g + 1)
                copy_attended(g)
            act.wait_ge(gate_seq, 1)
            nc.scalar.activation(stat[:, 6, :], stat[:, 5, :], ACT.Exp, scale=-1.0).then_inc(gate_exp, 1)
            root_of(1)
            copy_columns(h2T, 1)
            for f in range(NF1):
                act.wait_ge(g2_done, f + 1)
                nc.scalar.activation(sg1[:, f % 2, :], PS[:, 4 + f % 2, 0:SEL], ACT.Silu).then_inc(silu2, 1)

        @block.vector
        def _(dve):
            def lut_part(h, dst, v0, v1, at_op):
                n = at_op

                def counted(ins):
                    nonlocal n
                    ins.then_inc(lut_seq, 1)
                    n += 1
                    return n

                if v0 == 0:
                    dve.wait_ge(idx_in, 16 * h + 16)
                    seen = counted(nc.vector.tensor_copy(idx_bf[:, :], idx_raw[:, :]))
                    dve.wait_ge(lut_seq, LUT_OPS * h + seen)
                    seen = counted(nc.vector.tensor_scalar(lut_acc[:, :], idx_bf[:, :], 0.0, lut_sb[:, 0:1],
                                                           ALU.is_equal, ALU.mult))
                    v0 = 1
                else:
                    seen = n
                made = {}
                for v in range(v0, v1 + 1):
                    if v < v1:
                        ins = nc.vector.tensor_scalar(onehot[:, v % 3, :], idx_bf[:, :], float(v), None, ALU.is_equal)
                        made[v] = counted(ins)
                    if v > v0:
                        u = v - 1
                        dve.wait_ge(lut_seq, LUT_OPS * h + max(made[u], seen))
                        seen = counted(nc.vector.scalar_tensor_tensor(
                            lut_acc[:, :], onehot[:, u % 3, :], lut_sb[:, u:u + 1], lut_acc[:, :], ALU.mult, ALU.add))
                if v1 == LUTN:
                    dve.wait_ge(lut_seq, LUT_OPS * h + seen)
                    done = counted(nc.vector.tensor_copy(dst[0], lut_acc[:, :]))
                    dve.wait_ge(lut_seq, LUT_OPS * h + done)
                    nc.vector.tensor_tensor(dst[1], lut_acc[:, :], dst[0].bitcast(F32), ALU.subtract).then_inc(tab_ready, 1)
                return n

            SOFT = 8

            def split_w(m, n):
                dve.wait_ge(w_hi, m + 1)
                nc.vector.tensor_tensor(w_sb[n][1][:, :, :], w_raw[n][:, :, :], w_sb[n][0][:, :, :].bitcast(F32),
                                        ALU.subtract).then_inc(w_lo, 1)

            def split_x(c):
                dve.wait_ge(x_hi, c + 1)
                nc.vector.tensor_tensor(xs[1][:, :, :], xr[:, :, :], xs[0][:, :, :].bitcast(F32),
                                        ALU.subtract).then_inc(x_lo, 1)

            split_w(0, 1)
            split_x(0)
            split_w(1, 0)
            split_w(2, 2)
            split_w(3, 3)
            dve.wait_ge(consts_in, 48)
            nc.vector.tensor_scalar(beta[:, :], beta[:, :], 4.0, float(HD0) ** -0.5, ALU.min, ALU.mult).then_inc(beta_ready, 1)
            dve.wait_ge(beta_ready, 1)
            split_x(1)

            def scale_and_mask(i):
                dve.wait_ge(s_done, i + 1)
                if not (isinstance(i, int) and i == 0):
                    dve.wait_ge(pt_done, 2 * i)
                for t in range(NP_):
                    out = prob[:, t, :, :].rearrange("p (e h) k -> p e (h k)", e=KD)
                    src = PS[:, 0:KD, t * 256:(t + 1) * 256]
                    m4 = mask[:, :].unsqueeze(1).to_broadcast([P, KD, 4 * S])
                    nc.vector.scalar_tensor_tensor(out, src, beta[:, bass.ds(2 * i + t, 1)], m4,
                                                   ALU.mult, ALU.add).then_inc(soft, 1)

            def subtract_max(i):
                b0 = SOFT * i
                for t in range(NP_):
                    dve.wait_ge(soft, b0 + 1 + t)
                    nc.vector.tensor_reduce(rowmax[:, t, :], prob[:, t, :, :], AX, ALU.max).then_inc(soft, 1)
                for t in range(NP_):
                    dve.wait_ge(soft, b0 + 3 + t)
                    nc.vector.tensor_tensor(prob[:, t, :, :], prob[:, t, :, :],
                                            rowmax[:, t, :].unsqueeze(2).to_broadcast([P, NH0, S]),
                                            ALU.subtract).then_inc(shifted, 1)

            def sums(i):
                b0 = SOFT * i + 4
                for t in range(NP_):
                    dve.wait_ge(exped, 2 * i + t + 1)
                    nc.vector.tensor_reduce(rowsum[:, t, :], prob[:, t, :, :], AX, ALU.add).then_inc(soft, 1)
                for t in range(NP_):
                    dve.wait_ge(soft, b0 + 1 + t)
                    nc.vector.reciprocal(rowinv[:, t, :], rowsum[:, t, :]).then_inc(soft, 1)

            def normalise(i):
                for t in range(NP_):
                    dve.wait_ge(pv_done, 2 * i + t + 1)
                    dve.wait_ge(soft, SOFT * i + 7 + t)
                    nc.vector.tensor_tensor(oN[:, t, :].rearrange("p (h d) -> p h d", d=HD0),
                                            PS[:, 6 + t, :].rearrange("p (h d) -> p h d", d=HD0),
                                            rowinv[:, t, :].unsqueeze(2).to_broadcast([P, NH0, HD0]),
                                            ALU.mult).then_inc(o_normed, 1)

            def split_out(i):
                for t in range(NP_):
                    dve.wait_ge(ot_hi, 2 * i + t + 1)
                    nc.vector.tensor_tensor(oT[1][:, :, t * P:(t + 1) * P],
                                            PS[:, 4 + t, :].rearrange("p (e q) -> p e q", e=KD),
                                            oT[0][:, :, t * P:(t + 1) * P].bitcast(F32), ALU.subtract).then_inc(ot_lo, 1)

            def turn(i, first=False, last=False, split=True):
                dst = [wtabA[a][:, bass.ds(HALF * i, HALF)] for a in range(2)]
                if not first:
                    normalise(i - 1)
                n = lut_part(i, dst, 0, 4, 0)
                scale_and_mask(i)
                if not first:
                    split_out(i - 1)
                subtract_max(i)
                n = lut_part(i, dst, 4, 6, n)
                sums(i)
                n = lut_part(i, dst, 6, 16, n)
                if split:
                    split_x(i + 2)

            turn(0, first=True)
            with dve.Fori(1, NCA - 2) as i:
                turn(i)
            turn(NCA - 2, split=False)
            turn(NCA - 1, split=False)
            normalise(NCA - 1)
            split_out(NCA - 1)

            for c in range(NCF):
                dve.wait_ge(y_hi, c + 1)
                nc.vector.tensor_tensor(ys[1][:, :, c * CF:(c + 1) * CF], y_raw[:, :, c * CF:(c + 1) * CF],
                                        ys[0][:, :, c * CF:(c + 1) * CF].bitcast(F32), ALU.subtract).then_inc(y_lo, 1)
            dve.wait_ge(x1_in, 16)

            def add_down(g, f, c):
                s = group_step[g] + GROUPS[g][1] * c + f
                dve.wait_ge(d_done, s + 1)
                if g:
                    dve.wait_ge(acc_added, 4 * (NCF * g + c))
                for d in range(KD):
                    part = x1[:, d, bass.ds(c * CF, CF)]
                    nc.vector.tensor_tensor(part, PS[:, d, :], part, ALU.add).then_inc(acc_added, 1)

            def ffn_step(g, f, c, before):
                s = group_step[g] + GROUPS[g][1] * c + f
                p = f % 2
                dve.wait_ge(gu_done, s + 1)
                dve.wait_ge(silu_done, s + 1)
                repeat = f == 0 and (GROUPS[g][1] % 2 and not (isinstance(c, int) and c == 0)
                                     or g and GROUPS[g - 1][1] % 2 and isinstance(c, int) and c == 0)
                if not (isinstance(s, int) and s < 2):
                    dve.wait_ge(h_lo, s if repeat else s - 1)
                nc.vector.tensor_tensor(hf[:, p, :], sg[:, p, :], PS[:, 5 + 2 * p, :], ALU.mult).then_inc(mul_done, 1)
                dve.wait_ge(h_hi, s + 1)
                nc.vector.tensor_tensor(hs[1][:, p, :], hf[:, p, :], hs[0][:, p, :].bitcast(F32),
                                        ALU.subtract).then_inc(h_lo, 1)
                if f == 0 and before is not None:
                    add_down(*before)

            def chunk(g, c, before, first_half, dst):
                nb = GROUPS[g][1]
                parts = [(first_half, 0), (first_half, 1), (first_half + 1, 0), (first_half + 1, 1)] if dst else []
                cut = {4: [1, 2, 3, 4], 3: [2, 3, 4]}[nb]
                n, k = 0, 0
                for f in range(nb):
                    ffn_step(g, f, c, before)
                    while parts and k < cut[f]:
                        h, late = parts[k]
                        n = lut_part(h, dst[k // 2], 8 * late, 8 * late + 8, n)
                        if late:
                            n = 0
                        k += 1

            def halves(tabs, h, first):
                return [[tabs[a][:, bass.ds(HALF * (h + q - first), HALF)] for a in range(2)] for q in range(2)]

            h0 = 2 * GROUPS[1][0]
            chunk(0, 0, None, h0, halves(wtabB, h0, h0))
            with dve.Fori(1, NCF - 1) as c:
                chunk(0, c, (0, 3, c - 1), 2 * c + h0, halves(wtabB, 2 * c + h0, h0))
            chunk(0, NCF - 1, (0, 3, NCF - 2), 0, None)
            h0 = 2 * GROUPS[2][0]
            nb = GROUPS[1][1]
            ffn_step(1, 0, 0, (0, 3, NCF - 1))
            n = lut_part(h0, halves(wtabA, h0, h0)[0], 0, 8, 0)
            n = lut_part(h0, halves(wtabA, h0, h0)[0], 8, 16, n)
            ffn_step(1, 1, 0, None)
            n = lut_part(h0 + 1, halves(wtabA, h0, h0)[1], 0, 8, 0)
            ffn_step(1, 2, 0, None)
            n = lut_part(h0 + 1, halves(wtabA, h0, h0)[1], 8, 16, n)
            with dve.Fori(1, NCF) as c:
                chunk(1, c, (1, 2, c - 1), 2 * c + h0, halves(wtabA, 2 * c + h0, h0))
            dve.wait_ge(w1_hi, 3)
            for n, (part, raw) in enumerate(((w1_sb, w1_raw), (a_sb, a_raw), (b_sb, b_raw))):
                whole = tuple([slice(None)] * (3 if n < 2 else 2))
                nc.vector.tensor_tensor(part[1][whole], raw[whole], part[0][whole].bitcast(F32), ALU.subtract).then_inc(w1_lo, 1)
            chunk(2, 0, (1, 2, NCF - 1), 0, None)
            with dve.Fori(1, NCF) as c:
                chunk(2, c, (2, 3, c - 1), 0, None)
            add_down(2, 3, NCF - 1)

            dve.wait_ge(small_in, 16 * 9)
            nc.vector.tensor_copy(tok_adf[:, :], tok_ad[:, :]).then_inc(admask_made, 1)
            dve.wait_ge(admask_made, 1)
            nc.vector.tensor_scalar(admask[:, :], tok_adf[:, :], row_ad[:, 0:1], scal_sb[:, 0:1],
                                    ALU.is_equal, ALU.mult).then_inc(admask_made, 1)
            dve.wait_ge(admask_made, 2)

            def split_x1(c, u, first=False):
                dve.wait_ge(x1_hi, c + u + 1)
                nc.vector.tensor_tensor(x1s[1][:, u, :, :], x1[:, :, bass.ds((c + u) * CF, CF)],
                                        x1s[0][:, u, :, :].bitcast(F32), ALU.subtract).then_inc(x1_lo, 1)

            def linear_tiles(c, u, first=False):
                cu = c + u
                dve.wait_ge(xa_done, cu + 1)
                if u or not first:
                    dve.wait_ge(xa_lo, cu)
                    dve.wait_ge(xa_hi, cu)
                per = CF // S
                nc.vector.tensor_tensor(xa[:, :].rearrange("p (b t) -> p b t", t=S),
                                        PS[:, 4, :].rearrange("p (b t) -> p b t", t=S),
                                        admask[:, bass.ds(cu * per, per)].unsqueeze(2).to_broadcast([P, per, S]),
                                        ALU.mult).then_inc(xa_masked, 1)
                dve.wait_ge(xa_hi, cu + 1)
                dve.wait_ge(xa_masked, cu + 1)
                nc.vector.tensor_tensor(xas[1][:, :], xa[:, :], xas[0][:, :].bitcast(F32), ALU.subtract).then_inc(xa_lo, 1)
                for t in range(NT):
                    m = NT * cu + t
                    dve.wait_ge(h_copied, m + 1)
                    if not (first and u == 0 and t == 0):
                        dve.wait_ge(scored, m)
                    nc.vector.tensor_tensor_reduce(prod[:, :], h_tile[:, t % 2, :], router_sb[:, :], 1.0, 0.0,
                                                   ALU.mult, ALU.add, score[:, bass.ds(m, 1)]).then_inc(scored, 1)
                    dve.wait_ge(xn_done, m + 1)
                    if not (first and NT * u + t < 2):
                        dve.wait_ge(out_stored[t % 2], 16 * (NT // 2 * cu + t // 2))
                    nc.vector.tensor_tensor(out_tile[:, t % 2, :], h_tile[:, t % 2, :], PS[:, 2 + t % 2, :],
                                            ALU.add).then_inc(out_added, 1)

            split_x1(0, 0, first=True)
            split_x1(0, 1, first=True)
            linear_tiles(0, 0, first=True)
            linear_tiles(0, 1, first=True)
            with dve.Fori(1, NCF // 2) as pair:
                c = 2 * pair
                for u in range(2):
                    split_x1(c, u)
                for u in range(2):
                    linear_tiles(c, u)

            tops = [0]

            def step(ins):
                ins.then_inc(top, 1)
                tops[0] += 1
                dve.wait_ge(top, tops[0])

            R16 = slice(0, NPAIR)
            dve.wait_ge(top_pe, 1)
            step(nc.vector.tensor_copy(scoreT[R16, :], PS[R16, 5, 0:P]))
            for j in range(2):
                half = slice(j * S, (j + 1) * S)
                step(nc.vector.max(best[R16, j, :], scoreT[R16, half]))
                step(nc.vector.match_replace(replaced[R16, half], best[R16, j, :], scoreT[R16, half], -3.0e38))
            step(nc.vector.tensor_tensor(picked[R16, :], replaced[R16, :], scoreT[R16, :], ALU.not_equal))
            dve.wait_ge(zeroed, 3)
            for j in range(2):
                half = slice(j * S, (j + 1) * S)
                step(nc.vector.tensor_tensor_scan(rank[R16, half], onesr[R16, :], picked[R16, half], 0.0,
                                                  ALU.mult, ALU.add))
            step(nc.vector.tensor_tensor(rank[R16, :], rank[R16, :], picked[R16, :], ALU.mult))
            assert tops[0] == 9
            dve.wait_ge(top_pe, 2)
            step(nc.vector.tensor_copy(rankT[:, :], PS[:, 6, 0:NPAIR]))
            step(nc.vector.tensor_tensor(pick[:, :, :], rankT[:, :].unsqueeze(2).to_broadcast([P, NPAIR, 2 * TOPK]),
                                         slots_sb[:, :].unsqueeze(1).to_broadcast([P, NPAIR, 2 * TOPK]), ALU.is_equal))
            assert tops[0] == 11
            dve.wait_ge(top_pe, 3)
            step(nc.vector.tensor_copy(tables[:, :, :].rearrange("p a b -> p (a b)"), PS[:, 7, 0:NSB * TABW]))
            nc.vector.tensor_tensor(rowidx[:, :], tables[:, :, TABW - 1], pair_sb[:, :], ALU.add).then_inc(rows_ready, 1)

            def inverse_rms(src, n):
                seen = [9 * n]

                def step(ins):
                    ins.then_inc(norm, 1)
                    seen[0] += 1
                    dve.wait_ge(norm, seen[0])

                for sb in range(NSB):
                    step(nc.vector.tensor_tensor_reduce(scratch[:, :], src[:, sb, :], src[:, sb, :], 1.0, 0.0,
                                                        ALU.mult, ALU.add, stat[:, 7, sb:sb + 1]))
                step(nc.vector.tensor_scalar(stat[:, 0, :], stat[:, 7, :], 1.0 / D, EPS, ALU.mult, ALU.add))
                dve.wait_ge(root, n + 1)
                step(nc.vector.reciprocal(stat[:, 2, :], stat[:, 1, :]))
                step(nc.vector.tensor_tensor(stat[:, 3, :], stat[:, 2, :], stat[:, 2, :], ALU.mult))
                step(nc.vector.tensor_tensor(stat[:, 3, :], stat[:, 3, :], stat[:, 0, :], ALU.mult))
                step(nc.vector.tensor_scalar(stat[:, 3, :], stat[:, 3, :], -0.5, 1.5, ALU.mult, ALU.add))
                step(nc.vector.tensor_tensor(stat[:, 4, :], stat[:, 2, :], stat[:, 3, :], ALU.mult))

            dve.wait_ge(sel_in, 32)
            inverse_rms(hsel, 0)
            for sb in range(NSB):
                ins = nc.vector.tensor_scalar(xres[:, sb, :], hsel[:, sb, :], stat[:, 4, sb:sb + 1], None, ALU.mult)
                ins.then_inc(norm, 1) if sb == 0 else ins.then_inc(normed, 1)
            for sb in range(NSB):
                dve.wait_ge(norm, 9)
                ins = nc.vector.tensor_tensor_reduce(scratch[:, :], hsel[:, sb, :], router_sb[:, :], 1.0, 0.0,
                                                     ALU.mult, ALU.add, stat[:, 5, sb:sb + 1])
                ins.then_inc(gate_seq, 1)
                dve.wait_ge(gate_seq, sb + 1)

            dve.wait_ge(bias_in, 16)
            seen = 0
            for m in range(16):
                nt, sb = m // 2, m % 2
                dve.wait_ge(qkv_done, m + 1)
                if m < 12:
                    if m >= 2:
                        dve.wait_ge(rt_done, m - 1)
                        dve.wait_ge(rope_seq, seen)
                    nc.vector.tensor_tensor(biased[:, 0, :], PS[:, m % 4, :], bias_sb[:, nt * 512:(nt + 1) * 512],
                                            ALU.add).then_inc(qkv_read, 1)
                    dve.wait_ge(qkv_read, m + 1)
                    x4 = biased[:, 0, :].rearrange("p (h a w) -> p h a w", h=4, a=2)
                    cos = tables[:, sb, 0:ROPE_W].unsqueeze(1).to_broadcast([P, 8, ROPE_W])
                    nc.vector.tensor_tensor(times_cos[:, :].rearrange("p (a w) -> p a w", a=8),
                                            biased[:, 0, :].rearrange("p (a w) -> p a w", a=8), cos,
                                            ALU.mult).then_inc(rope_seq, 1)
                    y4 = times_sin[:, :].rearrange("p (h a w) -> p h a w", h=4, a=2)
                    for a in range(2):
                        sin = tables[:, sb, (1 + a) * ROPE_W:(2 + a) * ROPE_W].unsqueeze(1).to_broadcast([P, 4, ROPE_W])
                        nc.vector.tensor_tensor(y4[:, :, a, :], x4[:, :, 1 - a, :], sin, ALU.mult).then_inc(rope_seq, 1)
                    seen += 3
                    dve.wait_ge(rope_seq, seen)
                    nc.vector.tensor_tensor(turned_of(m), times_cos[:, :], times_sin[:, :], ALU.add).then_inc(roped, 1)
                    dve.wait_ge(roped, m + 1)
                else:
                    nc.vector.tensor_tensor(v2[:, sb, (nt - 6) * 512:(nt - 5) * 512], PS[:, m % 4, :],
                                            bias_sb[:, nt * 512:(nt + 1) * 512], ALU.add).then_inc(qkv_read, 1)

            def mask_and_max(g):
                dve.wait_ge(s2_done, g + 1)
                if g == 0:
                    dve.wait_ge(qkv_done, 16)
                if g >= 2:
                    dve.wait_ge(p2t_done, HG * (g - 1))
                nc.vector.scalar_tensor_tensor(prob2[:, g % 2, :, :], PS[:, 0:HG, 0:3 * P], float(HD) ** -0.5,
                                               mask2[:, :].unsqueeze(1).to_broadcast([P, HG, 3 * P]),
                                               ALU.mult, ALU.add).then_inc(s2_masked, 1)
                dve.wait_ge(s2_masked, g + 1)
                for sb in range(NSB):
                    nc.vector.tensor_reduce(st2[:, g % 2, :, sb], prob2[:, g % 2, :, sb * P:(2 * sb + 1) * P], AX, ALU.max,
                                            negate=True).then_inc(s2_max, 1)

            def divide(g):
                dve.wait_ge(s2_exp, 2 * HG * (g + 1))
                nc.vector.reciprocal(st2[:, 2 + g % 2, :, :], st2[:, 2 + g % 2, :, :]).then_inc(s2_inv, 1)
                dve.wait_ge(s2_inv, g + 1)
                for sb in range(NSB):
                    part = prob2[:, g % 2, :, sb * P:(2 * sb + 1) * P]
                    nc.vector.tensor_tensor(part, part, st2[:, 2 + g % 2, :, sb:sb + 1].to_broadcast([P, HG, (sb + 1) * P]),
                                            ALU.mult).then_inc(s2_norm, 1)

            mask_and_max(0)
            for g in range(NHQ // HG):
                if g + 1 < NHQ // HG:
                    mask_and_max(g + 1)
                divide(g)
            dve.wait_ge(gate_exp, 1)
            nc.vector.tensor_scalar(stat[:, 6, :], stat[:, 6, :], 1.0, None, ALU.add).then_inc(gate_seq, 1)
            dve.wait_ge(gate_seq, 3)
            nc.vector.reciprocal(stat[:, 5, :], stat[:, 6, :]).then_inc(gate_seq, 1)
            dve.wait_ge(gate_seq, 4)

            for sb in range(NSB):
                dve.wait_ge(wo2_done, sb + 1)
                dve.wait_ge(ht_done, 1)
                nc.vector.tensor_tensor(xres[:, sb, :], PS[:, sb, :], hsel[:, sb, :], ALU.add).then_inc(gate_seq, 1)
            dve.wait_ge(gate_seq, 6)
            inverse_rms(xres, 1)
            for sb in range(NSB):
                ins = nc.vector.tensor_scalar(hsel_normed[:, sb, :], xres[:, sb, :], stat[:, 4, sb:sb + 1], None, ALU.mult)
                ins.then_inc(norm, 1) if sb == 0 else ins.then_inc(normed, 1)
            for sb in range(NSB):
                nc.vector.tensor_tensor(hsel[:, sb, :], xres[:, sb, :], hsel[:, sb, :], ALU.subtract).then_inc(gate_seq, 1)

            for f in range(NF1):
                dve.wait_ge(silu2, f + 1)
                nc.vector.tensor_tensor(mT[:, f, :], sg1[:, f % 2, :], PS[:, 4 + f % 2, SEL:2 * SEL], ALU.mult).then_inc(mul2, 1)

            dve.wait_ge(outsel_in, 32)
            dve.wait_ge(gate_seq, 8)
            dve.wait_ge(d2_done, NF1)
            for sb in range(NSB):
                nc.vector.tensor_tensor(hsel[:, sb, :], PS[:, 2 + sb, :], hsel[:, sb, :], ALU.add).then_inc(gate_seq, 1)
            for sb in range(NSB):
                dve.wait_ge(gate_seq, 9 + sb)
                nc.vector.scalar_tensor_tensor(fin[:, sb, :], hsel[:, sb, :], stat[:, 5, sb:sb + 1], outsel[:, sb, :],
                                               ALU.mult, ALU.add).then_inc(fin_ready, 1)


def kernel(**inputs):
    import numpy as np
    import concourse.bacc as bacc
    from concourse.bass_utils import run_bass_kernel_spmd

    nc = bacc.Bacc("TRN2", target_bir_lowering=False, num_devices=1, dynamic_dma_scratch_size=4096)
    con = np.ascontiguousarray

    def features_first(w):
        return con(np.asarray(w).reshape(w.shape[0], -1, P).transpose(2, 1, 0))

    arrays = {}
    arrays["xT"] = features_first(np.asarray(inputs["x"]).reshape(TOK, D))
    arrays["w0"] = np.stack([features_first(inputs[f"L0_cond_{n}"]) for n in ("Wq", "Wk", "Wv", "Wo")])
    pad = NBLK * P - INTER

    def in_blocks(w):
        w = np.pad(np.asarray(w), ((0, pad), (0, 0)))
        return w.reshape(NBLK, P, KD, P).transpose(0, 3, 2, 1).reshape(NBLK, P, D)

    gate, up = (in_blocks(inputs[f"L0_ffn_{n}_idx"]) for n in ("gate", "up"))
    down = np.pad(np.asarray(inputs["L0_ffn_down_idx"]).T, ((0, pad), (0, 0))).reshape(NBLK, P, D)
    both = np.concatenate([gate, up, down], axis=2).reshape(NBLK, P, 2, HALF)
    arrays["idx"] = con(both.transpose(0, 2, 1, 3).reshape(2 * NBLK, P, HALF))
    arrays["lut"] = con(np.broadcast_to(np.asarray(inputs["L0_ffn_lut"]), (P, LUTN)))
    arrays["cond"] = con(np.repeat(np.asarray(inputs["cond_1"]).reshape(B // 2, 2).T, S, axis=0))
    t = np.arange(S)
    below = np.where(t[None, :] <= t[:, None], 0.0, -3.0e38).astype(np.float32)
    arrays["causal"] = con(np.tile(below, (2, 4)))
    arrays["w1"] = features_first(inputs["L1_cond_W"])
    arrays["aT"] = features_first(np.asarray(inputs["L1_cond_A"]).reshape(NA * RANK, D))
    arrays["bmT"] = con(np.asarray(inputs["L1_cond_Bm"]).transpose(0, 2, 1).reshape(NA * RANK, D))
    arrays["tokens_adapter"] = con(np.broadcast_to(np.asarray(inputs["itok_B_0_6"]), (P, B)))
    arrays["adapter_of_row"] = np.repeat(np.arange(NA, dtype=np.float32), RANK)[:, None]
    arrays["scalings"] = con(np.repeat(np.asarray(inputs["L1_cond_scalings"]), RANK)[:, None])
    arrays["router"] = con(np.broadcast_to(np.asarray(inputs["L1_ffn_w_router"]), (P, D)))
    n = np.arange(1, TOPK + 1, dtype=np.float32)
    none = -np.ones(TOPK, np.float32)
    arrays["slots"] = np.repeat(np.stack([np.concatenate([n, none]), np.concatenate([none, n])]), S, axis=0)
    inv = np.float32(1.0) / np.float32(10000.0) ** (np.arange(0, HD, 2, dtype=np.float32) / np.float32(HD))
    angle = np.tile(t.astype(np.float32), 2)[:, None] * inv
    arrays["rope"] = np.concatenate([np.cos(angle), -np.sin(angle), np.sin(angle),
                                     np.arange(P, dtype=np.float32)[:, None]], axis=1).astype(np.float32)
    t = np.arange(P)
    below = np.where(t[None, :] <= t[:, None], 0.0, -3.0e38).astype(np.float32)
    arrays["causal2"] = con(np.concatenate([below, np.zeros((P, P), np.float32), below], axis=1))
    sel = np.arange(SEL).reshape(NSB, P).T
    arrays["pair_base"] = con((sel // (2 * TOPK) * P).astype(np.float32))
    arrays["ln"] = con(np.stack([np.asarray(inputs[f"L1_ffn_ln{n}_w"]).reshape(KD, P).T for n in (1, 2)], axis=1))

    def rows_first(w):
        return con(np.asarray(w).reshape(-1, P, w.shape[1]).transpose(1, 0, 2))

    for name, key in (("wq", "wq"), ("wk", "wk"), ("wv", "wv"), ("wo", "wo"), ("wgate", "w_gate"), ("wup", "w_up"),
                      ("wdown", "w_down")):
        arrays[name] = rows_first(inputs[f"L1_ffn_{key}"])
    arrays["bias"] = con(np.broadcast_to(np.concatenate([np.asarray(inputs[f"L1_ffn_{n}"]) for n in ("bq", "bk", "bv")]),
                                         (P, (NHQ + 2 * NHKV) * HD)))
    aps = {n: nc.dram_tensor(f"in_{n}", a.shape, mybir.dt.from_np(a.dtype), kind="ExternalInput").ap()
           for n, a in arrays.items()}
    y_dram = nc.dram_tensor("y_dram", (P, KD, TOK), F32, kind="Internal").ap()
    h_dram = nc.dram_tensor("h_dram", (TOK, D), F32, kind="Internal").ap()
    out = nc.dram_tensor("out_rows", (TOK, D), F32, kind="ExternalOutput").ap()
    adaln_ffn_kernel(nc, y_dram=y_dram, h_dram=h_dram, out=out, **aps)
    r = run_bass_kernel_spmd(nc, [{f"in_{n}": a for n, a in arrays.items()}], core_ids=[0])
    return r.results[0]["out_rows"].reshape(B, S, D)
```

```python
import concourse.bass as bass
from concourse import mybir
from contextlib import ExitStack

F32 = mybir.dt.float32
F32R = mybir.dt.float32r
BF16 = mybir.dt.bfloat16
I32 = mybir.dt.int32
ALU = mybir.AluOpType
ACT = mybir.ActivationFunctionType
AX = mybir.AxisListType.X

P = 128
B, S, D = 32, 64, 512
KD = D // P
TOK = B * S
INTER = 1376
NBLK = -(-INTER // P)
LAST = INTER - (NBLK - 1) * P
NH0, HD0 = 16, 32
CA = 256
NCA = TOK // CA
BC = CA // S
NP_ = BC // 2
CF = 512
NCF = TOK // CF
BLKW = 3 * D
HALF = BLKW // 2
LUTN = 16
GROUPS = [(0, 4), (4, 3), (7, 2), (9, 2)]
PASSES = [(0, 0), (0, 1), (1, 0)]


NPAIR = B // 2
NA, RANK = 8, 16
TOPK = 8
SEL = B * TOPK
NSB = SEL // P
NHQ, NHKV, HD = 16, 8, 128
HG = 2
I1 = 2048
NF1 = I1 // P
EPS = 1e-6
ROPE_W = HD // 2
TABW = 3 * ROPE_W + 1


def adaln_ffn_kernel(nc, xT, w0, idx, lut, cond, causal, w1, aT, bmT, tokens_adapter, adapter_of_row, scalings,
                     router, slots, rope, causal2, pair_base, ln, wq, wk, wv, bias, wo, wgate, wup, wdown,
                     y_dram, h_dram, out):
    ctx = ExitStack()
    with ctx:
        base = [-(-nc.sbuf_base // 64) * 64]
        start = base[0]

        def at(name, offset, shape, dt):
            return nc.alloc_sbuf_tensor_at(name, [P] + shape, dt, offset=start + offset)

        def sem(name):
            return ctx.enter_context(nc.semaphore(name))

        ident = at("ident", 0, [P], F32)
        mask = at("mask", 512, [4 * S], F32)
        beta = at("beta", 1536, [B // 2], F32)
        lut_sb = at("lut_sb", 1600, [LUTN], F32)
        rowmax = at("rowmax", 1664, [NP_, NH0], F32)
        rowsum = at("rowsum", 1792, [NP_, NH0], F32)
        rowinv = at("rowinv", 1920, [NP_, NH0], F32)
        K1 = 2048
        SLOT = BLKW * 4
        wtabA = [at(f"wtabA{i}", K1 + 4 * SLOT * i, [4 * BLKW], F32R) for i in range(2)]
        wsumA = at("wsumA", K1 + 4 * SLOT, [4 * BLKW], F32)
        K2 = K1 + 8 * SLOT
        idx_raw = at("idx_raw", K2, [HALF], I32)
        idx_bf = at("idx_bf", K2 + 4 * HALF, [HALF], BF16)
        onehot = at("onehot", K2 + 6 * HALF, [3, HALF], BF16)
        K3 = K2 + 16 * HALF
        w_raw = [at(f"w_raw{n}", K1 + 4 * SLOT * (n // 2) + SLOT + 8192 * (n % 2), [KD, D], F32) for n in range(4)]
        o = K3
        w_sb = []
        for n in range(3):
            w_sb.append([at(f"w_sb{n}_{i}", o + 8192 * i, [KD, D], F32R) for i in range(2)])
            o += 16384
        xr = at("xr", o, [KD, CA], F32); o += 4096
        xs = [at(f"xs{i}", o + 4096 * i, [KD, CA], F32R) for i in range(2)]; o += 8192
        qT = at("qT", o, [KD, CA], F32); o += 4096
        w_sb.append([at(f"w_sb3_{i}", o + 8192 * i, [KD, D], F32R) for i in range(2)]); o += 16384
        yc = at("yc", o, [KD, CA], F32); o += 4096
        kbd = at("kbd", o, [KD, BC, 4 * S], F32); o += 16384
        vbd = at("vbd", o, [BC, NH0 // 2, 2 * HD0], F32); o += 8192
        prob = at("prob", o, [NP_, NH0, S], F32); o += 8192
        probT = at("probT", o, [NP_, NH0 // 2, P], F32); o += 8192
        oN = at("oN", o, [NP_, D], F32); o += 4096
        oT = [at(f"oT{i}", o + 4096 * i, [KD, CA], F32R) for i in range(2)]; o += 8192
        o = K3
        y_raw = at("y_raw", o, [KD, TOK], F32)
        ys = [at("ys1", o, [KD, TOK], F32R)]; o += 32768
        ys.insert(0, at("ys0", o, [KD, TOK], F32R)); o += 32768
        x1 = at("x1", o, [KD, TOK], F32); o += 32768
        wtabB = [at(f"wtabB{i}", o + 2 * SLOT * i, [2 * BLKW], F32R) for i in range(2)]
        wsumB = at("wsumB", o + 2 * SLOT, [2 * BLKW], F32); o += 4 * SLOT
        sg = at("sg", o, [2, CF], F32); o += 4096
        hf = at("hf", o, [2, CF], F32); o += 4096
        hs = [at(f"hs{i}", o + 4096 * i, [2, CF], F32R) for i in range(2)]; o += 8192
        wtabC = [at(f"wtabC{i}", o + SLOT * i, [BLKW], F32R) for i in range(2)]
        wsumC = at("wsumC", o + SLOT, [BLKW], F32); o += 2 * SLOT
        small = o
        o += 8192
        assert start + o <= nc.sbuf_usable_end, (start + o, nc.sbuf_usable_end)

        def little(name, shape, dt=F32):
            nonlocal small
            n = 1
            for x in shape:
                n *= x
            t = at(name, small, shape, dt)
            small += -(-4 * n // 32) * 32
            return t

        router_sb = little("router_sb", [D])
        slots_sb = little("slots_sb", [2 * TOPK])
        rope_sb = little("rope_sb", [TABW])
        mask2 = little("mask2", [3 * P])
        pair_sb = little("pair_sb", [NSB])
        ln_sb = little("ln_sb", [2, KD])
        tok_ad = little("tok_ad", [B], I32)
        tok_adf = little("tok_adf", [B])
        row_ad = little("row_ad", [1])
        scal_sb = little("scal_sb", [1])
        admask = little("admask", [B])
        score = little("score", [NPAIR])
        scoreT = little("scoreT", [P])
        replaced = little("replaced", [P])
        best = little("best", [2, TOPK])
        picked = little("picked", [P])
        rank = little("rank", [P])
        onesr = little("onesr", [S])
        rankT = little("rankT", [NPAIR])
        rowidx = little("rowidx", [NSB], I32)
        stat = little("stat", [8, NSB])
        assert small <= o

        AW, AI, AY, AX1, AB, AS = K1, K2, K3, K3 + 65536, K3 + 98304, K3 + 98304 + 6 * SLOT
        AC, AT = AB + 4 * SLOT + 16384, AB + 4 * SLOT
        w1_raw = at("w1_raw", AB, [KD, D], F32)
        w1_sb = [at(f"w1_sb{i}", AB + 8192 + 8192 * i, [KD, D], F32R) for i in range(2)]
        a_raw = at("a_raw", AC, [KD, P], F32)
        a_sb = [at(f"a_sb{i}", AC + 2048 + 2048 * i, [KD, P], F32R) for i in range(2)]
        b_raw = at("b_raw", AC + 6144, [D], F32)
        b_sb = [at(f"b_sb{i}", AC + 8192 + 2048 * i, [D], F32R) for i in range(2)]
        x1s = [at(f"x1s{i}", AY + 16384 + 16384 * i, [2, KD, CF], F32R) for i in range(2)]
        h_tile = at("h_tile", AT, [2, D], F32)
        out_tile = at("out_tile", AT + 4096, [2, D], F32)
        xa = at("xa", AT + 8192, [CF], F32)
        xas = [at(f"xas{i}", AT + 10240 + 2048 * i, [CF], F32R) for i in range(2)]
        prod = at("prod", AT + 14336, [D], F32)
        wq_sb = at("wq_sb", AW, [KD, NHQ * HD], F32)
        wk_sb = at("wk_sb", AW + 32768, [KD, NHKV * HD], F32)
        wv_sb = at("wv_sb", AY + 49152, [KD, NHKV * HD], F32)
        wo_sb = at("wo_sb", AX1, [NHQ, D], F32)
        wd_sb = at("wd_sb", AB, [NF1, D], F32)
        bias_sb = at("bias_sb", AS, [(NHQ + 2 * NHKV) * HD], F32)
        qT2 = at("qT2", AY, [NHQ, SEL], F32)
        kT2 = at("kT2", AY + 16384, [NHKV, SEL], F32)
        v2 = at("v2", AY + 24576, [NSB, NHKV * HD], F32)
        hsel = at("hsel", AY + 32768, [NSB, D], F32)
        outsel = at("outsel", AY + 36864, [NSB, D], F32)
        hT = at("hT", AY + 40960, [KD, SEL], F32)
        xres = at("xres", AY + 45056, [NSB, D], F32)
        biased = at("biased", AI, [1, D], F32)
        times_cos = at("times_cos", AI + 4096, [D], F32)
        times_sin = at("times_sin", AI + 6144, [D], F32)
        turned = at("turned", AI + 8192, [D], F32)
        tables = at("tables", AI + 10240, [NSB, TABW], F32)
        pick = at("pick", AB + 32768, [NPAIR, 2 * TOPK], F32)
        scratch = at("scratch", AB + 33792, [D], F32)
        prob2 = at("prob2", AW, [4, HG, 3 * P], F32)
        prob2T = at("prob2T", AW + 12288, [4, 3 * P], F32)
        oT2 = at("oT2", AW + 24576, [NHQ, SEL], F32)
        negmax2 = at("negmax2", AW + 40960, [4, HG, NSB], F32)
        rowsum2 = at("rowsum2", AW + 41088, [4, HG, NSB], F32)
        h2T = at("h2T", AW + 45056, [KD, SEL], F32)
        wg_sb = [at("wg_sb0", AY + 49152, [KD // 2, I1], F32), at("wg_sb1", AS, [KD // 2, I1], F32)]
        wu_sb = at("wu_sb", AY, [KD, I1], F32)
        mT = at("mT", AW, [NF1, SEL], F32)
        sg1 = at("sg1", AW + 16384, [2, SEL], F32)
        fin = at("fin", AI, [NSB, D], F32)

        turned_b = at("turned_b", AI + 2048, [D], F32)
        hsel_normed = at("hsel_normed", AI, [NSB, D], F32)

        def turned_of(m):
            return turned[:, :] if m % 2 else turned_b[:, :]

        PS = ctx.enter_context(nc.psum_tensor("PS", [P, 8, 512], F32))

        def wtab(blk, part):
            if blk == GROUPS[1][0]:
                return wtabC[part][:, :]
            if blk < GROUPS[2][0] and blk > GROUPS[1][0]:
                s = blk - GROUPS[1][0] - 1
                return wtabB[part][:, s * BLKW:(s + 1) * BLKW]
            s = blk if blk < GROUPS[1][0] else blk - GROUPS[2][0]
            return wtabA[part][:, s * BLKW:(s + 1) * BLKW]

        def half_block(g, h):
            if g == 1 and h // 2 == GROUPS[1][0]:
                hi, lo, whole = wtabC + [wsumC]
                first = GROUPS[1][0]
            elif g == 1:
                hi, lo, whole = wtabB + [wsumB]
                first = GROUPS[1][0] + 1
            else:
                hi, lo, whole = wtabA + [wsumA]
                first = GROUPS[2][0] if g else 0
            return [t[:, bass.ds(HALF * (h - 2 * first), HALF)] for t in (hi, lo, whole)]

        consts_in = sem("consts_in")
        lut_in = sem("lut_in")
        ident_made = sem("ident_made")
        zeroed = sem("zeroed")
        beta_ready = sem("beta_ready")
        w_in = [sem(f"w_in{n}") for n in range(4)]
        w_hi = sem("w_hi")
        w_lo = sem("w_lo")
        x_in = sem("x_in")
        x_hi = sem("x_hi")
        x_lo = sem("x_lo")
        q_done = sem("q_done")
        k_done = sem("k_done")
        v_done = sem("v_done")
        q_copied = sem("q_copied")
        k_copied = sem("k_copied")
        v_copied = sem("v_copied")
        s_done = sem("s_done")
        shifted = sem("shifted")
        exped = sem("exped")
        pt_done = sem("pt_done")
        pt_copied = sem("pt_copied")
        pv_done = sem("pv_done")
        o_normed = sem("o_normed")
        ot_done = sem("ot_done")
        ot_hi = sem("ot_hi")
        ot_lo = sem("ot_lo")
        wo_done = sem("wo_done")
        y_copied = sem("y_copied")
        y_stored = sem("y_stored")
        soft = sem("soft")
        idx_in = sem("idx_in")
        idx_conv = sem("idx_conv")
        lut_seq = sem("lut_seq")
        tab_hi = sem("tab_hi")
        tab_ready = sem("tab_ready")
        y_in = [sem(f"y_in{c}") for c in range(NCF)]
        x1_in = sem("x1_in")
        y_hi = sem("y_hi")
        y_lo = sem("y_lo")
        gu_done = sem("gu_done")
        silu_done = sem("silu_done")
        mul_done = sem("mul_done")
        h_hi = sem("h_hi")
        h_lo = sem("h_lo")
        d_done = sem("d_done")
        acc_added = sem("acc_added")
        small_in = sem("small_in")
        w1_in = sem("w1_in")
        w1_hi = sem("w1_hi")
        w1_lo = sem("w1_lo")
        admask_made = sem("admask_made")
        x1_hi = sem("x1_hi")
        x1_lo = sem("x1_lo")
        xa_done = sem("xa_done")
        xa_masked = sem("xa_masked")
        xa_hi = sem("xa_hi")
        xa_lo = sem("xa_lo")
        h_done = sem("h_done")
        xn_done = sem("xn_done")
        h_copied = sem("h_copied")
        scored = sem("scored")
        out_added = sem("out_added")
        h_stored = [sem(f"h_stored{i}") for i in range(2)]
        out_stored = [sem(f"out_stored{i}") for i in range(2)]
        top = sem("top")
        top_pe = sem("top_pe")
        rows_ready = sem("rows_ready")
        sel_in = sem("sel_in")
        outsel_in = sem("outsel_in")
        qkv_in = sem("qkv_in")
        wo_in = sem("wo_in")
        wd_in = sem("wd_in")
        bias_in = sem("bias_in")
        wg_in = sem("wg_in")
        wu_in = sem("wu_in")
        norm = sem("norm")
        root = sem("root")
        normed = sem("normed")
        ht_done = sem("ht_done")
        ht_copied = sem("ht_copied")
        qkv_done = sem("qkv_done")
        qkv_read = sem("qkv_read")
        rope_seq = sem("rope_seq")
        roped = sem("roped")
        rt_done = sem("rt_done")
        rt_copied = sem("rt_copied")
        s2_done = sem("s2_done")
        s2_masked = sem("s2_masked")
        s2_max = sem("s2_max")
        s2_exp = sem("s2_exp")
        s2_inv = sem("s2_inv")
        s2_norm = sem("s2_norm")
        p2t_done = sem("p2t_done")
        p2t_copied = sem("p2t_copied")
        pv2_done = sem("pv2_done")
        o2_copied = sem("o2_copied")
        wo2_done = sem("wo2_done")
        g2_done = sem("g2_done")
        silu2 = sem("silu2")
        mul2 = sem("mul2")
        d2_done = sem("d2_done")
        gate_seq = sem("gate_seq")
        gate_exp = sem("gate_exp")
        fin_ready = sem("fin_ready")
        scattered = sem("scattered")

        block = ctx.enter_context(nc.Block())

        NT = CF // P
        group_step = [sum(n for _, n in GROUPS[:g]) * NCF for g in range(len(GROUPS) + 1)]

        LUT_OPS = 2 * LUTN - 1

        first_parts = []
        for h in range(NCA + 1, 2 * GROUPS[2][0]):
            cuts = [0, 4, 8, 12, 16] if h == NCA + 1 else [0, 6, 11, 16]
            first_parts += [(h, a, b) for a, b in zip(cuts, cuts[1:])]
        assert len(first_parts) == GROUPS[0][1] * NCF
        ends_at = {n: (1, h) for n, (h, _, b) in enumerate(first_parts) if b == LUTN}
        ends_at[-1] = (1, NCA)
        last_before = [None, ends_at[GROUPS[0][1] * NCF - 1]] + \
            [(g, 2 * GROUPS[g][0] + NCF - 1) for g in range(2, len(GROUPS))]
        last_half = last_before[-1][1]

        @block.sync
        def _(sp):
            sp.dma_start(lut_sb[:, :], lut).then_inc(lut_in, 16)
            sp.dma_start(idx_raw[:, :], idx[0]).then_inc(idx_in, 16)
            for n in (1, 0, 2, 3):
                sp.dma_start(w_raw[n][:, :, :], w0[n]).then_inc(w_in[n], 16)
                if n == 1:
                    sp.dma_start(xr[:, :, :], xT[:, :, 0:CA]).then_inc(x_in, 16)
                    sp.dma_start(beta[:, :], cond).then_inc(consts_in, 16)
                    sp.dma_start(mask[:, :], causal).then_inc(consts_in, 16)
            sp.wait_ge(x_hi, 1)
            sp.wait_ge(x_lo, 1)
            sp.dma_start(xr[:, :, :], xT[:, :, CA:2 * CA]).then_inc(x_in, 16)

            def load_idx(h):
                sp.wait_ge(idx_conv, h)
                sp.dma_start(idx_raw[:, :], idx[bass.ds(h, 1)].rearrange("a p n -> (a p) n")).then_inc(idx_in, 16)

            def load_x(c):
                sp.wait_ge(x_hi, c)
                sp.wait_ge(x_lo, c)
                sp.dma_start(xr[:, :, :], xT[:, :, bass.ds(c * CA, CA)]).then_inc(x_in, 16)

            def store_y(c):
                sp.wait_ge(y_copied, 2 * c + 2)
                sp.dma_start(y_dram[:, :, bass.ds(c * CA, CA)], yc[:, :, :]).then_inc(y_stored, 16)

            load_idx(1)
            load_x(2)
            load_idx(2)
            with sp.Fori(1, NCA - 2) as i:
                load_x(i + 2)
                load_idx(i + 2)
                store_y(i - 1)
            load_idx(NCA)
            store_y(NCA - 3)
            load_idx(NCA + 1)

            def load_y(c):
                sp.wait_ge(y_stored, 16 * (c + 1) * CF // CA)
                sp.dma_start(y_raw[:, :, c * CF:(c + 1) * CF], y_dram[:, :, c * CF:(c + 1) * CF]).then_inc(y_in[c], 16)

            sp.wait_ge(s_done, NCA)
            for c in range(NCF - 1):
                load_y(c)
            store_y(NCA - 2)
            store_y(NCA - 1)
            load_y(NCF - 1)
            sp.dma_start(x1[:, :, :], xT).then_inc(x1_in, 16)
            with sp.Fori(NCA + 2, 2 * NBLK) as h:
                load_idx(h)
            for dst, src in ((router_sb, router), (slots_sb, slots), (rope_sb, rope), (mask2, causal2), (pair_sb, pair_base),
                             (tok_ad, tokens_adapter), (row_ad, adapter_of_row), (scal_sb, scalings)):
                sp.dma_start(dst[:, :], src).then_inc(small_in, 16)
            sp.dma_start(ln_sb[:, :, :], ln).then_inc(small_in, 16)
            sp.wait_ge(d_done, group_step[2])
            sp.dma_start(w1_raw[:, :, :], w1).then_inc(w1_in, 16)
            sp.dma_start(a_raw[:, :, :], aT).then_inc(w1_in, 16)
            sp.dma_start(b_raw[:, :], bmT).then_inc(w1_in, 16)
            sp.wait_ge(d_done, group_step[-1])
            sp.dma_start(wq_sb[:, :, :], wq).then_inc(qkv_in, 16)
            sp.dma_start(wk_sb[:, :, :], wk).then_inc(qkv_in, 16)
            sp.dma_start(wv_sb[:, :, :], wv).then_inc(qkv_in, 16)

            def tile_rows(dram, n):
                return dram.rearrange("(n p) d -> n p d", p=P)[bass.ds(n, 1)].rearrange("a p d -> (a p) d")

            with sp.Fori(0, NCF) as c:
                for t in range(NT):
                    n = NT * c + t
                    sp.wait_ge(h_copied, n + 1)
                    sp.dma_start(tile_rows(h_dram, n), h_tile[:, t % 2, :]).then_inc(h_stored[t % 2], 16)
                    sp.wait_ge(out_added, n + 1)
                    sp.dma_start(tile_rows(out, n), out_tile[:, t % 2, :]).then_inc(out_stored[t % 2], 16)

            sp.wait_ge(h_done, NPAIR)
            sp.wait_ge(xn_done, NPAIR)
            for i in range(2):
                sp.wait_ge(h_stored[i], 16 * NPAIR // 2)
                sp.wait_ge(out_stored[i], 16 * NPAIR // 2)
            sp.wait_ge(scored, NPAIR)
            sp.dma_start(bias_sb[:, :], bias).then_inc(bias_in, 16)
            sp.wait_ge(sel_in, 16 * NSB)
            sp.dma_start(wo_sb[:, :, :], wo).then_inc(wo_in, 16)
            sp.dma_start(wd_sb[:, :, :], wdown).then_inc(wd_in, 16)
            sp.wait_ge(qkv_done, 16)
            sp.dma_start(wg_sb[0][:, :, :], wgate[:, 0:2, :]).then_inc(wg_in, 16)
            sp.wait_ge(qkv_read, 16)
            sp.dma_start(wg_sb[1][:, :, :], wgate[:, 2:4, :]).then_inc(wg_in, 16)
            sp.wait_ge(pv2_done, NHQ)
            sp.dma_start(wu_sb[:, :, :], wup).then_inc(wu_in, 16)

        @block.gpsimd
        def _(pool):
            nc.gpsimd.memset(ident[:, :], 0.0).then_inc(ident_made, 1)
            pool.wait_ge(ident_made, 1)
            nc.gpsimd.affine_select(out=ident[:, :], in_=ident[:, :], compare_op=ALU.not_equal, fill=1.0,
                                    base=0, pattern=[[-1, P]], channel_multiplier=1).then_inc(ident_made, 1)
            nc.gpsimd.memset(kbd[:, :, :, :], 0.0).then_inc(zeroed, 1)
            nc.gpsimd.memset(vbd[:, :, :, :], 0.0).then_inc(zeroed, 1)
            nc.gpsimd.memset(onesr[:, :], 1.0).then_inc(zeroed, 1)

            pool.wait_ge(rows_ready, 1)
            for i in range(2):
                pool.wait_ge(h_stored[i], 16 * NPAIR // 2)
                pool.wait_ge(out_stored[i], 16 * NPAIR // 2)
            pool.wait_ge(h_done, NPAIR)
            pool.wait_ge(xn_done, NPAIR)
            for sb in range(NSB):
                nc.gpsimd.indirect_dma_start(out=hsel[:, sb, :], out_offset=None, in_=h_dram[:, :],
                                             in_offset=bass.IndirectOffsetOnAxis(ap=rowidx[:, sb:sb + 1], axis=0)
                                             ).then_inc(sel_in, 16)
            for sb in range(NSB):
                nc.gpsimd.indirect_dma_start(out=outsel[:, sb, :], out_offset=None, in_=out[:, :],
                                             in_offset=bass.IndirectOffsetOnAxis(ap=rowidx[:, sb:sb + 1], axis=0)
                                             ).then_inc(outsel_in, 16)
            for sb in range(NSB):
                pool.wait_ge(fin_ready, sb + 1)
                nc.gpsimd.indirect_dma_start(out=out[:, :],
                                             out_offset=bass.IndirectOffsetOnAxis(ap=rowidx[:, sb:sb + 1], axis=0),
                                             in_=fin[:, sb, :], in_offset=None).then_inc(scattered, 16)
            pool.wait_ge(scattered, 16 * NSB)

        @block.tensor
        def _(pe):
            def project(w, bank0, done):
                for e in range(KD):
                    out = PS[:, bank0 + e // 2, (e % 2) * CA:(e % 2 + 1) * CA]
                    n = 0
                    for k in range(KD):
                        for a, b in PASSES:
                            mm = nc.tensor.matmul(out, w_sb[w][a][:, k, e * P:(e + 1) * P], xs[b][:, k, :],
                                                  start=(n == 0), stop=(n == 3 * KD - 1))
                            n += 1
                    if e % 2:
                        mm.then_inc(done, 1)

            def keys(c):
                pe.wait_ge(x_hi, c + 1)
                pe.wait_ge(x_lo, c + 1)
                project(1, 6, k_done)

            def queries(c):
                pe.wait_ge(k_copied, 2 * c + 2)
                project(0, 6, q_done)

            def values(c):
                for t in range(NP_):
                    n = 0
                    for k in range(KD):
                        for a, b in PASSES:
                            mm = nc.tensor.matmul(PS[:, 4 + t, :], xs[a][:, k, t * P:(t + 1) * P], w_sb[2][b][:, k, :],
                                                  start=(n == 0), stop=(n == 3 * KD - 1))
                            n += 1
                    mm.then_inc(v_done, 1)

            def scores(c):
                pe.wait_ge(q_copied, 2 * c + 2)
                pe.wait_ge(k_copied, 2 * c + 2)
                for e in range(KD):
                    for b in range(BC):
                        j, t = b % 2, b // 2
                        mm = nc.tensor.matmul(PS[64 * j:64 * j + 64, e, t * 256:(t + 1) * 256],
                                              qT[:, e, b * S:(b + 1) * S], kbd[:, e, b, :], start=True, stop=True,
                                              skip_group_check=True)
                mm.then_inc(s_done, 1)

            def prob_transposes(c):
                for t in range(NP_):
                    pe.wait_ge(exped, 2 * c + t + 1)
                    for m in range(NH0 // 2):
                        mm = nc.tensor.transpose(PS[:, 2 * t + m // 4, (m % 4) * P:(m % 4 + 1) * P],
                                                 prob[:, t, 2 * m:2 * m + 2, :].rearrange("p a b -> p (a b)"),
                                                 ident[:, :])
                    mm.then_inc(pt_done, 1)

            def attend(c):
                pe.wait_ge(q_copied, 2 * min_next(c) + 2)
                pe.wait_ge(v_copied, 2 * c + 2)
                for t in range(NP_):
                    pe.wait_ge(pt_copied, 2 * c + t + 1)
                    for j in range(2):
                        for m in range(NH0 // 2):
                            mm = nc.tensor.matmul(PS[64 * j:64 * j + 64, 6 + t, m * 64:(m + 1) * 64],
                                                  probT[:, t, m, 64 * j:64 * j + 64], vbd[:, 2 * t + j, m, :],
                                                  start=True, stop=True, skip_group_check=True)
                    mm.then_inc(pv_done, 1)

            def out_transposes(c):
                if not (isinstance(c, int) and c == NCA - 1):
                    pe.wait_ge(v_copied, 2 * c + 4)
                for t in range(NP_):
                    pe.wait_ge(o_normed, 2 * c + t + 1)
                    for e in range(KD):
                        mm = nc.tensor.transpose(PS[:, 4 + t, e * P:(e + 1) * P], oN[:, t, e * P:(e + 1) * P], ident[:, :])
                    mm.then_inc(ot_done, 1)

            def out_project(c):
                pe.wait_ge(ot_hi, 2 * c + 2)
                pe.wait_ge(ot_lo, 2 * c + 2)
                for e in range(KD):
                    out = PS[:, 4 + e // 2, (e % 2) * CA:(e % 2 + 1) * CA]
                    n = 0
                    for k in range(KD):
                        for a, b in PASSES:
                            mm = nc.tensor.matmul(out, w_sb[3][a][:, k, e * P:(e + 1) * P], oT[b][:, k, :],
                                                  start=(n == 0), stop=(n == 3 * KD - 1))
                            n += 1
                    if e % 2:
                        mm.then_inc(wo_done, 1)

            def min_next(c):
                return c + 1 if not isinstance(c, int) else min(c + 1, NCA - 1)

            def turn(i, first=False, last=False):
                scores(i)
                if not first:
                    out_transposes(i - 1)
                if not last:
                    keys(i + 1)
                if not first:
                    out_project(i - 1)
                if not last:
                    queries(i + 1)
                prob_transposes(i)
                if not last:
                    if not first:
                        pe.wait_ge(y_copied, 2 * i)
                    values(i + 1)
                attend(i)

            pe.wait_ge(w_hi, 1)
            pe.wait_ge(w_lo, 1)
            pe.wait_ge(ident_made, 2)
            keys(0)
            pe.wait_ge(w_hi, 2)
            pe.wait_ge(w_lo, 2)
            queries(0)
            pe.wait_ge(w_hi, 3)
            pe.wait_ge(w_lo, 3)
            values(0)
            pe.wait_ge(w_hi, 4)
            pe.wait_ge(w_lo, 4)
            pe.wait_ge(v_copied, 2)
            turn(0, first=True)
            with pe.Fori(1, NCA - 1) as i:
                turn(i)
            turn(NCA - 1, last=True)
            out_transposes(NCA - 1)
            out_project(NCA - 1)

            pe.wait_ge(y_copied, 2 * NCA)

            def gate_up(g, f, c):
                s = group_step[g] + GROUPS[g][1] * c + f
                blk = GROUPS[g][0] + f
                p = f % 2
                if not (isinstance(s, int) and s < 2):
                    repeat = f == 0 and (GROUPS[g][1] % 2 and not (isinstance(c, int) and c == 0)
                                         or g and GROUPS[g - 1][1] % 2 and isinstance(c, int) and c == 0)
                    pe.wait_ge(mul_done, s if repeat else s - 1)
                if g == 0 and f == 0:
                    pe.wait_ge(y_hi, c + 1)
                    pe.wait_ge(y_lo, c + 1)
                if isinstance(c, int) and c == 0:
                    pe.wait_ge(tab_ready, 2 * blk + 2)
                w = [wtab(blk, a) for a in range(2)]
                for q in range(2):
                    n = 0
                    for k in range(KD):
                        for a, b in PASSES:
                            mm = nc.tensor.matmul(PS[:, 4 + 2 * p + q, :], w[a][:, q * D + k * P:q * D + (k + 1) * P],
                                                  ys[b][:, k, bass.ds(c * CF, CF)],
                                                  start=(n == 0), stop=(n == 3 * KD - 1))
                            n += 1
                mm.then_inc(gu_done, 1)

            def down(g, f, c):
                s = group_step[g] + GROUPS[g][1] * c + f
                blk = GROUPS[g][0] + f
                rows = P if blk < NBLK - 1 else LAST
                p = f % 2
                pe.wait_ge(h_hi, s + 1)
                pe.wait_ge(h_lo, s + 1)
                if f == 0 and not (g == 0 and isinstance(c, int) and c == 0):
                    pe.wait_ge(acc_added, NCF * g + c)
                w = [wtab(blk, a) for a in range(2)]
                for d in range(KD):
                    for n, (a, b) in enumerate(PASSES):
                        mm = nc.tensor.matmul(PS[:, d, :], w[a][0:rows, 2 * D + d * P:2 * D + (d + 1) * P],
                                              hs[b][0:rows, p, :], start=(f == 0 and n == 0),
                                              stop=(f == GROUPS[g][1] - 1 and n == 2))
                mm.then_inc(d_done, 1)

            def ffn_chunk(g, c, before):
                for f in range(GROUPS[g][1]):
                    gate_up(g, f, c)
                    if f:
                        down(g, f - 1, c)
                    elif before is not None:
                        down(*before)

            before = None
            for g in range(len(GROUPS)):
                ffn_chunk(g, 0, before)
                with pe.Fori(1, NCF) as c:
                    ffn_chunk(g, c, (g, GROUPS[g][1] - 1, c - 1))
                before = (g, GROUPS[g][1] - 1, NCF - 1)
            down(*before)

            def linear_chunk(c):
                pe.wait_ge(x1_hi, c + 1)
                pe.wait_ge(x1_lo, c + 1)
                if c:
                    pe.wait_ge(xa_masked, c)
                n = 0
                for k in range(KD):
                    for a, b in PASSES:
                        mm = nc.tensor.matmul(PS[:, 4, :], a_sb[a][:, k, :], x1s[b][:, c % 2, k, :],
                                              start=(n == 0), stop=(n == 3 * KD - 1))
                        n += 1
                mm.then_inc(xa_done, 1)
                for t in range(NT):
                    m = NT * c + t
                    if m >= 2:
                        pe.wait_ge(scored, m - 1)
                        pe.wait_ge(out_added, m - 1)
                    for k in range(KD):
                        mm = nc.tensor.transpose(PS[:, 2 + t % 2, k * P:(k + 1) * P], x1[:, k, c * CF + t * P:c * CF + (t + 1) * P],
                                                 ident[:, :])
                    mm.then_inc(xn_done, 1)
                    n = 0
                    for k in range(KD):
                        for a, b in PASSES:
                            nc.tensor.matmul(PS[:, t % 2, :], x1s[a][:, c % 2, k, t * P:(t + 1) * P], w1_sb[b][:, k, :],
                                             start=(n == 0), stop=False)
                            n += 1
                    if t == 0:
                        pe.wait_ge(xa_hi, c + 1)
                        pe.wait_ge(xa_lo, c + 1)
                    for n, (a, b) in enumerate(PASSES):
                        mm = nc.tensor.matmul(PS[:, t % 2, :], xas[a][:, t * P:(t + 1) * P], b_sb[b][:, :],
                                              start=False, stop=(n == 2))
                    mm.then_inc(h_done, 1)

            pe.wait_ge(w1_hi, 3)
            pe.wait_ge(w1_lo, 3)
            pe.wait_ge(acc_added, NCF * len(GROUPS))
            pe.wait_ge(mul_done, group_step[-1])
            for c in range(NCF):
                linear_chunk(c)

            pe.wait_ge(scored, NPAIR)
            pe.wait_ge(out_added, NPAIR)
            nc.tensor.transpose(PS[0:NPAIR, 5, 0:P], score[:, :], ident[:, :]).then_inc(top_pe, 1)
            pe.wait_ge(top, 9)
            nc.tensor.transpose(PS[:, 6, 0:NPAIR], rank[0:NPAIR, :], ident[0:NPAIR, 0:NPAIR]).then_inc(top_pe, 1)
            pe.wait_ge(top, 11)
            for sb in range(NSB):
                mm = nc.tensor.matmul(PS[:, 7, sb * TABW:(sb + 1) * TABW],
                                      pick[:, 8 * sb:8 * sb + 8, :].rearrange("p a b -> p (a b)"), rope_sb[:, :],
                                      start=True, stop=True, skip_group_check=True)
            mm.then_inc(top_pe, 1)

            def rows_to_columns(src, bank):
                for sb in range(NSB):
                    for k in range(KD):
                        mm = nc.tensor.transpose(PS[:, bank + k // 2, (k % 2) * SEL + sb * P:(k % 2) * SEL + (sb + 1) * P],
                                                 src[:, sb, k * P:(k + 1) * P], ident[:, :])
                mm.then_inc(ht_done, 1)

            pe.wait_ge(normed, 1)
            rows_to_columns(xres, 4)
            pe.wait_ge(ht_copied, KD)
            pe.wait_ge(qkv_in, 48)
            tiles = [(w, n) for w, n in ((wq_sb, 4), (wk_sb, 2), (wv_sb, 2))]
            m = 0

            def turn_tile(m):
                pe.wait_ge(roped, m + 1)
                if m >= 2:
                    pe.wait_ge(rt_copied, m - 1)
                for h in range(4):
                    mm = nc.tensor.transpose(PS[:, 6 + m % 2, h * P:(h + 1) * P], turned_of(m)[:, h * P:(h + 1) * P],
                                             ident[:, :])
                mm.then_inc(rt_done, 1)

            for w, count in tiles:
                for nt in range(count):
                    for sb in range(NSB):
                        if m >= 4:
                            pe.wait_ge(qkv_read, m - 3)
                        for k in range(KD):
                            mm = nc.tensor.matmul(PS[:, m % 4, :], hT[:, k, sb * P:(sb + 1) * P],
                                                  w[:, k, nt * 512:(nt + 1) * 512], start=(k == 0), stop=(k == KD - 1))
                        mm.then_inc(qkv_done, 1)
                        if 2 <= m < 14:
                            turn_tile(m - 2)
                        m += 1

            pe.wait_ge(rt_copied, 12)
            pe.wait_ge(qkv_read, 16)

            def scores2(g):
                if g >= 2:
                    pe.wait_ge(s2_masked, g - 1)
                for j in range(HG):
                    h, bank = HG * g + j, HG * (g % 2) + j
                    nc.tensor.matmul(PS[:, bank, 0:P], qT2[:, h, 0:P], kT2[:, h // 2, 0:P], start=True, stop=True,
                                     skip_group_check=True)
                    mm = nc.tensor.matmul(PS[:, bank, P:3 * P], qT2[:, h, P:SEL], kT2[:, h // 2, :], start=True,
                                          stop=True, skip_group_check=True)
                mm.then_inc(s2_done, 1)

            def transposes2(h):
                g = h // HG
                pe.wait_ge(s2_norm, 2 * g + 2)
                if h >= 2:
                    pe.wait_ge(p2t_copied, h - 1)
                for n in range(3):
                    mm = nc.tensor.transpose(PS[:, 4 + h % 2, n * P:(n + 1) * P],
                                             prob2[:, g % 4, h % HG, n * P:(n + 1) * P], ident[:, :])
                mm.then_inc(p2t_done, 1)

            def values2(h):
                pe.wait_ge(p2t_copied, h + 1)
                if h >= 2:
                    pe.wait_ge(o2_copied, h - 1)
                o = 6 + h % 2
                hv = slice((h // 2) * HD, (h // 2 + 1) * HD)
                nc.tensor.matmul(PS[:, o, 0:SEL], v2[:, 0, hv], prob2T[:, h % 4, 0:SEL], start=True, stop=False)
                nc.tensor.matmul(PS[:, o, P:SEL], v2[:, 1, hv], prob2T[:, h % 4, SEL:3 * P],
                                 start=False, stop=True).then_inc(pv2_done, 1)

            NG2 = NHQ // HG
            scores2(0)
            scores2(1)
            for g in range(NG2):
                if g + 2 < NG2:
                    scores2(g + 2)
                for h in range(HG * g, HG * g + HG):
                    transposes2(h)
                    if h:
                        values2(h - 1)
            values2(NHQ - 1)

            pe.wait_ge(o2_copied, NHQ)
            pe.wait_ge(wo_in, 16)
            for sb in range(NSB):
                for h in range(NHQ):
                    mm = nc.tensor.matmul(PS[:, sb, :], oT2[:, h, sb * P:(sb + 1) * P], wo_sb[:, h, :],
                                          start=(h == 0), stop=(h == NHQ - 1))
                mm.then_inc(wo2_done, 1)

            pe.wait_ge(normed, 2)
            rows_to_columns(hsel_normed, 4)
            pe.wait_ge(ht_copied, 2 * KD)
            pe.wait_ge(wg_in, 32)
            pe.wait_ge(wu_in, 16)
            pe.wait_ge(wd_in, 16)

            def gate_up2(f):
                if f >= 2:
                    pe.wait_ge(mul2, f - 1)
                bank = 4 + f % 2
                for q in range(2):
                    for k in range(KD):
                        w = wu_sb[:, k, f * P:(f + 1) * P] if q else wg_sb[k // 2][:, k % 2, f * P:(f + 1) * P]
                        mm = nc.tensor.matmul(PS[:, bank, q * SEL:(q + 1) * SEL], w, h2T[:, k, :],
                                              start=(k == 0), stop=(k == KD - 1))
                mm.then_inc(g2_done, 1)

            def down2(f):
                pe.wait_ge(mul2, f + 1)
                for sb in range(NSB):
                    mm = nc.tensor.matmul(PS[:, 2 + sb, :], mT[:, f, sb * P:(sb + 1) * P], wd_sb[:, f, :],
                                          start=(f == 0), stop=(f == NF1 - 1))
                mm.then_inc(d2_done, 1)

            gate_up2(0)
            for f in range(NF1):
                if f + 1 < NF1:
                    gate_up2(f + 1)
                down2(f)

        @block.scalar
        def _(act):
            act.wait_ge(idx_in, 16)
            nc.scalar.copy(idx_bf[:, :], idx_raw[:, :]).then_inc(idx_conv, 1)
            order = (1, 0, 2, 3)
            for m, n in enumerate(order):
                act.wait_ge(w_in[n], 16)
                nc.scalar.copy(w_sb[n][0][:, :, :], w_raw[n][:, :, :]).then_inc(w_hi, 1)
                if m == 0:
                    act.wait_ge(x_in, 16)
                    nc.scalar.copy(xs[0][:, :, :], xr[:, :, :]).then_inc(x_hi, 1)

            def next_indices(h):
                act.wait_ge(idx_in, 16 * (h + 1))
                nc.scalar.copy(idx_bf[:, :], idx_raw[:, :]).then_inc(idx_conv, 1)

            def table_high(g, h, more=True):
                act.wait_ge(lut_seq, LUT_OPS * (h + 1))
                hi, _, whole = half_block(g, h)
                nc.scalar.copy(hi, whole).then_inc(tab_hi, 1)
                if more:
                    next_indices(h + 1)

            def copy_keys(c, bank):
                act.wait_ge(k_done, 2 * c + bank + 1)
                for e in (2 * bank, 2 * bank + 1):
                    for h in range(4):
                        src = PS[32 * h:32 * h + 32, 6 + bank, (e % 2) * CA:(e % 2 + 1) * CA].rearrange("p (b t) -> p b t", b=BC)
                        ins = nc.scalar.copy(kbd[32 * h:32 * h + 32, e, :, h * S:(h + 1) * S], src)
                ins.then_inc(k_copied, 1)

            def copy_queries(c):
                for bank in range(2):
                    act.wait_ge(q_done, 2 * c + bank + 1)
                    nc.scalar.copy(qT[:, 2 * bank:2 * bank + 2, :].rearrange("p a b -> p (a b)"),
                                   PS[:, 6 + bank, :]).then_inc(q_copied, 1)

            def copy_values(c):
                for t in range(NP_):
                    act.wait_ge(v_done, 2 * c + t + 1)
                    for j in range(2):
                        for h in range(2):
                            src = PS[64 * j:64 * j + 64, 4 + t, :].rearrange("p (m h d) -> p m h d", h=2, d=HD0)[:, :, h, :]
                            ins = nc.scalar.copy(vbd[64 * h:64 * h + 64, 2 * t + j, :, h * HD0:(h + 1) * HD0], src)
                    ins.then_inc(v_copied, 1)

            def split_x(c):
                act.wait_ge(v_done, 2 * c)
                act.wait_ge(x_in, 16 * c + 16)
                nc.scalar.copy(xs[0][:, :, :], xr[:, :, :]).then_inc(x_hi, 1)

            def exps(c):
                for t in range(NP_):
                    act.wait_ge(shifted, 2 * c + t + 1)
                    pr = prob[:, t, :, :].rearrange("p a b -> p (a b)")
                    nc.scalar.activation(pr, pr, ACT.Exp).then_inc(exped, 1)

            def copy_prob(c):
                for t in range(NP_):
                    act.wait_ge(pt_done, 2 * c + t + 1)
                    nc.scalar.copy(probT[:, t, :, :].rearrange("p a b -> p (a b)"),
                                   PS[:, 2 * t:2 * t + 2, :].rearrange("p a b -> p (a b)")).then_inc(pt_copied, 1)

            def split_out(c):
                for t in range(NP_):
                    act.wait_ge(ot_done, 2 * c + t + 1)
                    nc.scalar.copy(oT[0][:, :, t * P:(t + 1) * P],
                                   PS[:, 4 + t, :].rearrange("p (e q) -> p e q", e=KD)).then_inc(ot_hi, 1)

            def copy_y(c, stored=True):
                if stored:
                    act.wait_ge(y_stored, 16 * c)
                for bank in range(2):
                    act.wait_ge(wo_done, 2 * c + bank + 1)
                    nc.scalar.copy(yc[:, 2 * bank:2 * bank + 2, :].rearrange("p a b -> p (a b)"),
                                   PS[:, 4 + bank, :]).then_inc(y_copied, 1)

            def turn(i, first=False, second=False, last=False, split=True):
                act.wait_ge(s_done, i + 1)
                if not first:
                    split_out(i - 1)
                if not last:
                    copy_keys(i + 1, 0)
                    copy_keys(i + 1, 1)
                exps(i)
                if not first:
                    copy_y(i - 1, stored=not second)
                if not last:
                    copy_queries(i + 1)
                copy_prob(i)
                if not last:
                    if split:
                        split_x(i + 2)
                    table_high(0, i + 1)
                    act.wait_ge(pv_done, 2 * i + 2)
                    copy_values(i + 1)

            act.wait_ge(zeroed, 2)
            copy_keys(0, 0)
            copy_keys(0, 1)
            copy_queries(0)
            copy_values(0)
            split_x(1)
            table_high(0, 0)
            turn(0, first=True)
            turn(1, second=True)
            with act.Fori(2, NCA - 2) as i:
                turn(i)
            turn(NCA - 2, split=False)
            turn(NCA - 1, last=True)

            def split_y(c):
                act.wait_ge(y_in[c], 16)
                nc.scalar.copy(ys[0][:, :, c * CF:(c + 1) * CF], y_raw[:, :, c * CF:(c + 1) * CF]).then_inc(y_hi, 1)

            split_y(0)
            split_out(NCA - 1)
            copy_y(NCA - 1)

            def ffn_step(g, f, c, table=None):
                s = group_step[g] + GROUPS[g][1] * c + f
                p = f % 2
                act.wait_ge(gu_done, s + 1)
                nc.scalar.activation(sg[:, p, :], PS[:, 4 + 2 * p, :], ACT.Silu).then_inc(silu_done, 1)
                if table is not None:
                    table_high(*table, more=False)
                act.wait_ge(mul_done, s + 1)
                if not (isinstance(s, int) and s < 2):
                    repeat = f == 0 and (GROUPS[g][1] % 2 and not (isinstance(c, int) and c == 0)
                                         or g and GROUPS[g - 1][1] % 2 and isinstance(c, int) and c == 0)
                    act.wait_ge(d_done, s if repeat else s - 1)
                nc.scalar.copy(hs[0][:, p, :], hf[:, p, :]).then_inc(h_hi, 1)
                if table is not None and table[1] is not last_half:
                    next_indices(table[1] + 1)

            for c in range(NCF):
                for f in range(GROUPS[0][1]):
                    n = GROUPS[0][1] * c + f
                    ffn_step(0, f, c, ends_at.get(n - 1))
                    if n + 1 < NCF:
                        split_y(n + 1)
            for g in range(1, len(GROUPS)):
                nb = GROUPS[g][1]
                for f in range(nb):
                    ffn_step(g, f, 0, None if f else last_before[g])
                if g == len(GROUPS) - 1:
                    act.wait_ge(w1_in, 48)
                    nc.scalar.copy(w1_sb[0][:, :, :], w1_raw[:, :, :]).then_inc(w1_hi, 1)
                    nc.scalar.copy(a_sb[0][:, :, :], a_raw[:, :, :]).then_inc(w1_hi, 1)
                    nc.scalar.copy(b_sb[0][:, :], b_raw[:, :]).then_inc(w1_hi, 1)
                with act.Fori(1, NCF) as c:
                    for f in range(nb):
                        more = g + 1 < len(GROUPS) and f == 0
                        ffn_step(g, f, c, table=(g + 1, 2 * GROUPS[g + 1][0] + c - 1) if more else None)

            def split_x1(c):
                act.wait_ge(acc_added, (len(GROUPS) - 1) * NCF + c + 1)
                if c >= 2:
                    act.wait_ge(h_done, NT * (c - 1))
                nc.scalar.copy(x1s[0][:, c % 2, :, :], x1[:, :, c * CF:(c + 1) * CF]).then_inc(x1_hi, 1)

            def linear_tiles(c):
                act.wait_ge(xa_masked, c + 1)
                if c:
                    act.wait_ge(h_done, NT * c)
                nc.scalar.copy(xas[0][:, :], xa[:, :]).then_inc(xa_hi, 1)
                for t in range(NT):
                    m = NT * c + t
                    act.wait_ge(h_done, m + 1)
                    if m >= 2:
                        act.wait_ge(h_stored[t % 2], 16 * (NT // 2 * c + t // 2))
                        act.wait_ge(out_added, m - 1)
                        act.wait_ge(scored, m - 1)
                    nc.scalar.copy(h_tile[:, t % 2, :], PS[:, t % 2, :]).then_inc(h_copied, 1)

            act.wait_ge(d_done, group_step[-1])
            split_x1(0)
            for c in range(NCF):
                if c + 1 < NCF:
                    split_x1(c + 1)
                linear_tiles(c)

            def root_of(n):
                act.wait_ge(norm, 9 * n + 3)
                nc.scalar.activation(stat[:, 1, :], stat[:, 0, :], ACT.Sqrt).then_inc(root, 1)

            def copy_columns(dst, n):
                act.wait_ge(ht_done, n + 1)
                for k in range(KD):
                    nc.scalar.activation(dst[:, k, :], PS[:, 4 + k // 2, (k % 2) * SEL:(k % 2 + 1) * SEL], ACT.Copy,
                                         scale=ln_sb[:, n, k:k + 1]).then_inc(ht_copied, 1)

            root_of(0)
            copy_columns(hT, 0)
            for m in range(12):
                act.wait_ge(rt_done, m + 1)
                head, sb = 4 * (m // 2), m % 2
                dst = qT2[:, head:head + 4, sb * P:(sb + 1) * P] if m < 8 else kT2[:, head - 16:head - 12, sb * P:(sb + 1) * P]
                nc.scalar.copy(dst, PS[:, 6 + m % 2, :].rearrange("p (h q) -> p h q", h=4)).then_inc(rt_copied, 1)

            def exps2(g):
                act.wait_ge(s2_max, 2 * g + 2)
                for j in range(HG):
                    for sb in range(NSB):
                        part = prob2[:, g % 4, j, sb * P:(2 * sb + 1) * P]
                        nc.scalar.activation(part, part, ACT.Exp, bias=negmax2[:, g % 4, j, sb:sb + 1],
                                             accum_out=rowsum2[:, g % 4, j, sb:sb + 1]).then_inc(s2_exp, 1)

            def copy_prob2(h):
                act.wait_ge(p2t_done, h + 1)
                if h >= 4:
                    act.wait_ge(pv2_done, h - 3)
                nc.scalar.copy(prob2T[:, h % 4, :], PS[:, 4 + h % 2, 0:3 * P]).then_inc(p2t_copied, 1)

            def copy_out(h):
                act.wait_ge(pv2_done, h + 1)
                nc.scalar.copy(oT2[:, h, :], PS[:, 6 + h % 2, 0:SEL]).then_inc(o2_copied, 1)

            NG2 = NHQ // HG
            exps2(0)
            exps2(1)
            for g in range(NG2):
                for h in range(HG * g, HG * g + HG):
                    copy_prob2(h)
                    if h:
                        copy_out(h - 1)
                if g + 2 < NG2:
                    exps2(g + 2)
            copy_out(NHQ - 1)
            act.wait_ge(gate_seq, 1)
            nc.scalar.activation(stat[:, 6, :], stat[:, 5, :], ACT.Exp, scale=-1.0).then_inc(gate_exp, 1)
            root_of(1)
            copy_columns(h2T, 1)
            for f in range(NF1):
                act.wait_ge(g2_done, f + 1)
                nc.scalar.activation(sg1[:, f % 2, :], PS[:, 4 + f % 2, 0:SEL], ACT.Silu).then_inc(silu2, 1)

        @block.vector
        def _(dve):
            def lut_part(g, h, v0, v1, meanwhile=None):
                acc = half_block(g, h)[2]
                n = max(0, 2 * v0 - 1)

                def counted(ins):
                    nonlocal n
                    ins.then_inc(lut_seq, 1)
                    n += 1
                    return n

                seen = n
                if v0 == 0:
                    dve.wait_ge(idx_conv, h + 1)
                    seen = counted(nc.vector.tensor_scalar(acc, idx_bf[:, :], 0.0, lut_sb[:, 0:1],
                                                           ALU.is_equal, ALU.mult))
                    v0 = 1
                made = {}
                call_at = v0 + 1 if v0 == 1 else v0 + 2
                for v in range(v0, v1 + 1):
                    if v < v1:
                        ins = nc.vector.tensor_scalar(onehot[:, v % 3, :], idx_bf[:, :], float(v), None, ALU.is_equal)
                        made[v] = counted(ins)
                    if v == call_at and meanwhile is not None:
                        meanwhile()
                    if v > v0:
                        u = v - 1
                        dve.wait_ge(lut_seq, LUT_OPS * h + max(made[u], seen))
                        seen = counted(nc.vector.scalar_tensor_tensor(
                            acc, onehot[:, u % 3, :], lut_sb[:, u:u + 1], acc, ALU.mult, ALU.add))

            def table_low(g, h):
                dve.wait_ge(tab_hi, h + 1)
                hi, lo, whole = half_block(g, h)
                nc.vector.tensor_tensor(lo, whole, hi.bitcast(F32), ALU.subtract).then_inc(tab_ready, 1)

            SOFT = 8

            def split_w(m, n):
                dve.wait_ge(w_hi, m + 1)
                nc.vector.tensor_tensor(w_sb[n][1][:, :, :], w_raw[n][:, :, :], w_sb[n][0][:, :, :].bitcast(F32),
                                        ALU.subtract).then_inc(w_lo, 1)

            def split_x(c):
                dve.wait_ge(x_hi, c + 1)
                nc.vector.tensor_tensor(xs[1][:, :, :], xr[:, :, :], xs[0][:, :, :].bitcast(F32),
                                        ALU.subtract).then_inc(x_lo, 1)

            dve.wait_ge(lut_in, 16)
            lut_part(0, 0, 0, 6)
            split_w(0, 1)
            split_x(0)
            lut_part(0, 0, 6, 8)
            split_w(1, 0)
            lut_part(0, 0, 8, 11)
            split_w(2, 2)
            lut_part(0, 0, 11, 14)
            split_w(3, 3)
            lut_part(0, 0, 14, 16)
            dve.wait_ge(consts_in, 32)
            nc.vector.tensor_scalar(beta[:, :], beta[:, :], 4.0, float(HD0) ** -0.5, ALU.min, ALU.mult).then_inc(beta_ready, 1)
            dve.wait_ge(beta_ready, 1)
            split_x(1)
            table_low(0, 0)

            def scale_and_mask(i):
                dve.wait_ge(s_done, i + 1)
                if not (isinstance(i, int) and i == 0):
                    dve.wait_ge(pt_done, 2 * i)
                for t in range(NP_):
                    out = prob[:, t, :, :].rearrange("p (e h) k -> p e (h k)", e=KD)
                    src = PS[:, 0:KD, t * 256:(t + 1) * 256]
                    m4 = mask[:, :].unsqueeze(1).to_broadcast([P, KD, 4 * S])
                    nc.vector.scalar_tensor_tensor(out, src, beta[:, bass.ds(2 * i + t, 1)], m4,
                                                   ALU.mult, ALU.add).then_inc(soft, 1)

            def subtract_max(i):
                b0 = SOFT * i
                for t in range(NP_):
                    dve.wait_ge(soft, b0 + 1 + t)
                    nc.vector.tensor_reduce(rowmax[:, t, :], prob[:, t, :, :], AX, ALU.max).then_inc(soft, 1)
                for t in range(NP_):
                    dve.wait_ge(soft, b0 + 3 + t)
                    nc.vector.tensor_tensor(prob[:, t, :, :], prob[:, t, :, :],
                                            rowmax[:, t, :].unsqueeze(2).to_broadcast([P, NH0, S]),
                                            ALU.subtract).then_inc(shifted, 1)

            def sums(i):
                b0 = SOFT * i + 4
                for t in range(NP_):
                    dve.wait_ge(exped, 2 * i + t + 1)
                    nc.vector.tensor_reduce(rowsum[:, t, :], prob[:, t, :, :], AX, ALU.add).then_inc(soft, 1)
                for t in range(NP_):
                    dve.wait_ge(soft, b0 + 1 + t)
                    nc.vector.reciprocal(rowinv[:, t, :], rowsum[:, t, :]).then_inc(soft, 1)

            def normalise(i):
                for t in range(NP_):
                    dve.wait_ge(pv_done, 2 * i + t + 1)
                    dve.wait_ge(soft, SOFT * i + 7 + t)
                    nc.vector.tensor_tensor(oN[:, t, :].rearrange("p (h d) -> p h d", d=HD0),
                                            PS[:, 6 + t, :].rearrange("p (h d) -> p h d", d=HD0),
                                            rowinv[:, t, :].unsqueeze(2).to_broadcast([P, NH0, HD0]),
                                            ALU.mult).then_inc(o_normed, 1)

            def split_out(i):
                for t in range(NP_):
                    dve.wait_ge(ot_hi, 2 * i + t + 1)
                    nc.vector.tensor_tensor(oT[1][:, :, t * P:(t + 1) * P],
                                            PS[:, 4 + t, :].rearrange("p (e q) -> p e q", e=KD),
                                            oT[0][:, :, t * P:(t + 1) * P].bitcast(F32), ALU.subtract).then_inc(ot_lo, 1)

            def split_y(c):
                dve.wait_ge(y_hi, c + 1)
                nc.vector.tensor_tensor(ys[1][:, :, c * CF:(c + 1) * CF], y_raw[:, :, c * CF:(c + 1) * CF],
                                        ys[0][:, :, c * CF:(c + 1) * CF].bitcast(F32), ALU.subtract).then_inc(y_lo, 1)

            def turn(i, first=False, last=False, split=True):
                if not first:
                    normalise(i - 1)
                g = int(last)
                if not first:
                    lut_part(g, i + 1, 0, 4)
                scale_and_mask(i)
                if not first:
                    split_out(i - 1)
                subtract_max(i)
                lut_part(g, i + 1, 0 if first else 4, 6)
                sums(i)
                if not last:
                    lut_part(0, i + 1, 6, 16)
                    if split:
                        split_x(i + 2)
                    table_low(0, i + 1)

            turn(0, first=True)
            with dve.Fori(1, NCA - 2) as i:
                turn(i)
            turn(NCA - 2, split=False)
            turn(NCA - 1, last=True)
            split_y(0)
            normalise(NCA - 1)
            split_out(NCA - 1)
            lut_part(1, NCA, 6, 16)

            def add_down(g, f, c):
                s = group_step[g] + GROUPS[g][1] * c + f
                dve.wait_ge(d_done, s + 1)
                if g:
                    dve.wait_ge(acc_added, NCF * g + c)
                part = x1[:, :, bass.ds(c * CF, CF)]
                nc.vector.tensor_tensor(part, PS[:, 0:KD, :], part, ALU.add).then_inc(acc_added, 1)

            def ffn_step(g, f, c, before=None, table=None, part=None):
                s = group_step[g] + GROUPS[g][1] * c + f
                p = f % 2
                dve.wait_ge(gu_done, s + 1)
                dve.wait_ge(silu_done, s + 1)
                repeat = f == 0 and (GROUPS[g][1] % 2 and not (isinstance(c, int) and c == 0)
                                     or g and GROUPS[g - 1][1] % 2 and isinstance(c, int) and c == 0)
                if not (isinstance(s, int) and s < 2):
                    dve.wait_ge(h_lo, s if repeat else s - 1)
                nc.vector.tensor_tensor(hf[:, p, :], sg[:, p, :], PS[:, 5 + 2 * p, :], ALU.mult).then_inc(mul_done, 1)

                def h_low():
                    dve.wait_ge(h_hi, s + 1)
                    nc.vector.tensor_tensor(hs[1][:, p, :], hf[:, p, :], hs[0][:, p, :].bitcast(F32),
                                            ALU.subtract).then_inc(h_lo, 1)

                if before is not None:
                    add_down(*before)
                    h_low()
                if table is not None:
                    table_low(*table)
                if part is not None:
                    lut_part(*part, None if before is not None else h_low)
                elif before is None:
                    h_low()

            for c in range(NCF):
                for f in range(GROUPS[0][1]):
                    n = GROUPS[0][1] * c + f
                    if n == 3:
                        dve.wait_ge(x1_in, 16)
                    ffn_step(0, f, c, (0, GROUPS[0][1] - 1, c - 1) if c and f == 0 else None, ends_at.get(n - 1),
                             (1, *first_parts[n]))
                    if n + 1 < NCF:
                        split_y(n + 1)
            for g in range(1, len(GROUPS)):
                nb = GROUPS[g][1]
                cuts = [0] + [-(-LUTN * (f + 1) // nb) for f in range(nb)]
                more = g + 1 < len(GROUPS)

                def split_w1():
                    dve.wait_ge(w1_hi, 3)
                    for n, (part, raw) in enumerate(((w1_sb, w1_raw), (a_sb, a_raw), (b_sb, b_raw))):
                        whole = tuple([slice(None)] * (3 if n < 2 else 2))
                        nc.vector.tensor_tensor(part[1][whole], raw[whole], part[0][whole].bitcast(F32),
                                                ALU.subtract).then_inc(w1_lo, 1)

                def chunk(c, before, table):
                    for f in range(nb):
                        ffn_step(g, f, c, before if f == 0 else None, table if f == 0 else None,
                                 (g + 1, 2 * GROUPS[g + 1][0] + c, cuts[f], cuts[f + 1]) if more else None)

                chunk(0, (g - 1, GROUPS[g - 1][1] - 1, NCF - 1), last_before[g])
                if not more:
                    split_w1()
                with dve.Fori(1, NCF) as c:
                    chunk(c, (g, nb - 1, c - 1), (g + 1, 2 * GROUPS[g + 1][0] + c - 1) if more else None)
            add_down(len(GROUPS) - 1, GROUPS[-1][1] - 1, NCF - 1)

            dve.wait_ge(small_in, 16 * 9)
            nc.vector.tensor_copy(tok_adf[:, :], tok_ad[:, :]).then_inc(admask_made, 1)
            dve.wait_ge(admask_made, 1)
            nc.vector.tensor_scalar(admask[:, :], tok_adf[:, :], row_ad[:, 0:1], scal_sb[:, 0:1],
                                    ALU.is_equal, ALU.mult).then_inc(admask_made, 1)
            dve.wait_ge(admask_made, 2)

            def split_x1(c):
                dve.wait_ge(x1_hi, c + 1)
                nc.vector.tensor_tensor(x1s[1][:, c % 2, :, :], x1[:, :, c * CF:(c + 1) * CF],
                                        x1s[0][:, c % 2, :, :].bitcast(F32), ALU.subtract).then_inc(x1_lo, 1)

            def linear_tiles(c):
                dve.wait_ge(xa_done, c + 1)
                if c:
                    dve.wait_ge(xa_lo, c)
                    dve.wait_ge(xa_hi, c)
                per = CF // S
                nc.vector.tensor_tensor(xa[:, :].rearrange("p (b t) -> p b t", t=S),
                                        PS[:, 4, :].rearrange("p (b t) -> p b t", t=S),
                                        admask[:, c * per:(c + 1) * per].unsqueeze(2).to_broadcast([P, per, S]),
                                        ALU.mult).then_inc(xa_masked, 1)
                dve.wait_ge(xa_hi, c + 1)
                dve.wait_ge(xa_masked, c + 1)
                nc.vector.tensor_tensor(xas[1][:, :], xa[:, :], xas[0][:, :].bitcast(F32), ALU.subtract).then_inc(xa_lo, 1)
                for t in range(NT):
                    m = NT * c + t
                    dve.wait_ge(h_copied, m + 1)
                    if m:
                        dve.wait_ge(scored, m)
                    nc.vector.tensor_tensor_reduce(prod[:, :], h_tile[:, t % 2, :], router_sb[:, :], 1.0, 0.0,
                                                   ALU.mult, ALU.add, score[:, m:m + 1]).then_inc(scored, 1)
                    dve.wait_ge(xn_done, m + 1)
                    if m >= 2:
                        dve.wait_ge(out_stored[t % 2], 16 * (NT // 2 * c + t // 2))
                    nc.vector.tensor_tensor(out_tile[:, t % 2, :], h_tile[:, t % 2, :], PS[:, 2 + t % 2, :],
                                            ALU.add).then_inc(out_added, 1)

            split_x1(0)
            for c in range(NCF):
                if c + 1 < NCF:
                    split_x1(c + 1)
                linear_tiles(c)

            tops = [0]

            def step(ins):
                ins.then_inc(top, 1)
                tops[0] += 1
                dve.wait_ge(top, tops[0])

            R16 = slice(0, NPAIR)
            dve.wait_ge(top_pe, 1)
            step(nc.vector.tensor_copy(scoreT[R16, :], PS[R16, 5, 0:P]))
            for j in range(2):
                half = slice(j * S, (j + 1) * S)
                step(nc.vector.max(best[R16, j, :], scoreT[R16, half]))
                step(nc.vector.match_replace(replaced[R16, half], best[R16, j, :], scoreT[R16, half], -3.0e38))
            step(nc.vector.tensor_tensor(picked[R16, :], replaced[R16, :], scoreT[R16, :], ALU.not_equal))
            dve.wait_ge(zeroed, 3)
            for j in range(2):
                half = slice(j * S, (j + 1) * S)
                step(nc.vector.tensor_tensor_scan(rank[R16, half], onesr[R16, :], picked[R16, half], 0.0,
                                                  ALU.mult, ALU.add))
            step(nc.vector.tensor_tensor(rank[R16, :], rank[R16, :], picked[R16, :], ALU.mult))
            assert tops[0] == 9
            dve.wait_ge(top_pe, 2)
            step(nc.vector.tensor_copy(rankT[:, :], PS[:, 6, 0:NPAIR]))
            step(nc.vector.tensor_tensor(pick[:, :, :], rankT[:, :].unsqueeze(2).to_broadcast([P, NPAIR, 2 * TOPK]),
                                         slots_sb[:, :].unsqueeze(1).to_broadcast([P, NPAIR, 2 * TOPK]), ALU.is_equal))
            assert tops[0] == 11
            dve.wait_ge(top_pe, 3)
            step(nc.vector.tensor_copy(tables[:, :, :].rearrange("p a b -> p (a b)"), PS[:, 7, 0:NSB * TABW]))
            nc.vector.tensor_tensor(rowidx[:, :], tables[:, :, TABW - 1], pair_sb[:, :], ALU.add).then_inc(rows_ready, 1)

            def inverse_rms(src, n):
                seen = [9 * n]

                def step(ins):
                    ins.then_inc(norm, 1)
                    seen[0] += 1
                    dve.wait_ge(norm, seen[0])

                for sb in range(NSB):
                    step(nc.vector.tensor_tensor_reduce(scratch[:, :], src[:, sb, :], src[:, sb, :], 1.0, 0.0,
                                                        ALU.mult, ALU.add, stat[:, 7, sb:sb + 1]))
                step(nc.vector.tensor_scalar(stat[:, 0, :], stat[:, 7, :], 1.0 / D, EPS, ALU.mult, ALU.add))
                dve.wait_ge(root, n + 1)
                step(nc.vector.reciprocal(stat[:, 2, :], stat[:, 1, :]))
                step(nc.vector.tensor_tensor(stat[:, 3, :], stat[:, 2, :], stat[:, 2, :], ALU.mult))
                step(nc.vector.tensor_tensor(stat[:, 3, :], stat[:, 3, :], stat[:, 0, :], ALU.mult))
                step(nc.vector.tensor_scalar(stat[:, 3, :], stat[:, 3, :], -0.5, 1.5, ALU.mult, ALU.add))
                step(nc.vector.tensor_tensor(stat[:, 4, :], stat[:, 2, :], stat[:, 3, :], ALU.mult))

            dve.wait_ge(sel_in, 32)
            inverse_rms(hsel, 0)
            for sb in range(NSB):
                ins = nc.vector.tensor_scalar(xres[:, sb, :], hsel[:, sb, :], stat[:, 4, sb:sb + 1], None, ALU.mult)
                ins.then_inc(norm, 1) if sb == 0 else ins.then_inc(normed, 1)
            for sb in range(NSB):
                dve.wait_ge(norm, 9)
                ins = nc.vector.tensor_tensor_reduce(scratch[:, :], hsel[:, sb, :], router_sb[:, :], 1.0, 0.0,
                                                     ALU.mult, ALU.add, stat[:, 5, sb:sb + 1])
                ins.then_inc(gate_seq, 1)
                dve.wait_ge(gate_seq, sb + 1)

            dve.wait_ge(bias_in, 16)
            seen = 0
            for m in range(16):
                nt, sb = m // 2, m % 2
                dve.wait_ge(qkv_done, m + 1)
                if m < 12:
                    if m >= 2:
                        dve.wait_ge(rt_done, m - 1)
                        dve.wait_ge(rope_seq, seen)
                    nc.vector.tensor_tensor(biased[:, 0, :], PS[:, m % 4, :], bias_sb[:, nt * 512:(nt + 1) * 512],
                                            ALU.add).then_inc(qkv_read, 1)
                    dve.wait_ge(qkv_read, m + 1)
                    x4 = biased[:, 0, :].rearrange("p (h a w) -> p h a w", h=4, a=2)
                    cos = tables[:, sb, 0:ROPE_W].unsqueeze(1).to_broadcast([P, 8, ROPE_W])
                    nc.vector.tensor_tensor(times_cos[:, :].rearrange("p (a w) -> p a w", a=8),
                                            biased[:, 0, :].rearrange("p (a w) -> p a w", a=8), cos,
                                            ALU.mult).then_inc(rope_seq, 1)
                    y4 = times_sin[:, :].rearrange("p (h a w) -> p h a w", h=4, a=2)
                    for a in range(2):
                        sin = tables[:, sb, (1 + a) * ROPE_W:(2 + a) * ROPE_W].unsqueeze(1).to_broadcast([P, 4, ROPE_W])
                        nc.vector.tensor_tensor(y4[:, :, a, :], x4[:, :, 1 - a, :], sin, ALU.mult).then_inc(rope_seq, 1)
                    seen += 3
                    dve.wait_ge(rope_seq, seen)
                    nc.vector.tensor_tensor(turned_of(m), times_cos[:, :], times_sin[:, :], ALU.add).then_inc(roped, 1)
                    dve.wait_ge(roped, m + 1)
                else:
                    nc.vector.tensor_tensor(v2[:, sb, (nt - 6) * 512:(nt - 5) * 512], PS[:, m % 4, :],
                                            bias_sb[:, nt * 512:(nt + 1) * 512], ALU.add).then_inc(qkv_read, 1)

            def mask_and_max(g):
                dve.wait_ge(s2_done, g + 1)
                if g >= 4:
                    dve.wait_ge(p2t_done, HG * (g - 3))
                nc.vector.scalar_tensor_tensor(prob2[:, g % 4, :, :], PS[:, HG * (g % 2):HG * (g % 2) + HG, 0:3 * P],
                                               float(HD) ** -0.5, mask2[:, :].unsqueeze(1).to_broadcast([P, HG, 3 * P]),
                                               ALU.mult, ALU.add).then_inc(s2_masked, 1)
                dve.wait_ge(s2_masked, g + 1)
                for sb in range(NSB):
                    nc.vector.tensor_reduce(negmax2[:, g % 4, :, sb], prob2[:, g % 4, :, sb * P:(2 * sb + 1) * P], AX,
                                            ALU.max, negate=True).then_inc(s2_max, 1)

            def divide(g):
                dve.wait_ge(s2_exp, 2 * HG * (g + 1))
                nc.vector.reciprocal(rowsum2[:, g % 4, :, :], rowsum2[:, g % 4, :, :]).then_inc(s2_inv, 1)
                dve.wait_ge(s2_inv, g + 1)
                for sb in range(NSB):
                    part = prob2[:, g % 4, :, sb * P:(2 * sb + 1) * P]
                    nc.vector.tensor_tensor(part, part, rowsum2[:, g % 4, :, sb:sb + 1].to_broadcast([P, HG, (sb + 1) * P]),
                                            ALU.mult).then_inc(s2_norm, 1)

            NG2 = NHQ // HG
            mask_and_max(0)
            mask_and_max(1)
            for g in range(NG2):
                divide(g)
                if g + 2 < NG2:
                    mask_and_max(g + 2)
            dve.wait_ge(gate_exp, 1)
            nc.vector.tensor_scalar(stat[:, 6, :], stat[:, 6, :], 1.0, None, ALU.add).then_inc(gate_seq, 1)
            dve.wait_ge(gate_seq, 3)
            nc.vector.reciprocal(stat[:, 5, :], stat[:, 6, :]).then_inc(gate_seq, 1)
            dve.wait_ge(gate_seq, 4)

            for sb in range(NSB):
                dve.wait_ge(wo2_done, sb + 1)
                dve.wait_ge(ht_done, 1)
                nc.vector.tensor_tensor(xres[:, sb, :], PS[:, sb, :], hsel[:, sb, :], ALU.add).then_inc(gate_seq, 1)
            dve.wait_ge(gate_seq, 6)
            inverse_rms(xres, 1)
            for sb in range(NSB):
                ins = nc.vector.tensor_scalar(hsel_normed[:, sb, :], xres[:, sb, :], stat[:, 4, sb:sb + 1], None, ALU.mult)
                ins.then_inc(norm, 1) if sb == 0 else ins.then_inc(normed, 1)
            for sb in range(NSB):
                nc.vector.tensor_tensor(hsel[:, sb, :], xres[:, sb, :], hsel[:, sb, :], ALU.subtract).then_inc(gate_seq, 1)

            for f in range(NF1):
                dve.wait_ge(silu2, f + 1)
                nc.vector.tensor_tensor(mT[:, f, :], sg1[:, f % 2, :], PS[:, 4 + f % 2, SEL:2 * SEL], ALU.mult).then_inc(mul2, 1)

            dve.wait_ge(outsel_in, 32)
            dve.wait_ge(gate_seq, 8)
            dve.wait_ge(d2_done, NF1)
            for sb in range(NSB):
                nc.vector.tensor_tensor(hsel[:, sb, :], PS[:, 2 + sb, :], hsel[:, sb, :], ALU.add).then_inc(gate_seq, 1)
            for sb in range(NSB):
                dve.wait_ge(gate_seq, 9 + sb)
                nc.vector.scalar_tensor_tensor(fin[:, sb, :], hsel[:, sb, :], stat[:, 5, sb:sb + 1], outsel[:, sb, :],
                                               ALU.mult, ALU.add).then_inc(fin_ready, 1)


def kernel(**inputs):
    import numpy as np
    import concourse.bacc as bacc
    from concourse.bass_utils import run_bass_kernel_spmd

    nc = bacc.Bacc("TRN2", target_bir_lowering=False, num_devices=1, dynamic_dma_scratch_size=4096)
    con = np.ascontiguousarray

    def features_first(w):
        return con(np.asarray(w).reshape(w.shape[0], -1, P).transpose(2, 1, 0))

    arrays = {}
    arrays["xT"] = features_first(np.asarray(inputs["x"]).reshape(TOK, D))
    arrays["w0"] = np.stack([features_first(inputs[f"L0_cond_{n}"]) for n in ("Wq", "Wk", "Wv", "Wo")])
    pad = NBLK * P - INTER

    def in_blocks(w):
        w = np.pad(np.asarray(w), ((0, pad), (0, 0)))
        return w.reshape(NBLK, P, KD, P).transpose(0, 3, 2, 1).reshape(NBLK, P, D)

    gate, up = (in_blocks(inputs[f"L0_ffn_{n}_idx"]) for n in ("gate", "up"))
    down = np.pad(np.asarray(inputs["L0_ffn_down_idx"]).T, ((0, pad), (0, 0))).reshape(NBLK, P, D)
    both = np.concatenate([gate, up, down], axis=2).reshape(NBLK, P, 2, HALF)
    arrays["idx"] = con(both.transpose(0, 2, 1, 3).reshape(2 * NBLK, P, HALF))
    arrays["lut"] = con(np.broadcast_to(np.asarray(inputs["L0_ffn_lut"]), (P, LUTN)))
    arrays["cond"] = con(np.repeat(np.asarray(inputs["cond_1"]).reshape(B // 2, 2).T, S, axis=0))
    t = np.arange(S)
    below = np.where(t[None, :] <= t[:, None], 0.0, -3.0e38).astype(np.float32)
    arrays["causal"] = con(np.tile(below, (2, 4)))
    arrays["w1"] = features_first(inputs["L1_cond_W"])
    arrays["aT"] = features_first(np.asarray(inputs["L1_cond_A"]).reshape(NA * RANK, D))
    arrays["bmT"] = con(np.asarray(inputs["L1_cond_Bm"]).transpose(0, 2, 1).reshape(NA * RANK, D))
    arrays["tokens_adapter"] = con(np.broadcast_to(np.asarray(inputs["itok_B_0_6"]), (P, B)))
    arrays["adapter_of_row"] = np.repeat(np.arange(NA, dtype=np.float32), RANK)[:, None]
    arrays["scalings"] = con(np.repeat(np.asarray(inputs["L1_cond_scalings"]), RANK)[:, None])
    arrays["router"] = con(np.broadcast_to(np.asarray(inputs["L1_ffn_w_router"]), (P, D)))
    n = np.arange(1, TOPK + 1, dtype=np.float32)
    none = -np.ones(TOPK, np.float32)
    arrays["slots"] = np.repeat(np.stack([np.concatenate([n, none]), np.concatenate([none, n])]), S, axis=0)
    inv = np.float32(1.0) / np.float32(10000.0) ** (np.arange(0, HD, 2, dtype=np.float32) / np.float32(HD))
    angle = np.tile(t.astype(np.float32), 2)[:, None] * inv
    arrays["rope"] = np.concatenate([np.cos(angle), -np.sin(angle), np.sin(angle),
                                     np.arange(P, dtype=np.float32)[:, None]], axis=1).astype(np.float32)
    t = np.arange(P)
    below = np.where(t[None, :] <= t[:, None], 0.0, -3.0e38).astype(np.float32)
    arrays["causal2"] = con(np.concatenate([below, np.zeros((P, P), np.float32), below], axis=1))
    sel = np.arange(SEL).reshape(NSB, P).T
    arrays["pair_base"] = con((sel // (2 * TOPK) * P).astype(np.float32))
    arrays["ln"] = con(np.stack([np.asarray(inputs[f"L1_ffn_ln{n}_w"]).reshape(KD, P).T for n in (1, 2)], axis=1))

    def rows_first(w):
        return con(np.asarray(w).reshape(-1, P, w.shape[1]).transpose(1, 0, 2))

    for name, key in (("wq", "wq"), ("wk", "wk"), ("wv", "wv"), ("wo", "wo"), ("wgate", "w_gate"), ("wup", "w_up"),
                      ("wdown", "w_down")):
        arrays[name] = rows_first(inputs[f"L1_ffn_{key}"])
    arrays["bias"] = con(np.broadcast_to(np.concatenate([np.asarray(inputs[f"L1_ffn_{n}"]) for n in ("bq", "bk", "bv")]),
                                         (P, (NHQ + 2 * NHKV) * HD)))
    aps = {n: nc.dram_tensor(f"in_{n}", a.shape, mybir.dt.from_np(a.dtype), kind="ExternalInput").ap()
           for n, a in arrays.items()}
    y_dram = nc.dram_tensor("y_dram", (P, KD, TOK), F32, kind="Internal").ap()
    h_dram = nc.dram_tensor("h_dram", (TOK, D), F32, kind="Internal").ap()
    out = nc.dram_tensor("out_rows", (TOK, D), F32, kind="ExternalOutput").ap()
    adaln_ffn_kernel(nc, y_dram=y_dram, h_dram=h_dram, out=out, **aps)
    r = run_bass_kernel_spmd(nc, [{f"in_{n}": a for n, a in arrays.items()}], core_ids=[0])
    return r.results[0]["out_rows"].reshape(B, S, D)
```

```python
import concourse.bass as bass
from concourse import mybir
from contextlib import ExitStack

F32 = mybir.dt.float32
F32R = mybir.dt.float32r
BF16 = mybir.dt.bfloat16
I32 = mybir.dt.int32
ALU = mybir.AluOpType
ACT = mybir.ActivationFunctionType
AX = mybir.AxisListType.X

P = 128
B, S, D = 32, 64, 512
KD = D // P
TOK = B * S
INTER = 1376
NBLK = -(-INTER // P)
LAST = INTER - (NBLK - 1) * P
NH0, HD0 = 16, 32
CA = 256
NCA = TOK // CA
BC = CA // S
NP_ = BC // 2
CF = 512
NCF = TOK // CF
BLKW = 3 * D
HALF = BLKW // 2
LUTN = 16
GROUPS = [(0, 4), (4, 3), (7, 2), (9, 2)]
PASSES = [(0, 0), (0, 1), (1, 0)]


NPAIR = B // 2
NA, RANK = 8, 16
TOPK = 8
SEL = B * TOPK
NSB = SEL // P
NHQ, NHKV, HD = 16, 8, 128
HG = 2
I1 = 2048
NF1 = I1 // P
EPS = 1e-6
ROPE_W = HD // 2
TABW = 3 * ROPE_W + 1


def adaln_ffn_kernel(nc, xT, w0, idx, lut, cond, causal, w1, aT, bmT, tokens_adapter, adapter_of_row, scalings,
                     router, slots, rope, causal2, pair_base, ln, wq, wk, wv, bias, wo, wgate, wup, wdown,
                     y_dram, h_dram, out):
    ctx = ExitStack()
    with ctx:
        base = [-(-nc.sbuf_base // 64) * 64]
        start = base[0]

        def at(name, offset, shape, dt):
            return nc.alloc_sbuf_tensor_at(name, [P] + shape, dt, offset=start + offset)

        def sem(name):
            return ctx.enter_context(nc.semaphore(name))

        ident = at("ident", 0, [P], F32)
        mask = at("mask", 512, [4 * S], F32)
        beta = at("beta", 1536, [B // 2], F32)
        lut_sb = at("lut_sb", 1600, [LUTN], F32)
        rowmax = at("rowmax", 1664, [NP_, NH0], F32)
        rowsum = at("rowsum", 1792, [NP_, NH0], F32)
        rowinv = at("rowinv", 1920, [NP_, NH0], F32)
        K1 = 2048
        SLOT = BLKW * 4
        wtabA = [at(f"wtabA{i}", K1 + 4 * SLOT * i, [4 * BLKW], F32R) for i in range(2)]
        wsumA = at("wsumA", K1 + 4 * SLOT, [4 * BLKW], F32)
        K2 = K1 + 8 * SLOT
        idx_raw = at("idx_raw", K2, [HALF], I32)
        idx_bf = at("idx_bf", K2 + 4 * HALF, [HALF], BF16)
        onehot = at("onehot", K2 + 6 * HALF, [3, HALF], BF16)
        K3 = K2 + 16 * HALF
        w_raw = [at(f"w_raw{n}", K1 + 4 * SLOT * (n // 2) + SLOT + 8192 * (n % 2), [KD, D], F32) for n in range(4)]
        o = K3
        w_sb = []
        for n in range(3):
            w_sb.append([at(f"w_sb{n}_{i}", o + 8192 * i, [KD, D], F32R) for i in range(2)])
            o += 16384
        xr = at("xr", o, [KD, CA], F32); o += 4096
        xs = [at(f"xs{i}", o + 4096 * i, [KD, CA], F32R) for i in range(2)]; o += 8192
        qT = at("qT", o, [KD, CA], F32); o += 4096
        w_sb.append([at(f"w_sb3_{i}", o + 8192 * i, [KD, D], F32R) for i in range(2)]); o += 16384
        yc = at("yc", o, [KD, CA], F32); o += 4096
        kbd = at("kbd", o, [KD, BC, 4 * S], F32); o += 16384
        vbd = at("vbd", o, [BC, NH0 // 2, 2 * HD0], F32); o += 8192
        prob = at("prob", o, [NP_, NH0, S], F32); o += 8192
        probT = at("probT", o, [NP_, NH0 // 2, P], F32); o += 8192
        oN = at("oN", o, [NP_, D], F32); o += 4096
        oT = [at(f"oT{i}", o + 4096 * i, [KD, CA], F32R) for i in range(2)]; o += 8192
        o = K3
        y_raw = at("y_raw", o, [KD, TOK], F32)
        ys = [at("ys1", o, [KD, TOK], F32R)]; o += 32768
        ys.insert(0, at("ys0", o, [KD, TOK], F32R)); o += 32768
        x1 = at("x1", o, [KD, TOK], F32); o += 32768
        wtabB = [at(f"wtabB{i}", o + 2 * SLOT * i, [2 * BLKW], F32R) for i in range(2)]
        wsumB = at("wsumB", o + 2 * SLOT, [2 * BLKW], F32); o += 4 * SLOT
        sg = at("sg", o, [2, CF], F32); o += 4096
        hf = at("hf", o, [2, CF], F32); o += 4096
        hs = [at(f"hs{i}", o + 4096 * i, [2, CF], F32R) for i in range(2)]; o += 8192
        wtabC = [at(f"wtabC{i}", o + SLOT * i, [BLKW], F32R) for i in range(2)]
        wsumC = at("wsumC", o + SLOT, [BLKW], F32); o += 2 * SLOT
        small = o
        o += 8192
        assert start + o <= nc.sbuf_usable_end, (start + o, nc.sbuf_usable_end)

        def little(name, shape, dt=F32):
            nonlocal small
            n = 1
            for x in shape:
                n *= x
            t = at(name, small, shape, dt)
            small += -(-4 * n // 32) * 32
            return t

        router_sb = little("router_sb", [D])
        slots_sb = little("slots_sb", [2 * TOPK])
        rope_sb = little("rope_sb", [TABW])
        mask2 = little("mask2", [3 * P])
        pair_sb = little("pair_sb", [NSB])
        ln_sb = little("ln_sb", [2, KD])
        tok_ad = little("tok_ad", [B], I32)
        tok_adf = little("tok_adf", [B])
        row_ad = little("row_ad", [1])
        scal_sb = little("scal_sb", [1])
        admask = little("admask", [B])
        score = little("score", [NPAIR])
        scoreT = little("scoreT", [P])
        replaced = little("replaced", [P])
        best = little("best", [2, TOPK])
        picked = little("picked", [P])
        rank = little("rank", [P])
        onesr = little("onesr", [S])
        rankT = little("rankT", [NPAIR])
        rowidx = little("rowidx", [NSB], I32)
        stat = little("stat", [8, NSB])
        assert small <= o

        AW, AI, AY, AX1, AB, AS = K1, K2, K3, K3 + 65536, K3 + 98304, K3 + 98304 + 6 * SLOT
        AC, AT = AB + 4 * SLOT + 16384, AB + 4 * SLOT
        w1_raw = at("w1_raw", AB, [KD, D], F32)
        w1_sb = [at(f"w1_sb{i}", AB + 8192 + 8192 * i, [KD, D], F32R) for i in range(2)]
        a_raw = at("a_raw", AC, [KD, P], F32)
        a_sb = [at(f"a_sb{i}", AC + 2048 + 2048 * i, [KD, P], F32R) for i in range(2)]
        b_raw = at("b_raw", AC + 6144, [D], F32)
        b_sb = [at(f"b_sb{i}", AC + 8192 + 2048 * i, [D], F32R) for i in range(2)]
        x1s = [[at(f"x1s{i}_0", (AI, AW)[i], [KD, CF], F32R), at(f"x1s{i}_1", AY + 16384 + 8192 * i, [KD, CF], F32R)]
               for i in range(2)]
        h_tile = at("h_tile", AT, [2, D], F32)
        out_tile = at("out_tile", AT + 4096, [2, D], F32)
        xa = at("xa", AT + 8192, [CF], F32)
        xas = [at(f"xas{i}", AT + 10240 + 2048 * i, [CF], F32R) for i in range(2)]
        prod = at("prod", AT + 14336, [D], F32)
        wq_sb = at("wq_sb", AW, [KD, NHQ * HD], F32)
        wk_sb = at("wk_sb", AW + 32768, [KD, NHKV * HD], F32)
        wv_sb = at("wv_sb", AY + 49152, [KD, NHKV * HD], F32)
        wo_sb = at("wo_sb", AX1, [NHQ, D], F32)
        wd_sb = at("wd_sb", AB, [NF1, D], F32)
        bias_sb = at("bias_sb", AS, [(NHQ + 2 * NHKV) * HD], F32)
        qT2 = at("qT2", AY, [NHQ, SEL], F32)
        kT2 = at("kT2", AY + 16384, [NHKV, SEL], F32)
        v2 = at("v2", AB + 24576, [NSB, NHKV * HD], F32)
        hsel = at("hsel", AY + 32768, [NSB, D], F32)
        outsel = at("outsel", AY + 36864, [NSB, D], F32)
        hT = at("hT", AY + 40960, [KD, SEL], F32)
        xres = at("xres", AY + 45056, [NSB, D], F32)
        biased = at("biased", AI, [1, D], F32)
        times_cos = at("times_cos", AI + 4096, [D], F32)
        times_sin = at("times_sin", AI + 6144, [D], F32)
        turned = at("turned", AI + 8192, [D], F32)
        tables = at("tables", AI + 10240, [NSB, TABW], F32)
        pick = at("pick", AB + 32768, [NPAIR, 2 * TOPK], F32)
        scratch = at("scratch", AB + 33792, [D], F32)
        prob2 = at("prob2", AW, [4, HG, 3 * P], F32)
        prob2T = at("prob2T", AW + 12288, [4, 3 * P], F32)
        outs = [at(f"outs{i}", AW + 24576 + 2048 * i, [2, SEL], F32R) for i in range(2)]
        wos = [at(f"wos{i}", AW + 28672 + 4096 * i, [2, D], F32R) for i in range(2)]
        negmax2 = at("negmax2", AW + 40960, [4, HG, NSB], F32)
        rowsum2 = at("rowsum2", AW + 41088, [4, HG, NSB], F32)
        h2s = [at("h2s0", AW + 45056, [KD, SEL], F32R), at("h2s1", AI + 4096, [KD, SEL], F32R)]
        wg_sb = [at("wg_sb0", AY + 49152, [KD // 2, I1], F32), at("wg_sb1", AS, [KD // 2, I1], F32)]
        wu_sb = at("wu_sb", AY, [KD, I1], F32)
        gus = [at(f"gus{i}", AW + 8192 * i, [2, 2 * KD, P], F32R) for i in range(2)]
        wds = [at(f"wds{i}", AW + 16384 + 4096 * i, [2, D], F32R) for i in range(2)]
        sg1 = at("sg1", AW + 41472, [2, SEL], F32)
        inner = at("inner", AI + 8192, [2, SEL], F32)
        inner_s = [at("inner_s0", AI + 10240, [2, SEL], F32R), at("inner_s1", AW + 24576, [2, SEL], F32R)]
        fin = at("fin", AI, [NSB, D], F32)

        turned_b = at("turned_b", AI + 2048, [D], F32)
        hsel_normed = at("hsel_normed", AI, [NSB, D], F32)

        def turned_of(m):
            return turned[:, :] if m % 2 else turned_b[:, :]

        PS = ctx.enter_context(nc.psum_tensor("PS", [P, 8, 512], F32))

        def wtab(blk, part):
            if blk == GROUPS[1][0]:
                return wtabC[part][:, :]
            if blk < GROUPS[2][0] and blk > GROUPS[1][0]:
                s = blk - GROUPS[1][0] - 1
                return wtabB[part][:, s * BLKW:(s + 1) * BLKW]
            s = blk if blk < GROUPS[1][0] else blk - GROUPS[2][0]
            return wtabA[part][:, s * BLKW:(s + 1) * BLKW]

        def half_block(g, h):
            if g == 1 and h // 2 == GROUPS[1][0]:
                hi, lo, whole = wtabC + [wsumC]
                first = GROUPS[1][0]
            elif g == 1:
                hi, lo, whole = wtabB + [wsumB]
                first = GROUPS[1][0] + 1
            else:
                hi, lo, whole = wtabA + [wsumA]
                first = GROUPS[2][0] if g else 0
            return [t[:, bass.ds(HALF * (h - 2 * first), HALF)] for t in (hi, lo, whole)]

        consts_in = sem("consts_in")
        lut_in = sem("lut_in")
        ident_made = sem("ident_made")
        zeroed = sem("zeroed")
        beta_ready = sem("beta_ready")
        w_in = [sem(f"w_in{n}") for n in range(4)]
        w_hi = sem("w_hi")
        w_lo = sem("w_lo")
        x_in = sem("x_in")
        x_hi = sem("x_hi")
        x_lo = sem("x_lo")
        q_done = sem("q_done")
        k_done = sem("k_done")
        v_done = sem("v_done")
        q_copied = sem("q_copied")
        k_copied = sem("k_copied")
        v_copied = sem("v_copied")
        s_done = sem("s_done")
        shifted = sem("shifted")
        exped = sem("exped")
        pt_done = sem("pt_done")
        pt_copied = sem("pt_copied")
        pv_done = sem("pv_done")
        o_normed = sem("o_normed")
        ot_done = sem("ot_done")
        ot_hi = sem("ot_hi")
        ot_lo = sem("ot_lo")
        wo_done = sem("wo_done")
        y_copied = sem("y_copied")
        y_stored = sem("y_stored")
        soft = sem("soft")
        idx_in = sem("idx_in")
        idx_conv = sem("idx_conv")
        lut_seq = sem("lut_seq")
        tab_hi = sem("tab_hi")
        tab_ready = sem("tab_ready")
        y_in = [sem(f"y_in{c}") for c in range(NCF)]
        x1_in = sem("x1_in")
        y_hi = sem("y_hi")
        y_lo = sem("y_lo")
        gu_done = sem("gu_done")
        silu_done = sem("silu_done")
        mul_done = sem("mul_done")
        h_hi = sem("h_hi")
        h_lo = sem("h_lo")
        d_done = sem("d_done")
        acc_added = sem("acc_added")
        small_in = sem("small_in")
        w1_in = sem("w1_in")
        w1_hi = sem("w1_hi")
        w1_lo = sem("w1_lo")
        admask_made = sem("admask_made")
        x1_hi = sem("x1_hi")
        x1_lo = sem("x1_lo")
        xa_done = sem("xa_done")
        xa_masked = sem("xa_masked")
        xa_hi = sem("xa_hi")
        xa_lo = sem("xa_lo")
        h_done = sem("h_done")
        xn_done = sem("xn_done")
        h_copied = sem("h_copied")
        scored = sem("scored")
        out_added = sem("out_added")
        h_stored = [sem(f"h_stored{i}") for i in range(2)]
        out_stored = [sem(f"out_stored{i}") for i in range(2)]
        top = sem("top")
        top_pe = sem("top_pe")
        rows_ready = sem("rows_ready")
        sel_in = sem("sel_in")
        outsel_in = sem("outsel_in")
        qkv_in = sem("qkv_in")
        wo_in = sem("wo_in")
        wd_in = sem("wd_in")
        wd_late_in = sem("wd_late_in")
        bias_in = sem("bias_in")
        wg_in = sem("wg_in")
        wu_in = sem("wu_in")
        norm = sem("norm")
        root = sem("root")
        normed = sem("normed")
        ht_done = sem("ht_done")
        ht_copied = sem("ht_copied")
        qkv_done = sem("qkv_done")
        qkv_read = sem("qkv_read")
        rope_seq = sem("rope_seq")
        roped = sem("roped")
        rt_done = sem("rt_done")
        rt_copied = sem("rt_copied")
        s2_done = sem("s2_done")
        s2_masked = sem("s2_masked")
        s2_max = sem("s2_max")
        s2_exp = sem("s2_exp")
        s2_inv = sem("s2_inv")
        s2_norm = sem("s2_norm")
        p2t_done = sem("p2t_done")
        p2t_copied = sem("p2t_copied")
        pv2_done = sem("pv2_done")
        out2_hi = sem("out2_hi")
        out2_lo = sem("out2_lo")
        wo2_hi = sem("wo2_hi")
        wo2_lo = sem("wo2_lo")
        wo2_done = sem("wo2_done")
        g2_done = sem("g2_done")
        silu2 = sem("silu2")
        mul2 = sem("mul2")
        d2_done = sem("d2_done")
        h2_lo = sem("h2_lo")
        gu_hi = sem("gu_hi")
        gu_lo = sem("gu_lo")
        wd_hi = sem("wd_hi")
        wd_lo = sem("wd_lo")
        inner_hi = sem("inner_hi")
        inner_lo = sem("inner_lo")
        gate_seq = sem("gate_seq")
        gate_exp = sem("gate_exp")
        fin_ready = sem("fin_ready")
        scattered = sem("scattered")

        block = ctx.enter_context(nc.Block())

        NT = CF // P
        group_step = [sum(n for _, n in GROUPS[:g]) * NCF for g in range(len(GROUPS) + 1)]

        def steps_before(g, f, c):
            s = group_step[g] + GROUPS[g][1] * c + f
            first_chunk = isinstance(c, int) and c == 0
            blocks_before = GROUPS[g - 1][1] if first_chunk else GROUPS[g][1]
            return s if f == 0 and blocks_before % 2 else s - 1

        LUT_OPS = 2 * LUTN - 1

        first_parts = []
        for h in range(NCA + 1, 2 * GROUPS[2][0]):
            cuts = [0, 4, 8, 12, 16] if h == NCA + 1 else [0, 6, 11, 16]
            first_parts += [(h, a, b) for a, b in zip(cuts, cuts[1:])]
        assert len(first_parts) == GROUPS[0][1] * NCF
        ends_at = {n: (1, h) for n, (h, _, b) in enumerate(first_parts) if b == LUTN}
        ends_at[-1] = (1, NCA)
        last_before = [None, ends_at[GROUPS[0][1] * NCF - 1]] + \
            [(g, 2 * GROUPS[g][0] + NCF - 1) for g in range(2, len(GROUPS))]
        last_half = last_before[-1][1]

        @block.sync
        def _(sp):
            sp.dma_start(lut_sb[:, :], lut).then_inc(lut_in, 16)
            sp.dma_start(idx_raw[:, :], idx[0]).then_inc(idx_in, 16)
            for n in (1, 0, 2, 3):
                sp.dma_start(w_raw[n][:, :, :], w0[n]).then_inc(w_in[n], 16)
                if n == 1:
                    sp.dma_start(xr[:, :, :], xT[:, :, 0:CA]).then_inc(x_in, 16)
                    sp.dma_start(beta[:, :], cond).then_inc(consts_in, 16)
                    sp.dma_start(mask[:, :], causal).then_inc(consts_in, 16)
            sp.wait_ge(x_hi, 1)
            sp.wait_ge(x_lo, 1)
            sp.dma_start(xr[:, :, :], xT[:, :, CA:2 * CA]).then_inc(x_in, 16)

            def load_idx(h):
                sp.wait_ge(idx_conv, h)
                sp.dma_start(idx_raw[:, :], idx[bass.ds(h, 1)].rearrange("a p n -> (a p) n")).then_inc(idx_in, 16)

            def load_x(c):
                sp.wait_ge(x_hi, c)
                sp.wait_ge(x_lo, c)
                sp.dma_start(xr[:, :, :], xT[:, :, bass.ds(c * CA, CA)]).then_inc(x_in, 16)

            def store_y(c):
                sp.wait_ge(y_copied, 2 * c + 2)
                sp.dma_start(y_dram[:, :, bass.ds(c * CA, CA)], yc[:, :, :]).then_inc(y_stored, 16)

            load_idx(1)
            load_x(2)
            load_idx(2)
            with sp.Fori(1, NCA - 2) as i:
                load_x(i + 2)
                load_idx(i + 2)
                store_y(i - 1)
            load_idx(NCA)
            store_y(NCA - 3)
            load_idx(NCA + 1)

            def load_y(c):
                sp.wait_ge(y_stored, 16 * (c + 1) * CF // CA)
                sp.dma_start(y_raw[:, :, c * CF:(c + 1) * CF], y_dram[:, :, c * CF:(c + 1) * CF]).then_inc(y_in[c], 16)

            sp.wait_ge(s_done, NCA)
            for c in range(NCF - 1):
                load_y(c)
            store_y(NCA - 2)
            store_y(NCA - 1)
            load_y(NCF - 1)
            sp.dma_start(x1[:, :, :], xT).then_inc(x1_in, 16)
            with sp.Fori(NCA + 2, 2 * NBLK) as h:
                load_idx(h)
            for dst, src in ((router_sb, router), (slots_sb, slots), (rope_sb, rope), (mask2, causal2), (pair_sb, pair_base),
                             (tok_ad, tokens_adapter), (row_ad, adapter_of_row), (scal_sb, scalings)):
                sp.dma_start(dst[:, :], src).then_inc(small_in, 16)
            sp.dma_start(ln_sb[:, :, :], ln).then_inc(small_in, 16)
            sp.wait_ge(d_done, group_step[2])
            sp.dma_start(w1_raw[:, :, :], w1).then_inc(w1_in, 16)
            sp.dma_start(a_raw[:, :, :], aT).then_inc(w1_in, 16)
            sp.dma_start(b_raw[:, :], bmT).then_inc(w1_in, 16)
            sp.wait_ge(d_done, group_step[-1])
            sp.dma_start(wq_sb[:, 1:KD, :], wq[:, 1:KD, :]).then_inc(qkv_in, 16)
            sp.dma_start(wk_sb[:, :, :], wk).then_inc(qkv_in, 16)
            sp.dma_start(wv_sb[:, :, :], wv).then_inc(qkv_in, 16)

            def tile_rows(dram, n):
                return dram.rearrange("(n p) d -> n p d", p=P)[bass.ds(n, 1)].rearrange("a p d -> (a p) d")

            with sp.Fori(0, NCF) as c:
                for t in range(NT):
                    n = NT * c + t
                    sp.wait_ge(h_copied, n + 1)
                    sp.dma_start(tile_rows(h_dram, n), h_tile[:, t % 2, :]).then_inc(h_stored[t % 2], 16)
                    sp.wait_ge(out_added, n + 1)
                    sp.dma_start(tile_rows(out, n), out_tile[:, t % 2, :]).then_inc(out_stored[t % 2], 16)

            sp.wait_ge(h_done, NT * (NCF - 1))
            sp.dma_start(wq_sb[:, 0:1, :], wq[:, 0:1, :]).then_inc(qkv_in, 16)
            sp.wait_ge(h_done, NPAIR)
            sp.wait_ge(xn_done, NPAIR)
            for i in range(2):
                sp.wait_ge(h_stored[i], 16 * NPAIR // 2)
                sp.wait_ge(out_stored[i], 16 * NPAIR // 2)
            sp.wait_ge(scored, NPAIR)
            sp.dma_start(bias_sb[:, :], bias).then_inc(bias_in, 16)
            sp.wait_ge(sel_in, 16 * NSB)
            sp.dma_start(wo_sb[:, :, :], wo).then_inc(wo_in, 16)
            WD_EARLY = NF1 - 4
            sp.dma_start(wd_sb[:, 0:WD_EARLY, :], wdown[:, 0:WD_EARLY, :]).then_inc(wd_in, 16)
            sp.wait_ge(qkv_done, 16)
            sp.dma_start(wg_sb[0][:, :, :], wgate[:, 0:2, :]).then_inc(wg_in, 16)
            sp.wait_ge(qkv_read, 16)
            sp.dma_start(wg_sb[1][:, :, :], wgate[:, 2:4, :]).then_inc(wg_in, 16)
            sp.wait_ge(s2_done, NHQ // HG // 2)
            for k in (0, 3):
                sp.dma_start(wu_sb[:, k:k + 1, :], wup[:, k:k + 1, :]).then_inc(wu_in, 16)
            sp.wait_ge(s2_done, NHQ // HG)
            for k in (1, 2):
                sp.dma_start(wu_sb[:, k:k + 1, :], wup[:, k:k + 1, :]).then_inc(wu_in, 16)
            sp.wait_ge(pv2_done, NHQ)
            sp.dma_start(wd_sb[:, WD_EARLY:NF1, :], wdown[:, WD_EARLY:NF1, :]).then_inc(wd_late_in, 16)

        @block.gpsimd
        def _(pool):
            nc.gpsimd.memset(ident[:, :], 0.0).then_inc(ident_made, 1)
            pool.wait_ge(ident_made, 1)
            nc.gpsimd.affine_select(out=ident[:, :], in_=ident[:, :], compare_op=ALU.not_equal, fill=1.0,
                                    base=0, pattern=[[-1, P]], channel_multiplier=1).then_inc(ident_made, 1)
            nc.gpsimd.memset(kbd[:, :, :, :], 0.0).then_inc(zeroed, 1)
            nc.gpsimd.memset(vbd[:, :, :, :], 0.0).then_inc(zeroed, 1)
            nc.gpsimd.memset(onesr[:, :], 1.0).then_inc(zeroed, 1)

            pool.wait_ge(rows_ready, 1)
            for i in range(2):
                pool.wait_ge(h_stored[i], 16 * NPAIR // 2)
                pool.wait_ge(out_stored[i], 16 * NPAIR // 2)
            pool.wait_ge(h_done, NPAIR)
            pool.wait_ge(xn_done, NPAIR)
            for sb in range(NSB):
                nc.gpsimd.indirect_dma_start(out=hsel[:, sb, :], out_offset=None, in_=h_dram[:, :],
                                             in_offset=bass.IndirectOffsetOnAxis(ap=rowidx[:, sb:sb + 1], axis=0)
                                             ).then_inc(sel_in, 16)
            for sb in range(NSB):
                nc.gpsimd.indirect_dma_start(out=outsel[:, sb, :], out_offset=None, in_=out[:, :],
                                             in_offset=bass.IndirectOffsetOnAxis(ap=rowidx[:, sb:sb + 1], axis=0)
                                             ).then_inc(outsel_in, 16)
            for sb in range(NSB):
                pool.wait_ge(fin_ready, sb + 1)
                nc.gpsimd.indirect_dma_start(out=out[:, :],
                                             out_offset=bass.IndirectOffsetOnAxis(ap=rowidx[:, sb:sb + 1], axis=0),
                                             in_=fin[:, sb, :], in_offset=None).then_inc(scattered, 16)
            pool.wait_ge(scattered, 16 * NSB)

        @block.tensor
        def _(pe):
            def project(w, bank0, done):
                for e in range(KD):
                    out = PS[:, bank0 + e // 2, (e % 2) * CA:(e % 2 + 1) * CA]
                    n = 0
                    for k in range(KD):
                        for a, b in PASSES:
                            mm = nc.tensor.matmul(out, w_sb[w][a][:, k, e * P:(e + 1) * P], xs[b][:, k, :],
                                                  start=(n == 0), stop=(n == 3 * KD - 1))
                            n += 1
                    if e % 2:
                        mm.then_inc(done, 1)

            def keys(c):
                pe.wait_ge(x_hi, c + 1)
                pe.wait_ge(x_lo, c + 1)
                project(1, 6, k_done)

            def queries(c):
                pe.wait_ge(k_copied, 2 * c + 2)
                project(0, 6, q_done)

            def values(c):
                for t in range(NP_):
                    n = 0
                    for k in range(KD):
                        for a, b in PASSES:
                            mm = nc.tensor.matmul(PS[:, 4 + t, :], xs[a][:, k, t * P:(t + 1) * P], w_sb[2][b][:, k, :],
                                                  start=(n == 0), stop=(n == 3 * KD - 1))
                            n += 1
                    mm.then_inc(v_done, 1)

            def scores(c):
                pe.wait_ge(q_copied, 2 * c + 2)
                pe.wait_ge(k_copied, 2 * c + 2)
                for e in range(KD):
                    for b in range(BC):
                        j, t = b % 2, b // 2
                        mm = nc.tensor.matmul(PS[64 * j:64 * j + 64, e, t * 256:(t + 1) * 256],
                                              qT[:, e, b * S:(b + 1) * S], kbd[:, e, b, :], start=True, stop=True,
                                              skip_group_check=True)
                mm.then_inc(s_done, 1)

            def prob_transposes(c):
                for t in range(NP_):
                    pe.wait_ge(exped, 2 * c + t + 1)
                    for m in range(NH0 // 2):
                        mm = nc.tensor.transpose(PS[:, 2 * t + m // 4, (m % 4) * P:(m % 4 + 1) * P],
                                                 prob[:, t, 2 * m:2 * m + 2, :].rearrange("p a b -> p (a b)"),
                                                 ident[:, :])
                    mm.then_inc(pt_done, 1)

            def attend(c):
                pe.wait_ge(q_copied, 2 * min_next(c) + 2)
                pe.wait_ge(v_copied, 2 * c + 2)
                for t in range(NP_):
                    pe.wait_ge(pt_copied, 2 * c + t + 1)
                    for j in range(2):
                        for m in range(NH0 // 2):
                            mm = nc.tensor.matmul(PS[64 * j:64 * j + 64, 6 + t, m * 64:(m + 1) * 64],
                                                  probT[:, t, m, 64 * j:64 * j + 64], vbd[:, 2 * t + j, m, :],
                                                  start=True, stop=True, skip_group_check=True)
                    mm.then_inc(pv_done, 1)

            def out_transposes(c):
                if not (isinstance(c, int) and c == NCA - 1):
                    pe.wait_ge(v_copied, 2 * c + 4)
                for t in range(NP_):
                    pe.wait_ge(o_normed, 2 * c + t + 1)
                    for e in range(KD):
                        mm = nc.tensor.transpose(PS[:, 4 + t, e * P:(e + 1) * P], oN[:, t, e * P:(e + 1) * P], ident[:, :])
                    mm.then_inc(ot_done, 1)

            def out_project(c):
                pe.wait_ge(ot_hi, 2 * c + 2)
                pe.wait_ge(ot_lo, 2 * c + 2)
                for e in range(KD):
                    out = PS[:, 4 + e // 2, (e % 2) * CA:(e % 2 + 1) * CA]
                    n = 0
                    for k in range(KD):
                        for a, b in PASSES:
                            mm = nc.tensor.matmul(out, w_sb[3][a][:, k, e * P:(e + 1) * P], oT[b][:, k, :],
                                                  start=(n == 0), stop=(n == 3 * KD - 1))
                            n += 1
                    if e % 2:
                        mm.then_inc(wo_done, 1)

            def min_next(c):
                return c + 1 if not isinstance(c, int) else min(c + 1, NCA - 1)

            def turn(i, first=False, last=False):
                scores(i)
                if not first:
                    out_transposes(i - 1)
                if not last:
                    keys(i + 1)
                if not first:
                    out_project(i - 1)
                if not last:
                    queries(i + 1)
                prob_transposes(i)
                if not last:
                    if not first:
                        pe.wait_ge(y_copied, 2 * i)
                    values(i + 1)
                attend(i)

            pe.wait_ge(w_hi, 1)
            pe.wait_ge(w_lo, 1)
            pe.wait_ge(ident_made, 2)
            keys(0)
            pe.wait_ge(w_hi, 2)
            pe.wait_ge(w_lo, 2)
            queries(0)
            pe.wait_ge(w_hi, 3)
            pe.wait_ge(w_lo, 3)
            values(0)
            pe.wait_ge(w_hi, 4)
            pe.wait_ge(w_lo, 4)
            pe.wait_ge(v_copied, 2)
            turn(0, first=True)
            with pe.Fori(1, NCA - 1) as i:
                turn(i)
            turn(NCA - 1, last=True)
            out_transposes(NCA - 1)
            out_project(NCA - 1)

            pe.wait_ge(y_copied, 2 * NCA)

            def gate_up(g, f, c):
                s = group_step[g] + GROUPS[g][1] * c + f
                blk = GROUPS[g][0] + f
                p = f % 2
                if not (isinstance(s, int) and s < 2):
                    pe.wait_ge(mul_done, steps_before(g, f, c))
                if g == 0 and f == 0:
                    pe.wait_ge(y_hi, c + 1)
                    pe.wait_ge(y_lo, c + 1)
                if isinstance(c, int) and c == 0:
                    pe.wait_ge(tab_ready, 2 * blk + 2)
                w = [wtab(blk, a) for a in range(2)]
                for q in range(2):
                    n = 0
                    for k in range(KD):
                        for a, b in PASSES:
                            mm = nc.tensor.matmul(PS[:, 4 + 2 * p + q, :], w[a][:, q * D + k * P:q * D + (k + 1) * P],
                                                  ys[b][:, k, bass.ds(c * CF, CF)],
                                                  start=(n == 0), stop=(n == 3 * KD - 1))
                            n += 1
                mm.then_inc(gu_done, 1)

            def down(g, f, c):
                s = group_step[g] + GROUPS[g][1] * c + f
                blk = GROUPS[g][0] + f
                rows = P if blk < NBLK - 1 else LAST
                p = f % 2
                pe.wait_ge(h_hi, s + 1)
                pe.wait_ge(h_lo, s + 1)
                if f == 0 and not (g == 0 and isinstance(c, int) and c == 0):
                    pe.wait_ge(acc_added, NCF * g + c)
                w = [wtab(blk, a) for a in range(2)]
                for d in range(KD):
                    for n, (a, b) in enumerate(PASSES):
                        mm = nc.tensor.matmul(PS[:, d, :], w[a][0:rows, 2 * D + d * P:2 * D + (d + 1) * P],
                                              hs[b][0:rows, p, :], start=(f == 0 and n == 0),
                                              stop=(f == GROUPS[g][1] - 1 and n == 2))
                mm.then_inc(d_done, 1)

            def ffn_chunk(g, c, before):
                for f in range(GROUPS[g][1]):
                    gate_up(g, f, c)
                    if f:
                        down(g, f - 1, c)
                    elif before is not None:
                        down(*before)

            before = None
            for g in range(len(GROUPS)):
                ffn_chunk(g, 0, before)
                with pe.Fori(1, NCF) as c:
                    ffn_chunk(g, c, (g, GROUPS[g][1] - 1, c - 1))
                before = (g, GROUPS[g][1] - 1, NCF - 1)
            down(*before)

            def linear_chunk(c):
                pe.wait_ge(x1_hi, c + 1)
                pe.wait_ge(x1_lo, c + 1)
                if c:
                    pe.wait_ge(xa_masked, c)
                n = 0
                for k in range(KD):
                    for a, b in PASSES:
                        mm = nc.tensor.matmul(PS[:, 4, :], a_sb[a][:, k, :], x1s[b][c % 2][:, k, :],
                                              start=(n == 0), stop=(n == 3 * KD - 1))
                        n += 1
                mm.then_inc(xa_done, 1)
                if c == 0:
                    pe.wait_ge(acc_added, NCF * len(GROUPS))
                for t in range(NT):
                    m = NT * c + t
                    if m >= 2:
                        pe.wait_ge(scored, m - 1)
                        pe.wait_ge(out_added, m - 1)
                    for k in range(KD):
                        mm = nc.tensor.transpose(PS[:, 2 + t % 2, k * P:(k + 1) * P], x1[:, k, c * CF + t * P:c * CF + (t + 1) * P],
                                                 ident[:, :])
                    mm.then_inc(xn_done, 1)
                    n = 0
                    for k in range(KD):
                        for a, b in PASSES:
                            nc.tensor.matmul(PS[:, t % 2, :], x1s[a][c % 2][:, k, t * P:(t + 1) * P], w1_sb[b][:, k, :],
                                             start=(n == 0), stop=False)
                            n += 1
                    if t == 0:
                        pe.wait_ge(xa_hi, c + 1)
                        pe.wait_ge(xa_lo, c + 1)
                    for n, (a, b) in enumerate(PASSES):
                        mm = nc.tensor.matmul(PS[:, t % 2, :], xas[a][:, t * P:(t + 1) * P], b_sb[b][:, :],
                                              start=False, stop=(n == 2))
                    mm.then_inc(h_done, 1)

            pe.wait_ge(w1_hi, 3)
            pe.wait_ge(w1_lo, 3)
            pe.wait_ge(mul_done, group_step[-1])
            for c in range(NCF):
                linear_chunk(c)

            pe.wait_ge(scored, NPAIR)
            nc.tensor.transpose(PS[0:NPAIR, 5, 0:P], score[:, :], ident[:, :]).then_inc(top_pe, 1)
            pe.wait_ge(top, 9)
            nc.tensor.transpose(PS[:, 6, 0:NPAIR], rank[0:NPAIR, :], ident[0:NPAIR, 0:NPAIR]).then_inc(top_pe, 1)
            pe.wait_ge(top, 11)
            for sb in range(NSB):
                mm = nc.tensor.matmul(PS[:, 7, sb * TABW:(sb + 1) * TABW],
                                      pick[:, 8 * sb:8 * sb + 8, :].rearrange("p a b -> p (a b)"), rope_sb[:, :],
                                      start=True, stop=True, skip_group_check=True)
            mm.then_inc(top_pe, 1)

            def rows_to_columns(src, bank):
                for sb in range(NSB):
                    for k in range(KD):
                        mm = nc.tensor.transpose(PS[:, bank + k // 2, (k % 2) * SEL + sb * P:(k % 2) * SEL + (sb + 1) * P],
                                                 src[:, sb, k * P:(k + 1) * P], ident[:, :])
                mm.then_inc(ht_done, 1)

            pe.wait_ge(out_added, NPAIR)
            pe.wait_ge(sel_in, 16 * NSB)
            rows_to_columns(hsel, 4)
            pe.wait_ge(ht_copied, KD)
            pe.wait_ge(qkv_in, 64)
            tiles = [(w, n) for w, n in ((wq_sb, 4), (wk_sb, 2), (wv_sb, 2))]
            m = 0

            def turn_tile(m):
                pe.wait_ge(roped, m + 1)
                if m >= 2:
                    pe.wait_ge(rt_copied, m - 1)
                for h in range(4):
                    mm = nc.tensor.transpose(PS[:, 6 + m % 2, h * P:(h + 1) * P], turned_of(m)[:, h * P:(h + 1) * P],
                                             ident[:, :])
                mm.then_inc(rt_done, 1)

            for w, count in tiles:
                for nt in range(count):
                    for sb in range(NSB):
                        if m >= 4:
                            pe.wait_ge(qkv_read, m - 3)
                        for k in range(KD):
                            mm = nc.tensor.matmul(PS[:, m % 4, :], hT[:, k, sb * P:(sb + 1) * P],
                                                  w[:, k, nt * 512:(nt + 1) * 512], start=(k == 0), stop=(k == KD - 1))
                        mm.then_inc(qkv_done, 1)
                        if 2 <= m < 14:
                            turn_tile(m - 2)
                        m += 1

            pe.wait_ge(rt_copied, 12)
            pe.wait_ge(qkv_read, 16)

            def scores2(g):
                if g >= 2:
                    pe.wait_ge(s2_masked, g - 1)
                for j in range(HG):
                    h, bank = HG * g + j, HG * (g % 2) + j
                    nc.tensor.matmul(PS[:, bank, 0:P], qT2[:, h, 0:P], kT2[:, h // 2, 0:P], start=True, stop=True,
                                     skip_group_check=True)
                    mm = nc.tensor.matmul(PS[:, bank, P:3 * P], qT2[:, h, P:SEL], kT2[:, h // 2, :], start=True,
                                          stop=True, skip_group_check=True)
                mm.then_inc(s2_done, 1)

            def transposes2(h):
                g = h // HG
                pe.wait_ge(s2_norm, 2 * g + 2)
                if h:
                    pe.wait_ge(p2t_copied, h)
                for n in range(3):
                    mm = nc.tensor.transpose(PS[:, 4, n * P:(n + 1) * P],
                                             prob2[:, g % 4, h % HG, n * P:(n + 1) * P], ident[:, :])
                mm.then_inc(p2t_done, 1)

            def values2(h):
                pe.wait_ge(p2t_copied, h + 1)
                if h:
                    pe.wait_ge(out2_lo, h)
                hv = slice((h // 2) * HD, (h // 2 + 1) * HD)
                nc.tensor.matmul(PS[:, 5, 0:SEL], v2[:, 0, hv], prob2T[:, h % 4, 0:SEL], start=True, stop=False)
                nc.tensor.matmul(PS[:, 5, P:SEL], v2[:, 1, hv], prob2T[:, h % 4, SEL:3 * P],
                                 start=False, stop=True).then_inc(pv2_done, 1)

            def out_project2(h):
                pe.wait_ge(out2_lo, h + 1)
                pe.wait_ge(wo2_lo, h + 1)
                for sb in range(NSB):
                    for n, (a, b) in enumerate(PASSES):
                        mm = nc.tensor.matmul(PS[:, 6 + sb, :], outs[a][:, h % 2, sb * P:(sb + 1) * P],
                                              wos[b][:, h % 2, :], start=(h == 0 and n == 0),
                                              stop=(h == NHQ - 1 and n == 2))
                mm.then_inc(wo2_done, 1)

            NG2 = NHQ // HG
            scores2(0)
            scores2(1)
            for g in range(NG2):
                if g + 2 < NG2:
                    scores2(g + 2)
                for h in range(HG * g, HG * g + HG):
                    transposes2(h)
                    if h >= 1:
                        values2(h - 1)
                    if h >= 2:
                        out_project2(h - 2)
            values2(NHQ - 1)
            out_project2(NHQ - 2)
            out_project2(NHQ - 1)

            pe.wait_ge(normed, 1)
            rows_to_columns(hsel_normed, 4)
            pe.wait_ge(ht_copied, 2 * KD)
            pe.wait_ge(h2_lo, KD)

            def gate_up2(f, u, first=False):
                if not first:
                    pe.wait_ge(mul2, f - 1)
                pe.wait_ge(gu_hi, f + 1)
                pe.wait_ge(gu_lo, f + 1)
                for q in range(2):
                    n = 0
                    for k in range(KD):
                        for a, b in PASSES:
                            mm = nc.tensor.matmul(PS[:, 4 + u, q * SEL:(q + 1) * SEL], gus[a][:, u, q * KD + k, :],
                                                  h2s[b][:, k, :], start=(n == 0), stop=(n == 3 * KD - 1))
                            n += 1
                mm.then_inc(g2_done, 1)

            def down2(f, u, first=False, last=False):
                pe.wait_ge(inner_hi, f + 1)
                pe.wait_ge(inner_lo, f + 1)
                pe.wait_ge(wd_hi, f + 1)
                pe.wait_ge(wd_lo, f + 1)
                for sb in range(NSB):
                    for n, (a, b) in enumerate(PASSES):
                        mm = nc.tensor.matmul(PS[:, 2 + sb, :], inner_s[a][:, u, sb * P:(sb + 1) * P], wds[b][:, u, :],
                                              start=(first and n == 0), stop=(last and n == 2))
                    if last or sb == NSB - 1:
                        mm.then_inc(d2_done, 1)

            def pair_of_blocks(pair, first=False, last=False):
                for u in range(2):
                    f = 2 * pair + u
                    if not (last and u):
                        gate_up2(f + 1, 1 - u, first=first and u == 0)
                    down2(f, u, first=first and u == 0, last=last and u == 1)

            gate_up2(0, 0, first=True)
            pair_of_blocks(0, first=True)
            with pe.Fori(1, NF1 // 2 - 1) as pair:
                pair_of_blocks(pair)
            pair_of_blocks(NF1 // 2 - 1, last=True)

        @block.scalar
        def _(act):
            act.wait_ge(idx_in, 16)
            nc.scalar.copy(idx_bf[:, :], idx_raw[:, :]).then_inc(idx_conv, 1)
            order = (1, 0, 2, 3)
            for m, n in enumerate(order):
                act.wait_ge(w_in[n], 16)
                nc.scalar.copy(w_sb[n][0][:, :, :], w_raw[n][:, :, :]).then_inc(w_hi, 1)
                if m == 0:
                    act.wait_ge(x_in, 16)
                    nc.scalar.copy(xs[0][:, :, :], xr[:, :, :]).then_inc(x_hi, 1)

            def next_indices(h):
                act.wait_ge(idx_in, 16 * (h + 1))
                nc.scalar.copy(idx_bf[:, :], idx_raw[:, :]).then_inc(idx_conv, 1)

            def table_high(g, h, more=True):
                act.wait_ge(lut_seq, LUT_OPS * (h + 1))
                hi, _, whole = half_block(g, h)
                nc.scalar.copy(hi, whole).then_inc(tab_hi, 1)
                if more:
                    next_indices(h + 1)

            def copy_keys(c, bank):
                act.wait_ge(k_done, 2 * c + bank + 1)
                for e in (2 * bank, 2 * bank + 1):
                    for h in range(4):
                        src = PS[32 * h:32 * h + 32, 6 + bank, (e % 2) * CA:(e % 2 + 1) * CA].rearrange("p (b t) -> p b t", b=BC)
                        ins = nc.scalar.copy(kbd[32 * h:32 * h + 32, e, :, h * S:(h + 1) * S], src)
                ins.then_inc(k_copied, 1)

            def copy_queries(c):
                for bank in range(2):
                    act.wait_ge(q_done, 2 * c + bank + 1)
                    nc.scalar.copy(qT[:, 2 * bank:2 * bank + 2, :].rearrange("p a b -> p (a b)"),
                                   PS[:, 6 + bank, :]).then_inc(q_copied, 1)

            def copy_values(c):
                for t in range(NP_):
                    act.wait_ge(v_done, 2 * c + t + 1)
                    for j in range(2):
                        for h in range(2):
                            src = PS[64 * j:64 * j + 64, 4 + t, :].rearrange("p (m h d) -> p m h d", h=2, d=HD0)[:, :, h, :]
                            ins = nc.scalar.copy(vbd[64 * h:64 * h + 64, 2 * t + j, :, h * HD0:(h + 1) * HD0], src)
                    ins.then_inc(v_copied, 1)

            def split_x(c):
                act.wait_ge(v_done, 2 * c)
                act.wait_ge(x_in, 16 * c + 16)
                nc.scalar.copy(xs[0][:, :, :], xr[:, :, :]).then_inc(x_hi, 1)

            def exps(c):
                for t in range(NP_):
                    act.wait_ge(shifted, 2 * c + t + 1)
                    pr = prob[:, t, :, :].rearrange("p a b -> p (a b)")
                    nc.scalar.activation(pr, pr, ACT.Exp).then_inc(exped, 1)

            def copy_prob(c):
                for t in range(NP_):
                    act.wait_ge(pt_done, 2 * c + t + 1)
                    nc.scalar.copy(probT[:, t, :, :].rearrange("p a b -> p (a b)"),
                                   PS[:, 2 * t:2 * t + 2, :].rearrange("p a b -> p (a b)")).then_inc(pt_copied, 1)

            def split_out(c):
                for t in range(NP_):
                    act.wait_ge(ot_done, 2 * c + t + 1)
                    nc.scalar.copy(oT[0][:, :, t * P:(t + 1) * P],
                                   PS[:, 4 + t, :].rearrange("p (e q) -> p e q", e=KD)).then_inc(ot_hi, 1)

            def copy_y(c, stored=True):
                if stored:
                    act.wait_ge(y_stored, 16 * c)
                for bank in range(2):
                    act.wait_ge(wo_done, 2 * c + bank + 1)
                    nc.scalar.copy(yc[:, 2 * bank:2 * bank + 2, :].rearrange("p a b -> p (a b)"),
                                   PS[:, 4 + bank, :]).then_inc(y_copied, 1)

            def turn(i, first=False, second=False, last=False, split=True):
                act.wait_ge(s_done, i + 1)
                if not first:
                    split_out(i - 1)
                if not last:
                    copy_keys(i + 1, 0)
                    copy_keys(i + 1, 1)
                exps(i)
                if not first:
                    copy_y(i - 1, stored=not second)
                if not last:
                    copy_queries(i + 1)
                copy_prob(i)
                if not last:
                    if split:
                        split_x(i + 2)
                    table_high(0, i + 1)
                    act.wait_ge(pv_done, 2 * i + 2)
                    copy_values(i + 1)

            act.wait_ge(zeroed, 2)
            copy_keys(0, 0)
            copy_keys(0, 1)
            copy_queries(0)
            table_high(0, 0)
            copy_values(0)
            split_x(1)
            turn(0, first=True)
            turn(1, second=True)
            with act.Fori(2, NCA - 2) as i:
                turn(i)
            turn(NCA - 2, split=False)
            turn(NCA - 1, last=True)

            def split_y(c):
                act.wait_ge(y_in[c], 16)
                nc.scalar.copy(ys[0][:, :, c * CF:(c + 1) * CF], y_raw[:, :, c * CF:(c + 1) * CF]).then_inc(y_hi, 1)

            split_y(0)
            split_out(NCA - 1)
            copy_y(NCA - 1)

            def ffn_step(g, f, c, table=None):
                s = group_step[g] + GROUPS[g][1] * c + f
                p = f % 2
                act.wait_ge(gu_done, s + 1)
                nc.scalar.activation(sg[:, p, :], PS[:, 4 + 2 * p, :], ACT.Silu).then_inc(silu_done, 1)
                if table is not None:
                    table_high(*table, more=False)
                act.wait_ge(mul_done, s + 1)
                if not (isinstance(s, int) and s < 2):
                    act.wait_ge(d_done, steps_before(g, f, c))
                nc.scalar.copy(hs[0][:, p, :], hf[:, p, :]).then_inc(h_hi, 1)
                if table is not None and table[1] is not last_half:
                    next_indices(table[1] + 1)

            for c in range(NCF):
                for f in range(GROUPS[0][1]):
                    n = GROUPS[0][1] * c + f
                    ffn_step(0, f, c, ends_at.get(n - 1))
                    if n + 1 < NCF:
                        split_y(n + 1)

            def split_x1(c):
                act.wait_ge(acc_added, (len(GROUPS) - 1) * NCF + c + 1)
                if c >= 2:
                    act.wait_ge(h_done, NT * (c - 1))
                nc.scalar.copy(x1s[0][c % 2][:, :, :], x1[:, :, c * CF:(c + 1) * CF]).then_inc(x1_hi, 1)

            for g in range(1, len(GROUPS)):
                nb = GROUPS[g][1]
                for f in range(nb):
                    ffn_step(g, f, 0, None if f else last_before[g])
                if g == len(GROUPS) - 1:
                    act.wait_ge(w1_in, 48)
                    nc.scalar.copy(w1_sb[0][:, :, :], w1_raw[:, :, :]).then_inc(w1_hi, 1)
                    nc.scalar.copy(a_sb[0][:, :, :], a_raw[:, :, :]).then_inc(w1_hi, 1)
                    nc.scalar.copy(b_sb[0][:, :], b_raw[:, :]).then_inc(w1_hi, 1)
                more = g + 1 < len(GROUPS)
                with act.Fori(1, NCF if more else NCF - 1) as c:
                    for f in range(nb):
                        ffn_step(g, f, c, table=(g + 1, 2 * GROUPS[g + 1][0] + c - 1) if more and f == 0 else None)
            split_x1(0)
            for f in range(GROUPS[-1][1]):
                ffn_step(len(GROUPS) - 1, f, NCF - 1)

            def linear_tiles(c):
                act.wait_ge(xa_masked, c + 1)
                if c:
                    act.wait_ge(h_done, NT * c)
                nc.scalar.copy(xas[0][:, :], xa[:, :]).then_inc(xa_hi, 1)
                if c + 1 < NCF:
                    split_x1(c + 1)
                for t in range(NT):
                    m = NT * c + t
                    act.wait_ge(h_done, m + 1)
                    if m >= 2:
                        act.wait_ge(h_stored[t % 2], 16 * (NT // 2 * c + t // 2))
                        act.wait_ge(out_added, m - 1)
                        act.wait_ge(scored, m - 1)
                    nc.scalar.copy(h_tile[:, t % 2, :], PS[:, t % 2, :]).then_inc(h_copied, 1)

            act.wait_ge(d_done, group_step[-1])
            for c in range(NCF):
                linear_tiles(c)

            def root_of(n):
                act.wait_ge(norm, 8 * n + 3)
                nc.scalar.activation(stat[:, 1, :], stat[:, 0, :], ACT.Sqrt).then_inc(root, 1)

            def copy_columns(dst, n):
                act.wait_ge(ht_done, n + 1)
                for k in range(KD):
                    nc.scalar.activation(dst[:, k, :], PS[:, 4 + k // 2, (k % 2) * SEL:(k % 2 + 1) * SEL], ACT.Copy,
                                         scale=ln_sb[:, n, k:k + 1]).then_inc(ht_copied, 1)

            root_of(0)
            copy_columns(hT, 0)
            for m in range(12):
                act.wait_ge(rt_done, m + 1)
                head, sb = 4 * (m // 2), m % 2
                dst = qT2[:, head:head + 4, sb * P:(sb + 1) * P] if m < 8 else kT2[:, head - 16:head - 12, sb * P:(sb + 1) * P]
                nc.scalar.copy(dst, PS[:, 6 + m % 2, :].rearrange("p (h q) -> p h q", h=4)).then_inc(rt_copied, 1)

            def exps2(g):
                act.wait_ge(s2_max, 2 * g + 2)
                for j in range(HG):
                    for sb in range(NSB):
                        part = prob2[:, g % 4, j, sb * P:(2 * sb + 1) * P]
                        nc.scalar.activation(part, part, ACT.Exp, bias=negmax2[:, g % 4, j, sb:sb + 1],
                                             accum_out=rowsum2[:, g % 4, j, sb:sb + 1]).then_inc(s2_exp, 1)

            def copy_prob2(h):
                act.wait_ge(p2t_done, h + 1)
                if h >= 4:
                    act.wait_ge(pv2_done, h - 3)
                nc.scalar.copy(prob2T[:, h % 4, :], PS[:, 4, 0:3 * P]).then_inc(p2t_copied, 1)

            def copy_out(h):
                act.wait_ge(pv2_done, h + 1)
                if h >= 2:
                    act.wait_ge(wo2_done, h - 1)
                nc.scalar.copy(outs[0][:, h % 2, :], PS[:, 5, 0:SEL]).then_inc(out2_hi, 1)
                nc.scalar.copy(wos[0][:, h % 2, :], wo_sb[:, h, :]).then_inc(wo2_hi, 1)

            NG2 = NHQ // HG
            act.wait_ge(wo_in, 16)
            exps2(0)
            exps2(1)
            for g in range(NG2):
                for h in range(HG * g, HG * g + HG):
                    copy_prob2(h)
                    if h:
                        copy_out(h - 1)
                if g + 2 < NG2:
                    exps2(g + 2)
            copy_out(NHQ - 1)
            act.wait_ge(gate_seq, 1)
            nc.scalar.activation(stat[:, 6, :], stat[:, 5, :], ACT.Exp, scale=-1.0).then_inc(gate_exp, 1)

            def gate_up_high(f, u):
                cols = slice(f * P, (f + 1) * P) if isinstance(f, int) else bass.ds(f * P, P)
                for k in range(2):
                    nc.scalar.copy(gus[0][:, u, 2 * k:2 * k + 2, :], wg_sb[k][:, :, cols])
                nc.scalar.copy(gus[0][:, u, KD:2 * KD, :], wu_sb[:, :, cols]).then_inc(gu_hi, 1)

            def down_high(f, u):
                src = wd_sb[:, f, :] if isinstance(f, int) else wd_sb[:, bass.ds(f, 1), :].rearrange("p a b -> p (a b)")
                nc.scalar.copy(wds[0][:, u, :], src).then_inc(wd_hi, 1)

            act.wait_ge(pv2_done, NHQ)
            act.wait_ge(wg_in, 32)
            act.wait_ge(wu_in, 16 * KD)
            gate_up_high(0, 0)
            gate_up_high(1, 1)
            act.wait_ge(wd_in, 16)
            down_high(0, 0)
            root_of(1)
            copy_columns(h2s[0], 1)

            def block_of_inner(f, u, first=False, more=2):
                act.wait_ge(g2_done, f + 1)
                if not first:
                    act.wait_ge(mul2, f - 1)
                nc.scalar.activation(sg1[:, u, :], PS[:, 4 + u, 0:SEL], ACT.Silu).then_inc(silu2, 1)
                if more >= 2:
                    gate_up_high(f + 2, u)
                act.wait_ge(mul2, f + 1)
                if not first:
                    act.wait_ge(d2_done, f - 1)
                nc.scalar.copy(inner_s[0][:, u, :], inner[:, u, :]).then_inc(inner_hi, 1)
                if more >= 1:
                    if not (first and u == 0):
                        act.wait_ge(d2_done, f)
                    down_high(f + 1, 1 - u)

            for u in range(2):
                block_of_inner(u, u, first=True)
            act.wait_ge(wd_late_in, 16)
            with act.Fori(1, NF1 // 2 - 1) as pair:
                for u in range(2):
                    block_of_inner(2 * pair + u, u)
            for u in range(2):
                block_of_inner(NF1 - 2 + u, u, more=1 - u)

        @block.vector
        def _(dve):
            def lut_part(g, h, v0, v1, meanwhile=None):
                acc = half_block(g, h)[2]
                n = max(0, 2 * v0 - 1)

                def counted(ins):
                    nonlocal n
                    ins.then_inc(lut_seq, 1)
                    n += 1
                    return n

                seen = n
                if v0 == 0:
                    dve.wait_ge(idx_conv, h + 1)
                    seen = counted(nc.vector.tensor_scalar(acc, idx_bf[:, :], 0.0, lut_sb[:, 0:1],
                                                           ALU.is_equal, ALU.mult))
                    v0 = 1
                made = {}
                call_at = v0 + 1 if v0 == 1 else v0 + 2
                for v in range(v0, v1 + 1):
                    if v < v1:
                        ins = nc.vector.tensor_scalar(onehot[:, v % 3, :], idx_bf[:, :], float(v), None, ALU.is_equal)
                        made[v] = counted(ins)
                    if v == call_at and meanwhile is not None:
                        meanwhile()
                    if v > v0:
                        u = v - 1
                        dve.wait_ge(lut_seq, LUT_OPS * h + max(made[u], seen))
                        seen = counted(nc.vector.scalar_tensor_tensor(
                            acc, onehot[:, u % 3, :], lut_sb[:, u:u + 1], acc, ALU.mult, ALU.add))

            def table_low(g, h):
                dve.wait_ge(tab_hi, h + 1)
                hi, lo, whole = half_block(g, h)
                nc.vector.tensor_tensor(lo, whole, hi.bitcast(F32), ALU.subtract).then_inc(tab_ready, 1)

            SOFT = 8

            def split_w(m, n):
                dve.wait_ge(w_hi, m + 1)
                nc.vector.tensor_tensor(w_sb[n][1][:, :, :], w_raw[n][:, :, :], w_sb[n][0][:, :, :].bitcast(F32),
                                        ALU.subtract).then_inc(w_lo, 1)

            def split_x(c):
                dve.wait_ge(x_hi, c + 1)
                nc.vector.tensor_tensor(xs[1][:, :, :], xr[:, :, :], xs[0][:, :, :].bitcast(F32),
                                        ALU.subtract).then_inc(x_lo, 1)

            dve.wait_ge(lut_in, 16)
            lut_part(0, 0, 0, 6)
            split_w(0, 1)
            split_x(0)
            lut_part(0, 0, 6, 8)
            split_w(1, 0)
            lut_part(0, 0, 8, 11)
            split_w(2, 2)
            lut_part(0, 0, 11, 14)
            split_w(3, 3)
            lut_part(0, 0, 14, 16)
            dve.wait_ge(consts_in, 32)
            nc.vector.tensor_scalar(beta[:, :], beta[:, :], 4.0, float(HD0) ** -0.5, ALU.min, ALU.mult).then_inc(beta_ready, 1)
            dve.wait_ge(beta_ready, 1)
            table_low(0, 0)
            lut_part(0, 1, 0, 5)
            split_x(1)

            def scale_and_mask(i):
                dve.wait_ge(s_done, i + 1)
                if not (isinstance(i, int) and i == 0):
                    dve.wait_ge(pt_done, 2 * i)
                for t in range(NP_):
                    out = prob[:, t, :, :].rearrange("p (e h) k -> p e (h k)", e=KD)
                    src = PS[:, 0:KD, t * 256:(t + 1) * 256]
                    m4 = mask[:, :].unsqueeze(1).to_broadcast([P, KD, 4 * S])
                    nc.vector.scalar_tensor_tensor(out, src, beta[:, bass.ds(2 * i + t, 1)], m4,
                                                   ALU.mult, ALU.add).then_inc(soft, 1)

            def subtract_max(i):
                b0 = SOFT * i
                for t in range(NP_):
                    dve.wait_ge(soft, b0 + 1 + t)
                    nc.vector.tensor_reduce(rowmax[:, t, :], prob[:, t, :, :], AX, ALU.max).then_inc(soft, 1)
                for t in range(NP_):
                    dve.wait_ge(soft, b0 + 3 + t)
                    nc.vector.tensor_tensor(prob[:, t, :, :], prob[:, t, :, :],
                                            rowmax[:, t, :].unsqueeze(2).to_broadcast([P, NH0, S]),
                                            ALU.subtract).then_inc(shifted, 1)

            def sums(i):
                b0 = SOFT * i + 4
                for t in range(NP_):
                    dve.wait_ge(exped, 2 * i + t + 1)
                    nc.vector.tensor_reduce(rowsum[:, t, :], prob[:, t, :, :], AX, ALU.add).then_inc(soft, 1)
                for t in range(NP_):
                    dve.wait_ge(soft, b0 + 1 + t)
                    nc.vector.reciprocal(rowinv[:, t, :], rowsum[:, t, :]).then_inc(soft, 1)

            def normalise(i):
                for t in range(NP_):
                    dve.wait_ge(pv_done, 2 * i + t + 1)
                    dve.wait_ge(soft, SOFT * i + 7 + t)
                    nc.vector.tensor_tensor(oN[:, t, :].rearrange("p (h d) -> p h d", d=HD0),
                                            PS[:, 6 + t, :].rearrange("p (h d) -> p h d", d=HD0),
                                            rowinv[:, t, :].unsqueeze(2).to_broadcast([P, NH0, HD0]),
                                            ALU.mult).then_inc(o_normed, 1)

            def split_out(i):
                for t in range(NP_):
                    dve.wait_ge(ot_hi, 2 * i + t + 1)
                    nc.vector.tensor_tensor(oT[1][:, :, t * P:(t + 1) * P],
                                            PS[:, 4 + t, :].rearrange("p (e q) -> p e q", e=KD),
                                            oT[0][:, :, t * P:(t + 1) * P].bitcast(F32), ALU.subtract).then_inc(ot_lo, 1)

            def split_y(c):
                dve.wait_ge(y_hi, c + 1)
                nc.vector.tensor_tensor(ys[1][:, :, c * CF:(c + 1) * CF], y_raw[:, :, c * CF:(c + 1) * CF],
                                        ys[0][:, :, c * CF:(c + 1) * CF].bitcast(F32), ALU.subtract).then_inc(y_lo, 1)

            def turn(i, first=False, last=False, split=True):
                if not first:
                    normalise(i - 1)
                g = int(last)
                if not first:
                    lut_part(g, i + 1, 0, 4)
                scale_and_mask(i)
                if not first:
                    split_out(i - 1)
                subtract_max(i)
                lut_part(g, i + 1, 5 if first else 4, 6)
                sums(i)
                if not last:
                    lut_part(0, i + 1, 6, 16)
                    if split:
                        split_x(i + 2)
                    table_low(0, i + 1)

            turn(0, first=True)
            with dve.Fori(1, NCA - 2) as i:
                turn(i)
            turn(NCA - 2, split=False)
            turn(NCA - 1, last=True)
            split_y(0)
            normalise(NCA - 1)
            split_out(NCA - 1)
            lut_part(1, NCA, 6, 16)

            def add_down(g, f, c):
                s = group_step[g] + GROUPS[g][1] * c + f
                dve.wait_ge(d_done, s + 1)
                if g:
                    dve.wait_ge(acc_added, NCF * g + c)
                part = x1[:, :, bass.ds(c * CF, CF)]
                nc.vector.tensor_tensor(part, PS[:, 0:KD, :], part, ALU.add).then_inc(acc_added, 1)

            def ffn_step(g, f, c, before=None, table=None, part=None):
                s = group_step[g] + GROUPS[g][1] * c + f
                p = f % 2
                dve.wait_ge(gu_done, s + 1)
                dve.wait_ge(silu_done, s + 1)
                if not (isinstance(s, int) and s < 2):
                    dve.wait_ge(h_lo, steps_before(g, f, c))
                nc.vector.tensor_tensor(hf[:, p, :], sg[:, p, :], PS[:, 5 + 2 * p, :], ALU.mult).then_inc(mul_done, 1)

                def h_low():
                    dve.wait_ge(h_hi, s + 1)
                    nc.vector.tensor_tensor(hs[1][:, p, :], hf[:, p, :], hs[0][:, p, :].bitcast(F32),
                                            ALU.subtract).then_inc(h_lo, 1)

                if before is not None:
                    add_down(*before)
                    h_low()
                if table is not None:
                    table_low(*table)
                if part is not None:
                    lut_part(*part, None if before is not None else h_low)
                elif before is None:
                    h_low()

            for c in range(NCF):
                for f in range(GROUPS[0][1]):
                    n = GROUPS[0][1] * c + f
                    if n == GROUPS[0][1] - 1:
                        dve.wait_ge(x1_in, 16)
                    ffn_step(0, f, c, (0, GROUPS[0][1] - 1, c - 1) if c and f == 0 else None, ends_at.get(n - 1),
                             (1, *first_parts[n]))
                    if n + 1 < NCF:
                        split_y(n + 1)

            def split_x1(c):
                dve.wait_ge(x1_hi, c + 1)
                nc.vector.tensor_tensor(x1s[1][c % 2][:, :, :], x1[:, :, c * CF:(c + 1) * CF],
                                        x1s[0][c % 2][:, :, :].bitcast(F32), ALU.subtract).then_inc(x1_lo, 1)

            def mask_adapters():
                dve.wait_ge(small_in, 16 * 9)
                nc.vector.tensor_copy(tok_adf[:, :], tok_ad[:, :]).then_inc(admask_made, 1)
                dve.wait_ge(admask_made, 1)
                nc.vector.tensor_scalar(admask[:, :], tok_adf[:, :], row_ad[:, 0:1], scal_sb[:, 0:1],
                                        ALU.is_equal, ALU.mult).then_inc(admask_made, 1)
                dve.wait_ge(admask_made, 2)

            for g in range(1, len(GROUPS)):
                nb = GROUPS[g][1]
                cuts = [0] + [-(-LUTN * (f + 1) // nb) for f in range(nb)]
                more = g + 1 < len(GROUPS)

                def split_w1():
                    dve.wait_ge(w1_hi, 3)
                    for n, (part, raw) in enumerate(((w1_sb, w1_raw), (a_sb, a_raw), (b_sb, b_raw))):
                        whole = tuple([slice(None)] * (3 if n < 2 else 2))
                        nc.vector.tensor_tensor(part[1][whole], raw[whole], part[0][whole].bitcast(F32),
                                                ALU.subtract).then_inc(w1_lo, 1)

                def chunk(c, before, table):
                    for f in range(nb):
                        ffn_step(g, f, c, before if f == 0 else None, table if f == 0 else None,
                                 (g + 1, 2 * GROUPS[g + 1][0] + c, cuts[f], cuts[f + 1]) if more else None)

                chunk(0, (g - 1, GROUPS[g - 1][1] - 1, NCF - 1), last_before[g])
                if not more:
                    split_w1()
                    mask_adapters()
                with dve.Fori(1, NCF if more else NCF - 1) as c:
                    chunk(c, (g, nb - 1, c - 1), (g + 1, 2 * GROUPS[g + 1][0] + c - 1) if more else None)
            split_x1(0)
            chunk(NCF - 1, (g, nb - 1, NCF - 2), None)
            add_down(g, nb - 1, NCF - 1)

            def linear_tiles(c):
                dve.wait_ge(xa_done, c + 1)
                if c:
                    dve.wait_ge(xa_lo, c)
                    dve.wait_ge(xa_hi, c)
                per = CF // S
                nc.vector.tensor_tensor(xa[:, :].rearrange("p (b t) -> p b t", t=S),
                                        PS[:, 4, :].rearrange("p (b t) -> p b t", t=S),
                                        admask[:, c * per:(c + 1) * per].unsqueeze(2).to_broadcast([P, per, S]),
                                        ALU.mult).then_inc(xa_masked, 1)
                dve.wait_ge(xa_hi, c + 1)
                dve.wait_ge(xa_masked, c + 1)
                nc.vector.tensor_tensor(xas[1][:, :], xa[:, :], xas[0][:, :].bitcast(F32), ALU.subtract).then_inc(xa_lo, 1)
                if c + 1 < NCF:
                    split_x1(c + 1)
                for t in range(NT):
                    m = NT * c + t
                    dve.wait_ge(h_copied, m + 1)
                    if m:
                        dve.wait_ge(scored, m)
                    nc.vector.tensor_tensor_reduce(prod[:, :], h_tile[:, t % 2, :], router_sb[:, :], 1.0, 0.0,
                                                   ALU.mult, ALU.add, score[:, m:m + 1]).then_inc(scored, 1)
                    dve.wait_ge(xn_done, m + 1)
                    if m >= 2:
                        dve.wait_ge(out_stored[t % 2], 16 * (NT // 2 * c + t // 2))
                    nc.vector.tensor_tensor(out_tile[:, t % 2, :], h_tile[:, t % 2, :], PS[:, 2 + t % 2, :],
                                            ALU.add).then_inc(out_added, 1)

            for c in range(NCF):
                linear_tiles(c)

            tops = [0]

            def step(ins):
                ins.then_inc(top, 1)
                tops[0] += 1
                dve.wait_ge(top, tops[0])

            R16 = slice(0, NPAIR)
            dve.wait_ge(top_pe, 1)
            step(nc.vector.tensor_copy(scoreT[R16, :], PS[R16, 5, 0:P]))
            for j in range(2):
                half = slice(j * S, (j + 1) * S)
                step(nc.vector.max(best[R16, j, :], scoreT[R16, half]))
                step(nc.vector.match_replace(replaced[R16, half], best[R16, j, :], scoreT[R16, half], -3.0e38))
            step(nc.vector.tensor_tensor(picked[R16, :], replaced[R16, :], scoreT[R16, :], ALU.not_equal))
            dve.wait_ge(zeroed, 3)
            for j in range(2):
                half = slice(j * S, (j + 1) * S)
                step(nc.vector.tensor_tensor_scan(rank[R16, half], onesr[R16, :], picked[R16, half], 0.0,
                                                  ALU.mult, ALU.add))
            step(nc.vector.tensor_tensor(rank[R16, :], rank[R16, :], picked[R16, :], ALU.mult))
            assert tops[0] == 9
            dve.wait_ge(top_pe, 2)
            step(nc.vector.tensor_copy(rankT[:, :], PS[:, 6, 0:NPAIR]))
            step(nc.vector.tensor_tensor(pick[:, :, :], rankT[:, :].unsqueeze(2).to_broadcast([P, NPAIR, 2 * TOPK]),
                                         slots_sb[:, :].unsqueeze(1).to_broadcast([P, NPAIR, 2 * TOPK]), ALU.is_equal))
            assert tops[0] == 11
            dve.wait_ge(top_pe, 3)
            step(nc.vector.tensor_copy(tables[:, :, :].rearrange("p a b -> p (a b)"), PS[:, 7, 0:NSB * TABW]))
            nc.vector.tensor_tensor(rowidx[:, :], tables[:, :, TABW - 1], pair_sb[:, :], ALU.add).then_inc(rows_ready, 1)

            def inverse_rms(src, n):
                seen = [8 * n]

                def step(ins):
                    ins.then_inc(norm, 1)
                    seen[0] += 1
                    dve.wait_ge(norm, seen[0])

                for sb in range(NSB):
                    step(nc.vector.tensor_tensor_reduce(scratch[:, :], src[:, sb, :], src[:, sb, :], 1.0, 0.0,
                                                        ALU.mult, ALU.add, stat[:, 7, sb:sb + 1]))
                step(nc.vector.tensor_scalar(stat[:, 0, :], stat[:, 7, :], 1.0 / D, EPS, ALU.mult, ALU.add))
                dve.wait_ge(root, n + 1)
                step(nc.vector.reciprocal(stat[:, 2, :], stat[:, 1, :]))
                step(nc.vector.tensor_tensor(stat[:, 3, :], stat[:, 2, :], stat[:, 2, :], ALU.mult))
                step(nc.vector.tensor_tensor(stat[:, 3, :], stat[:, 3, :], stat[:, 0, :], ALU.mult))
                step(nc.vector.tensor_scalar(stat[:, 3, :], stat[:, 3, :], -0.5, 1.5, ALU.mult, ALU.add))
                step(nc.vector.tensor_tensor(stat[:, 4, :], stat[:, 2, :], stat[:, 3, :], ALU.mult))

            dve.wait_ge(sel_in, 32)
            inverse_rms(hsel, 0)
            for sb in range(NSB):
                dve.wait_ge(norm, 8)
                ins = nc.vector.tensor_tensor_reduce(scratch[:, :], hsel[:, sb, :], router_sb[:, :], 1.0, 0.0,
                                                     ALU.mult, ALU.add, stat[:, 5, sb:sb + 1])
                ins.then_inc(gate_seq, 1)
                dve.wait_ge(gate_seq, sb + 1)

            dve.wait_ge(bias_in, 16)
            seen = 0
            rms_inv = stat[:, 4, :]
            for m in range(16):
                nt, sb = m // 2, m % 2
                dve.wait_ge(qkv_done, m + 1)
                if m < 12:
                    if m >= 2:
                        dve.wait_ge(rt_done, m - 1)
                        dve.wait_ge(rope_seq, seen)
                    nc.vector.scalar_tensor_tensor(biased[:, 0, :], PS[:, m % 4, :], rms_inv[:, sb:sb + 1],
                                                   bias_sb[:, nt * 512:(nt + 1) * 512],
                                                   ALU.mult, ALU.add).then_inc(qkv_read, 1)
                    dve.wait_ge(qkv_read, m + 1)
                    x4 = biased[:, 0, :].rearrange("p (h a w) -> p h a w", h=4, a=2)
                    cos = tables[:, sb, 0:ROPE_W].unsqueeze(1).to_broadcast([P, 8, ROPE_W])
                    nc.vector.tensor_tensor(times_cos[:, :].rearrange("p (a w) -> p a w", a=8),
                                            biased[:, 0, :].rearrange("p (a w) -> p a w", a=8), cos,
                                            ALU.mult).then_inc(rope_seq, 1)
                    y4 = times_sin[:, :].rearrange("p (h a w) -> p h a w", h=4, a=2)
                    for a in range(2):
                        sin = tables[:, sb, (1 + a) * ROPE_W:(2 + a) * ROPE_W].unsqueeze(1).to_broadcast([P, 4, ROPE_W])
                        nc.vector.tensor_tensor(y4[:, :, a, :], x4[:, :, 1 - a, :], sin, ALU.mult).then_inc(rope_seq, 1)
                    seen += 3
                    dve.wait_ge(rope_seq, seen)
                    nc.vector.tensor_tensor(turned_of(m), times_cos[:, :], times_sin[:, :], ALU.add).then_inc(roped, 1)
                    dve.wait_ge(roped, m + 1)
                else:
                    nc.vector.scalar_tensor_tensor(v2[:, sb, (nt - 6) * 512:(nt - 5) * 512], PS[:, m % 4, :],
                                                   rms_inv[:, sb:sb + 1], bias_sb[:, nt * 512:(nt + 1) * 512],
                                                   ALU.mult, ALU.add).then_inc(qkv_read, 1)

            def mask_and_max(g):
                dve.wait_ge(s2_done, g + 1)
                if g >= 4:
                    dve.wait_ge(p2t_done, HG * (g - 3))
                nc.vector.scalar_tensor_tensor(prob2[:, g % 4, :, :], PS[:, HG * (g % 2):HG * (g % 2) + HG, 0:3 * P],
                                               float(HD) ** -0.5, mask2[:, :].unsqueeze(1).to_broadcast([P, HG, 3 * P]),
                                               ALU.mult, ALU.add).then_inc(s2_masked, 1)
                dve.wait_ge(s2_masked, g + 1)
                for sb in range(NSB):
                    nc.vector.tensor_reduce(negmax2[:, g % 4, :, sb], prob2[:, g % 4, :, sb * P:(2 * sb + 1) * P], AX,
                                            ALU.max, negate=True).then_inc(s2_max, 1)

            def divide(g):
                dve.wait_ge(s2_exp, 2 * HG * (g + 1))
                nc.vector.reciprocal(rowsum2[:, g % 4, :, :], rowsum2[:, g % 4, :, :]).then_inc(s2_inv, 1)
                dve.wait_ge(s2_inv, g + 1)
                for sb in range(NSB):
                    part = prob2[:, g % 4, :, sb * P:(2 * sb + 1) * P]
                    nc.vector.tensor_tensor(part, part, rowsum2[:, g % 4, :, sb:sb + 1].to_broadcast([P, HG, (sb + 1) * P]),
                                            ALU.mult).then_inc(s2_norm, 1)

            def out_low(h):
                dve.wait_ge(out2_hi, h + 1)
                nc.vector.tensor_tensor(outs[1][:, h % 2, :], PS[:, 5, 0:SEL], outs[0][:, h % 2, :].bitcast(F32),
                                        ALU.subtract).then_inc(out2_lo, 1)
                dve.wait_ge(wo2_hi, h + 1)
                nc.vector.tensor_tensor(wos[1][:, h % 2, :], wo_sb[:, h, :], wos[0][:, h % 2, :].bitcast(F32),
                                        ALU.subtract).then_inc(wo2_lo, 1)

            NG2 = NHQ // HG
            mask_and_max(0)
            mask_and_max(1)
            divide(0)
            for g in range(NG2):
                if g + 2 < NG2:
                    mask_and_max(g + 2)
                if g:
                    out_low(HG * g - 1)
                if g + 1 < NG2:
                    divide(g + 1)
                out_low(HG * g)
            out_low(NHQ - 1)
            dve.wait_ge(gate_exp, 1)
            nc.vector.tensor_scalar(stat[:, 6, :], stat[:, 6, :], 1.0, None, ALU.add).then_inc(gate_seq, 1)
            dve.wait_ge(gate_seq, 3)
            nc.vector.reciprocal(stat[:, 5, :], stat[:, 6, :]).then_inc(gate_seq, 1)
            dve.wait_ge(gate_seq, 4)

            def gate_up_low(f, u):
                cols = slice(f * P, (f + 1) * P) if isinstance(f, int) else bass.ds(f * P, P)
                dve.wait_ge(gu_hi, f + 1)
                for k in range(2):
                    nc.vector.tensor_tensor(gus[1][:, u, 2 * k:2 * k + 2, :], wg_sb[k][:, :, cols],
                                            gus[0][:, u, 2 * k:2 * k + 2, :].bitcast(F32), ALU.subtract)
                nc.vector.tensor_tensor(gus[1][:, u, KD:2 * KD, :], wu_sb[:, :, cols],
                                        gus[0][:, u, KD:2 * KD, :].bitcast(F32), ALU.subtract).then_inc(gu_lo, 1)

            def down_low(f, u):
                src = wd_sb[:, f, :] if isinstance(f, int) else wd_sb[:, bass.ds(f, 1), :].rearrange("p a b -> p (a b)")
                dve.wait_ge(wd_hi, f + 1)
                nc.vector.tensor_tensor(wds[1][:, u, :], src, wds[0][:, u, :].bitcast(F32),
                                        ALU.subtract).then_inc(wd_lo, 1)

            gate_up_low(0, 0)
            for sb in range(NSB):
                dve.wait_ge(wo2_done, NHQ)
                dve.wait_ge(ht_done, 1)
                nc.vector.tensor_tensor(xres[:, sb, :], PS[:, 6 + sb, :], hsel[:, sb, :], ALU.add).then_inc(gate_seq, 1)
            dve.wait_ge(gate_seq, 6)
            inverse_rms(xres, 1)
            for sb in range(NSB):
                ins = nc.vector.tensor_scalar(hsel_normed[:, sb, :], xres[:, sb, :], stat[:, 4, sb:sb + 1], None, ALU.mult)
            ins.then_inc(normed, 1)
            gate_up_low(1, 1)
            down_low(0, 0)
            for k in range(KD):
                dve.wait_ge(ht_copied, KD + 2 * (k // 2) + 2)
                nc.vector.scalar_tensor_tensor(h2s[1][:, k, :], PS[:, 4 + k // 2, (k % 2) * SEL:(k % 2 + 1) * SEL],
                                               ln_sb[:, 1, k:k + 1], h2s[0][:, k, :].bitcast(F32),
                                               ALU.mult, ALU.subtract).then_inc(h2_lo, 1)

            for sb in range(NSB):
                nc.vector.tensor_tensor(hsel[:, sb, :], xres[:, sb, :], hsel[:, sb, :], ALU.subtract).then_inc(gate_seq, 1)

            def block_of_inner(f, u, first=False, more=2):
                dve.wait_ge(silu2, f + 1)
                if not first:
                    dve.wait_ge(inner_lo, f - 1)
                    dve.wait_ge(inner_hi, f - 1)
                nc.vector.tensor_tensor(inner[:, u, :], sg1[:, u, :], PS[:, 4 + u, SEL:2 * SEL], ALU.mult).then_inc(mul2, 1)
                if more >= 2:
                    gate_up_low(f + 2, u)
                dve.wait_ge(inner_hi, f + 1)
                dve.wait_ge(mul2, f + 1)
                nc.vector.tensor_tensor(inner_s[1][:, u, :], inner[:, u, :], inner_s[0][:, u, :].bitcast(F32),
                                        ALU.subtract).then_inc(inner_lo, 1)
                if more >= 1:
                    down_low(f + 1, 1 - u)

            for u in range(2):
                block_of_inner(u, u, first=True)
            dve.wait_ge(outsel_in, 16 * NSB)
            dve.wait_ge(gate_seq, 8)
            for sb in range(NSB):
                nc.vector.scalar_tensor_tensor(outsel[:, sb, :], hsel[:, sb, :], stat[:, 5, sb:sb + 1], outsel[:, sb, :],
                                               ALU.mult, ALU.add).then_inc(gate_seq, 1)
            dve.wait_ge(gate_seq, 10)
            with dve.Fori(1, NF1 // 2 - 1) as pair:
                for u in range(2):
                    block_of_inner(2 * pair + u, u)
            for u in range(2):
                block_of_inner(NF1 - 2 + u, u, more=1 - u)

            for sb in range(NSB):
                dve.wait_ge(d2_done, NF1 + sb)
                nc.vector.scalar_tensor_tensor(fin[:, sb, :], PS[:, 2 + sb, :], stat[:, 5, sb:sb + 1], outsel[:, sb, :],
                                               ALU.mult, ALU.add).then_inc(fin_ready, 1)


def kernel(**inputs):
    import numpy as np
    import concourse.bacc as bacc
    from concourse.bass_utils import run_bass_kernel_spmd

    nc = bacc.Bacc("TRN2", target_bir_lowering=False, num_devices=1, dynamic_dma_scratch_size=4096)
    con = np.ascontiguousarray

    def features_first(w):
        return con(np.asarray(w).reshape(w.shape[0], -1, P).transpose(2, 1, 0))

    arrays = {}
    arrays["xT"] = features_first(np.asarray(inputs["x"]).reshape(TOK, D))
    arrays["w0"] = np.stack([features_first(inputs[f"L0_cond_{n}"]) for n in ("Wq", "Wk", "Wv", "Wo")])
    pad = NBLK * P - INTER

    def in_blocks(w):
        w = np.pad(np.asarray(w), ((0, pad), (0, 0)))
        return w.reshape(NBLK, P, KD, P).transpose(0, 3, 2, 1).reshape(NBLK, P, D)

    gate, up = (in_blocks(inputs[f"L0_ffn_{n}_idx"]) for n in ("gate", "up"))
    down = np.pad(np.asarray(inputs["L0_ffn_down_idx"]).T, ((0, pad), (0, 0))).reshape(NBLK, P, D)
    both = np.concatenate([gate, up, down], axis=2).reshape(NBLK, P, 2, HALF)
    arrays["idx"] = con(both.transpose(0, 2, 1, 3).reshape(2 * NBLK, P, HALF))
    arrays["lut"] = con(np.broadcast_to(np.asarray(inputs["L0_ffn_lut"]), (P, LUTN)))
    arrays["cond"] = con(np.repeat(np.asarray(inputs["cond_1"]).reshape(B // 2, 2).T, S, axis=0))
    t = np.arange(S)
    below = np.where(t[None, :] <= t[:, None], 0.0, -3.0e38).astype(np.float32)
    arrays["causal"] = con(np.tile(below, (2, 4)))
    arrays["w1"] = features_first(inputs["L1_cond_W"])
    arrays["aT"] = features_first(np.asarray(inputs["L1_cond_A"]).reshape(NA * RANK, D))
    arrays["bmT"] = con(np.asarray(inputs["L1_cond_Bm"]).transpose(0, 2, 1).reshape(NA * RANK, D))
    arrays["tokens_adapter"] = con(np.broadcast_to(np.asarray(inputs["itok_B_0_6"]), (P, B)))
    arrays["adapter_of_row"] = np.repeat(np.arange(NA, dtype=np.float32), RANK)[:, None]
    arrays["scalings"] = con(np.repeat(np.asarray(inputs["L1_cond_scalings"]), RANK)[:, None])
    arrays["router"] = con(np.broadcast_to(np.asarray(inputs["L1_ffn_w_router"]), (P, D)))
    n = np.arange(1, TOPK + 1, dtype=np.float32)
    none = -np.ones(TOPK, np.float32)
    arrays["slots"] = np.repeat(np.stack([np.concatenate([n, none]), np.concatenate([none, n])]), S, axis=0)
    inv = np.float32(1.0) / np.float32(10000.0) ** (np.arange(0, HD, 2, dtype=np.float32) / np.float32(HD))
    angle = np.tile(t.astype(np.float32), 2)[:, None] * inv
    arrays["rope"] = np.concatenate([np.cos(angle), -np.sin(angle), np.sin(angle),
                                     np.arange(P, dtype=np.float32)[:, None]], axis=1).astype(np.float32)
    t = np.arange(P)
    below = np.where(t[None, :] <= t[:, None], 0.0, -3.0e38).astype(np.float32)
    arrays["causal2"] = con(np.concatenate([below, np.zeros((P, P), np.float32), below], axis=1))
    sel = np.arange(SEL).reshape(NSB, P).T
    arrays["pair_base"] = con((sel // (2 * TOPK) * P).astype(np.float32))
    arrays["ln"] = con(np.stack([np.asarray(inputs[f"L1_ffn_ln{n}_w"]).reshape(KD, P).T for n in (1, 2)], axis=1))

    def rows_first(w):
        return con(np.asarray(w).reshape(-1, P, w.shape[1]).transpose(1, 0, 2))

    for name, key in (("wq", "wq"), ("wk", "wk"), ("wv", "wv"), ("wo", "wo"), ("wgate", "w_gate"), ("wup", "w_up"),
                      ("wdown", "w_down")):
        arrays[name] = rows_first(inputs[f"L1_ffn_{key}"])
    arrays["bias"] = con(np.broadcast_to(np.concatenate([np.asarray(inputs[f"L1_ffn_{n}"]) for n in ("bq", "bk", "bv")]),
                                         (P, (NHQ + 2 * NHKV) * HD)))
    aps = {n: nc.dram_tensor(f"in_{n}", a.shape, mybir.dt.from_np(a.dtype), kind="ExternalInput").ap()
           for n, a in arrays.items()}
    y_dram = nc.dram_tensor("y_dram", (P, KD, TOK), F32, kind="Internal").ap()
    h_dram = nc.dram_tensor("h_dram", (TOK, D), F32, kind="Internal").ap()
    out = nc.dram_tensor("out_rows", (TOK, D), F32, kind="ExternalOutput").ap()
    adaln_ffn_kernel(nc, y_dram=y_dram, h_dram=h_dram, out=out, **aps)
    r = run_bass_kernel_spmd(nc, [{f"in_{n}": a for n, a in arrays.items()}], core_ids=[0])
    return r.results[0]["out_rows"].reshape(B, S, D)
```
